# Optimizing a Trainium2 kernel written in Bass

```python
import numpy as np
import jax
import jax.numpy as jnp

def _softmax(x, axis=-1):
    return jax.nn.softmax(x, axis=axis)

def _gelu(x):
    return jax.nn.gelu(x, approximate=True)

def _silu(x):
    return jax.nn.silu(x)

def _sigmoid(x):
    return jax.nn.sigmoid(x)

def _layernorm(x, axis=-1, eps=1e-05):
    m = jnp.mean(x, axis=axis, keepdims=True)
    v = jnp.var(x, axis=axis, keepdims=True)
    return (x - m) / jnp.sqrt(v + eps)

def _scatter_add(tgt, idx, src, axis=0):
    return tgt.at[idx].add(src)

def _segment_sum(src, seg, n):
    return jax.ops.segment_sum(src, seg, n)
kernel_name = 'mk_gnn_ffn_d1_gnn_r32_4b6ebf'

def setup_inputs(seed: int=0):
    np.random.seed(seed)
    _w = jnp.asarray

    def _rec_inputs():
        import jax
        import jax.numpy as jnp
        _gk = jax.random.key(seed)
        x = -6.415e-05 + 1 * jax.random.normal(jax.random.fold_in(_gk, 1), (10000, 512), jnp.float32)
        src = jax.random.randint(jax.random.fold_in(_gk, 2), (10000,), 0, 10000, jnp.int32)
        dst = jax.random.randint(jax.random.fold_in(_gk, 3), (10000,), 0, 10000, jnp.int32)
        _o = jnp.argsort(dst, stable=True)
        src = src[_o]
        dst = dst[_o]
        edge_attr_32 = jax.random.uniform(jax.random.fold_in(_gk, 11), (10000, 32), jnp.float32, 0.0, 1)
        edge_attr_4 = 0.000937891 + 0.999965 * jax.random.normal(jax.random.fold_in(_gk, 12), (10000, 4), jnp.float32)
        return (x, src, dst, edge_attr_32, edge_attr_4)
    x, src, dst, edge_attr_32, edge_attr_4 = _rec_inputs()

    def _L0_gnn_setup():
        import jax, jax.numpy as jnp
        import numpy as np
        import math
        N, E = (625, 6250)
        MUL = 128
        D = MUL + 3 * MUL
        EDGE_ATTR = 32
        HID = 32
        LOG2 = math.log(2.0)

        def ssp(x):
            return jax.nn.softplus(x) - LOG2

        def split_irreps(x):
            return (x[:, :MUL], x[:, MUL:].reshape(x.shape[0], MUL, 3))

        def merge_irreps(x0, x1):
            return jnp.concatenate([x0, x1.reshape(x1.shape[0], MUL * 3)], axis=-1)

        def irrep_linear(x, W0, b0, W1):
            x0, x1 = split_irreps(x)
            y0 = x0 @ W0 + b0
            y1 = jnp.einsum('nuc,uv->nvc', x1, W1)
            return merge_irreps(y0, y1)
        key = jax.random.key(seed)
        ks = iter(jax.random.split(key, 32))

        def randn(shape, scale=1.0):
            return (scale * jax.random.normal(next(ks), shape)).astype(jnp.float32)
        inp = {'x': randn((N, D)), 'edge_sh': randn((E, 4)), 'edge_attr': jax.random.uniform(next(ks), (E, EDGE_ATTR), dtype=jnp.float32), 'edge_index': jax.random.randint(next(ks), (2, E), 0, N, dtype=jnp.int32), 'W_pre0': randn((MUL, MUL), MUL ** (-0.5)), 'b_pre0': jnp.zeros((MUL,), jnp.float32), 'W_pre1': randn((MUL, MUL), MUL ** (-0.5)), 'W_nd0': randn((MUL, MUL), MUL ** (-0.5)), 'b_nd0': jnp.zeros((MUL,), jnp.float32), 'W_nd1': randn((MUL, MUL), MUL ** (-0.5)), 'W_g1': randn((2 * MUL, 2 * MUL), (2 * MUL) ** (-0.5)), 'b_g1': jnp.zeros((2 * MUL,), jnp.float32), 'W_g2': randn((2 * MUL, 2 * MUL), (2 * MUL) ** (-0.5)), 'b_g2': jnp.zeros((2 * MUL,), jnp.float32), 'W_f1': randn((EDGE_ATTR, HID), EDGE_ATTR ** (-0.5)), 'W_f2': randn((HID, 4 * MUL), HID ** (-0.5)), 'W_s1': randn((3 * MUL, HID), (3 * MUL) ** (-0.5)), 'W_s2': randn((HID, 4 * MUL), HID ** (-0.5)), 'W_o0': randn((MUL, MUL), MUL ** (-0.5)), 'b_o0': jnp.zeros((MUL,), jnp.float32), 'W_o1': randn((MUL, MUL), MUL ** (-0.5))}
        return inp
    _L0_gnn_all = _L0_gnn_setup()
    _L0_gnn_in = {k: v for k, v in _L0_gnn_all.items() if k in ('W_pre0', 'b_pre0', 'W_pre1', 'W_nd0', 'b_nd0', 'W_nd1', 'W_g1', 'b_g1', 'W_g2', 'b_g2', 'W_f1', 'W_f2', 'W_s1', 'W_s2', 'W_o0', 'b_o0', 'W_o1')}
    del _L0_gnn_all

    def _L0_ffn_setup():
        import jax, jax.numpy as jnp
        import numpy as np
        EPS = 1e-05
        TOP_K = 2

        def layer_norm(x, g, b):
            m = x.mean(-1, keepdims=True)
            v = ((x - m) ** 2).mean(-1, keepdims=True)
            return (x - m) / jnp.sqrt(v + EPS) * g + b
        key = jax.random.key(seed)
        ks = jax.random.split(key, 8)
        B, S, D, E, H = (8, 512, 512, 8, 64)
        x = jax.random.normal(ks[0], (B, S, D), dtype=jnp.float32)
        Wg = jax.random.normal(ks[1], (D, E), dtype=jnp.float32) * 0.02
        W1 = jax.random.normal(ks[2], (E, D, H), dtype=jnp.float32) * 0.02
        b1 = jnp.zeros((E, H), dtype=jnp.float32)
        W2 = jax.random.normal(ks[3], (E, H, D), dtype=jnp.float32) * 0.02
        b2 = jnp.zeros((E, D), dtype=jnp.float32)
        ln_g = jnp.ones((D,), dtype=jnp.float32)
        ln_b = jnp.zeros((D,), dtype=jnp.float32)
        out_g = jnp.ones((D,), dtype=jnp.float32)
        out_b = jnp.zeros((D,), dtype=jnp.float32)
        return {'x': x, 'Wg': Wg, 'W1': W1, 'b1': b1, 'W2': W2, 'b2': b2, 'ln_g': ln_g, 'ln_b': ln_b, 'out_g': out_g, 'out_b': out_b}
    _L0_ffn_all = _L0_ffn_setup()
    _L0_ffn_in = {k: v for k, v in _L0_ffn_all.items() if k in ('Wg', 'W1', 'b1', 'W2', 'b2', 'ln_g', 'ln_b', 'out_g', 'out_b')}
    del _L0_ffn_all
    return {'x': x, 'src': src, 'dst': dst, 'edge_attr_32': edge_attr_32, 'edge_attr_4': edge_attr_4, 'L0_gnn_W_pre0': _L0_gnn_in['W_pre0'], 'L0_gnn_b_pre0': _L0_gnn_in['b_pre0'], 'L0_gnn_W_pre1': _L0_gnn_in['W_pre1'], 'L0_gnn_W_nd0': _L0_gnn_in['W_nd0'], 'L0_gnn_b_nd0': _L0_gnn_in['b_nd0'], 'L0_gnn_W_nd1': _L0_gnn_in['W_nd1'], 'L0_gnn_W_g1': _L0_gnn_in['W_g1'], 'L0_gnn_b_g1': _L0_gnn_in['b_g1'], 'L0_gnn_W_g2': _L0_gnn_in['W_g2'], 'L0_gnn_b_g2': _L0_gnn_in['b_g2'], 'L0_gnn_W_f1': _L0_gnn_in['W_f1'], 'L0_gnn_W_f2': _L0_gnn_in['W_f2'], 'L0_gnn_W_s1': _L0_gnn_in['W_s1'], 'L0_gnn_W_s2': _L0_gnn_in['W_s2'], 'L0_gnn_W_o0': _L0_gnn_in['W_o0'], 'L0_gnn_b_o0': _L0_gnn_in['b_o0'], 'L0_gnn_W_o1': _L0_gnn_in['W_o1'], 'L0_ffn_Wg': _L0_ffn_in['Wg'], 'L0_ffn_W1': _L0_ffn_in['W1'], 'L0_ffn_b1': _L0_ffn_in['b1'], 'L0_ffn_W2': _L0_ffn_in['W2'], 'L0_ffn_b2': _L0_ffn_in['b2'], 'L0_ffn_ln_g': _L0_ffn_in['ln_g'], 'L0_ffn_ln_b': _L0_ffn_in['ln_b'], 'L0_ffn_out_g': _L0_ffn_in['out_g'], 'L0_ffn_out_b': _L0_ffn_in['out_b']}

def reference(x, src, dst, edge_attr_32, edge_attr_4, L0_gnn_W_pre0, L0_gnn_b_pre0, L0_gnn_W_pre1, L0_gnn_W_nd0, L0_gnn_b_nd0, L0_gnn_W_nd1, L0_gnn_W_g1, L0_gnn_b_g1, L0_gnn_W_g2, L0_gnn_b_g2, L0_gnn_W_f1, L0_gnn_W_f2, L0_gnn_W_s1, L0_gnn_W_s2, L0_gnn_W_o0, L0_gnn_b_o0, L0_gnn_W_o1, L0_ffn_Wg, L0_ffn_W1, L0_ffn_b1, L0_ffn_W2, L0_ffn_b2, L0_ffn_ln_g, L0_ffn_ln_b, L0_ffn_out_g, L0_ffn_out_b):
    import jax
    import jax.numpy as jnp

    def _L0_gnn_ref(x, edge_sh, edge_attr, edge_index, W_pre0, b_pre0, W_pre1, W_nd0, b_nd0, W_nd1, W_g1, b_g1, W_g2, b_g2, W_f1, W_f2, W_s1, W_s2, W_o0, b_o0, W_o1):
        import jax, jax.numpy as jnp
        import numpy as np
        import math
        N, E = (625, 6250)
        MUL = 128
        D = MUL + 3 * MUL
        EDGE_ATTR = 32
        HID = 32
        LOG2 = math.log(2.0)

        def ssp(x):
            return jax.nn.softplus(x) - LOG2

        def split_irreps(x):
            return (x[:, :MUL], x[:, MUL:].reshape(x.shape[0], MUL, 3))

        def merge_irreps(x0, x1):
            return jnp.concatenate([x0, x1.reshape(x1.shape[0], MUL * 3)], axis=-1)

        def irrep_linear(x, W0, b0, W1):
            x0, x1 = split_irreps(x)
            y0 = x0 @ W0 + b0
            y1 = jnp.einsum('nuc,uv->nvc', x1, W1)
            return merge_irreps(y0, y1)
        edge_dst, edge_src = (edge_index[0], edge_index[1])
        old_x = x
        pre = irrep_linear(x, W_pre0, b_pre0, W_pre1)
        p0, p1 = split_irreps(pre)
        pd0 = p0[edge_dst]
        ip1 = jnp.einsum('eum,eum->eu', p1[edge_dst], p1[edge_src]) / 3.0
        s0 = jnp.concatenate([pd0, pd0, ip1], axis=-1)
        x0, x1 = split_irreps(x)
        n1 = jnp.sqrt(jnp.sum(x1 * x1, axis=-1) / 3.0)
        g = jax.nn.silu(jnp.concatenate([x0, n1], -1) @ W_g1 + b_g1) @ W_g2 + b_g2
        xg = merge_irreps(g[:, :MUL], x1 * g[:, MUL:, None])
        x = irrep_linear(xg, W_nd0, b_nd0, W_nd1)
        self_x = x
        w = ssp(edge_attr @ W_f1) @ W_f2 * (ssp(s0 @ W_s1) @ W_s2)
        w1, w2, w3, w4 = jnp.split(w, 4, axis=-1)
        x0e, x1e = split_irreps(x[edge_src])
        sh0, sh1 = (edge_sh[:, 0], edge_sh[:, 1:4])
        out0 = w1 * x0e * sh0[:, None] + w4 * (jnp.einsum('eum,em->eu', x1e, sh1) / jnp.sqrt(3.0))
        out1 = w2[:, :, None] * x0e[:, :, None] * sh1[:, None, :] + w3[:, :, None] * x1e * sh0[:, None, None]
        edge_feat = merge_irreps(out0, out1)
        out = jax.ops.segment_sum(edge_feat, edge_dst, num_segments=old_x.shape[0])
        out = out + self_x
        out = irrep_linear(out, W_o0, b_o0, W_o1)
        return out + old_x

    def _L0_ffn_ref(x, Wg, W1, b1, W2, b2, ln_g, ln_b, out_g, out_b):
        import jax, jax.numpy as jnp
        import numpy as np
        EPS = 1e-05
        TOP_K = 2

        def layer_norm(x, g, b):
            m = x.mean(-1, keepdims=True)
            v = ((x - m) ** 2).mean(-1, keepdims=True)
            return (x - m) / jnp.sqrt(v + EPS) * g + b
        xn = layer_norm(x, ln_g, ln_b)
        logits = jnp.einsum('bsd,de->bse', xn, Wg)
        probs = jax.nn.softmax(logits, axis=-1)
        top_p, top_i = jax.lax.top_k(probs, TOP_K)
        conf = top_p / top_p.sum(-1, keepdims=True)
        h = jax.nn.gelu(jnp.einsum('bsd,edh->bseh', xn, W1) + b1)
        o = jnp.einsum('bseh,ehd->bsed', h, W2) + b2
        sel = jnp.take_along_axis(o, top_i[..., None], axis=2)
        combined = jnp.einsum('bskd,bsk->bsd', sel, conf)
        return layer_norm(x + combined, out_g, out_b)
    edge_index = jnp.stack([src, dst])
    x = x + _L0_gnn_ref(_layernorm(x, axis=-1), edge_attr_4, edge_attr_32, edge_index, L0_gnn_W_pre0, L0_gnn_b_pre0, L0_gnn_W_pre1, L0_gnn_W_nd0, L0_gnn_b_nd0, L0_gnn_W_nd1, L0_gnn_W_g1, L0_gnn_b_g1, L0_gnn_W_g2, L0_gnn_b_g2, L0_gnn_W_f1, L0_gnn_W_f2, L0_gnn_W_s1, L0_gnn_W_s2, L0_gnn_W_o0, L0_gnn_b_o0, L0_gnn_W_o1)
    x = x + _L0_ffn_ref(_layernorm(x, axis=-1)[None], L0_ffn_Wg, L0_ffn_W1, L0_ffn_b1, L0_ffn_W2, L0_ffn_b2, L0_ffn_ln_g, L0_ffn_ln_b, L0_ffn_out_g, L0_ffn_out_b)[0]
    return x

_drawn_inputs = setup_inputs


def setup_inputs(seed=0):
    import zlib

    import numpy as np

    out = dict(_drawn_inputs(seed))
    spreads = {'L0_gnn_b_pre0': (0.0, 0.8),
     'L0_gnn_b_nd0': (0.0, 0.314),
     'L0_gnn_b_g1': (0.0, 0.1),
     'L0_gnn_b_g2': (0.0, 0.1),
     'L0_gnn_b_o0': (0.0, 0.34),
     'L0_ffn_b1': (0.0, 0.8),
     'L0_ffn_b2': (0.0, 0.33),
     'L0_ffn_ln_g': (1.0, 0.6),
     'L0_ffn_ln_b': (0.0, 0.8),
     'L0_ffn_out_g': (1.0, 0.2),
     'L0_ffn_out_b': (0.0, 0.1)}
    factors = {'L0_gnn_W_pre1': 2.695, 'L0_ffn_W1': 5.683, 'L0_ffn_W2': 5.268}
    for name, (base, spread) in spreads.items():
        noise = np.random.default_rng([zlib.crc32(name.encode()), seed]).standard_normal(out[name].shape)
        drawn = base * np.exp(spread * noise) if base else spread * noise
        out[name] = jnp.asarray(drawn.astype(out[name].dtype))
    for name, factor in factors.items():
        out[name] = (out[name] * factor).astype(out[name].dtype)
    return out
```

```python
from contextlib import ExitStack
import math

import concourse.bass as bass
from concourse import mybir

FP32 = mybir.dt.float32
I32 = mybir.dt.int32
U32 = mybir.dt.uint32
ALU = mybir.AluOpType
ACT = mybir.ActivationFunctionType
AX = mybir.AxisListType

P = 128
N, D = 10000, 512
MUL = 128
NSUB = 4
TILE = NSUB * P
NT = -(-N // TILE)
E = 10000
EP = 125
EC = E // EP
ET = EC // NSUB
HID = 32
NX, EH = 8, 64
QP = HID + 3 * MUL
PX = 3 * MUL + D
ROW = HID + PX
EPS = 1e-5
FAR = 1 << 20
PAD_KEY = 1 << 14
assert EP * EC == E and NT == ET and NT % 2 == 0 and PAD_KEY > N


def after(engine, semaphore, value):
    if not isinstance(value, int) or value > 0:
        engine.wait_ge(semaphore, value)


def pipeline(engine, step, last):
    for s in range(4):
        step(s, s // 2, s % 2)
    with engine.Fori(2, NT // 2 - 1) as k:
        for b in range(2):
            step(2 * k + b, k, b)
    for s in range(NT - 2, last + 1):
        step(s, s // 2, s % 2)


def runs(s, lag):
    return not isinstance(s, int) or 0 <= s - lag < NT


def settled(engine, passed):
    engine.sem_inc(passed, 1)


def wait_all(engine, semaphores, value):
    for semaphore in semaphores:
        engine.wait_ge(semaphore, value)


def base(s):
    return min(TILE * s, N - TILE) if isinstance(s, int) else TILE * s


def before(k, b):
    return k if b else k - 1


def gnn_ffn_kernel(nc, x, src, dst, edge_attr_32, edge_attr_4,
                   W_pre0, b_pre0, W_pre1, W_nd0, b_nd0, W_nd1, W_g1, b_g1, W_g2, b_g2,
                   W_f1, W_f2, W_s1, W_s2, W_o0, b_o0, W_o1,
                   Wg, W1, b1, W2, b2, ln_g, ln_b, out_g, out_b, out):
    by_src = nc.dram_tensor("by_src", [N, QP], FP32, kind="Internal").ap()
    by_dst = nc.dram_tensor("by_dst", [N, PX], FP32, kind="Internal").ap()
    acc = nc.dram_tensor("acc", [N, D], FP32, kind="Internal").ap()

    def rows(dram, s):
        return dram[bass.ds(base(s), TILE), :].rearrange("(p j) d -> p j d", j=NSUB)

    ctx = ExitStack()
    with ctx:
        def sb(name, shape, dtype=FP32):
            return ctx.enter_context(nc.sbuf_tensor(name, shape, dtype))

        def sem(name):
            return ctx.enter_context(nc.semaphore(name))

        ident = sb("ident", [P, P])
        lower = sb("lower", [P, P])
        sel = sb("sel", [NX, NX * EH])
        iota_i = sb("iota_i", [P, NX], I32)
        iota8 = sb("iota8", [P, NX])
        mhalf = sb("mhalf", [P, NSUB])
        eps4 = sb("eps4", [P, NSUB])
        wpre0 = sb("wpre0", [P, MUL])
        wpre0T = sb("wpre0T", [P, MUL])
        wpre1 = sb("wpre1", [P, MUL])
        wnd0 = sb("wnd0", [P, MUL])
        wnd1 = sb("wnd1", [P, MUL])
        wo0 = sb("wo0", [P, MUL])
        wo1 = sb("wo1", [P, MUL])
        wg1 = sb("wg1", [P, 2, 2 * MUL])
        wg2 = sb("wg2", [P, 2, 2 * MUL])
        ws1 = sb("ws1", [P, 3, HID])
        wab = sb("wab", [P, NSUB, HID])
        wq = sb("wq", [P, HID])
        wc = sb("wc", [P, NSUB, P])
        wf1 = sb("wf1", [P, P])
        wf2 = sb("wf2", [P, D])
        ws2 = sb("ws2", [P, D])
        w1 = sb("w1", [P, NSUB, NX * EH])
        w2 = sb("w2", [P, NSUB, D])
        wg = sb("wg", [P, NSUB, NX])
        b2s = sb("b2s", [NX, D])
        cols = sb("cols", [P, 24])
        bpre0_c, bq_c = cols[:, 0:1], cols[:, 1:2]
        bg1_c, bg2_c, half_c = cols[:, 2:4], cols[:, 4:6], cols[:, 6:7]
        lng_c, lnb_c, b1_c, b1p_c = cols[:, 8:12], cols[:, 12:16], cols[:, 16:20], cols[:, 20:24]
        bnd0_r = sb("bnd0_r", [P, MUL])
        bo0_r = sb("bo0_r", [P, MUL])
        outg_r = sb("outg_r", [P, D])
        outb_r = sb("outb_r", [P, D])
        bgate_r = sb("bgate_r", [P, NX])
        stats = sb("stats", [P, NT, 2 * NSUB])
        ea32 = sb("ea32", [P, EC * HID])
        ea4 = sb("ea4", [P, EC * 4])
        key_i = sb("key_i", [P, EC], I32)
        gsrc_i = sb("gsrc_i", [P, EC], I32)
        gdst_i = sb("gdst_i", [P, EC], I32)

        ARENA = 31600
        arena = sb("arena", [P, ARENA])
        at = [0]

        def take(*shape):
            n = math.prod(shape)
            v = arena[:, at[0]:at[0] + n]
            at[0] += n
            assert at[0] <= ARENA, at
            if len(shape) == 2:
                v = v.rearrange("p (a b) -> p a b", a=shape[0])
            return v

        psum = [ctx.enter_context(nc.psum_tensor(f"bank{i}", [P, 512], FP32)) for i in range(8)]

        block = ctx.enter_context(nc.Block())

        w_in = sem("w_in")
        e_in = sem("e_in")
        z_pool = sem("z_pool")
        dve_passed, pool_passed = sem("dve_passed"), sem("pool_passed")
        z_dve = sem("z_dve")
        z_pe = sem("z_pe")
        loads = [(wpre0, W_pre0), (wpre1, W_pre1), (wnd0, W_nd0), (wnd1, W_nd1),
                 (wo0, W_o0), (wo1, W_o1), (b2s, b2)]

        @block.gpsimd
        def _(pool):
            for tile, value in ((ident, 0.0), (lower, 0.0), (sel, 1.0), (mhalf, -0.5), (eps4, EPS),
                                (ea32, 0.0), (ea4, 0.0), (wf1, 0.0), (wc, 0.0)):
                last = nc.gpsimd.memset(tile[:], value)
            nc.gpsimd.memset(half_c, 0.5)
            nc.gpsimd.memset(key_i[:], PAD_KEY)
            nc.gpsimd.memset(gsrc_i[:], 0)
            nc.gpsimd.memset(gdst_i[:], 0).then_inc(z_pool, 1)
            nc.gpsimd.iota(iota_i[:], pattern=[[1, NX]], base=0, channel_multiplier=0).then_inc(z_pool, 1)
            pool.wait_ge(z_pool, 2)
            nc.gpsimd.affine_select(out=ident[:], in_=ident[:], compare_op=ALU.not_equal, fill=1.0,
                                    base=0, pattern=[[-1, P]], channel_multiplier=1)
            nc.gpsimd.affine_select(out=lower[:], in_=lower[:], compare_op=ALU.is_ge, fill=1.0,
                                    base=0, pattern=[[1, P]], channel_multiplier=-1)
            nc.gpsimd.tensor_copy(iota8[:], iota_i[:])
            nc.gpsimd.affine_select(out=sel[:], in_=sel[:], compare_op=ALU.is_ge, fill=0.0,
                                    base=0, pattern=[[1, NX * EH]], channel_multiplier=-EH).then_inc(z_pool, 1)
            pool.wait_ge(z_pool, 3)
            nc.gpsimd.affine_select(out=sel[:], in_=sel[:], compare_op=ALU.is_ge, fill=0.0,
                                    base=EH - 1, pattern=[[-1, NX * EH]], channel_multiplier=EH).then_inc(z_pool, 1)

        W_TOTAL = 16 * (len(loads) + 10 + 2 * NSUB + NSUB + 5 + NSUB)

        @block.scalar
        def _(act):
            n = 0

            def load(dst_ap, src_ap):
                nonlocal n
                act.dma_start(dst_ap, src_ap).then_inc(w_in, 16)
                n += 16

            with nc.allow_non_contiguous_dma(reason="bias columns, once"):
                for tile, dram in loads:
                    load(tile[:], dram)
                load(wg1[:], W_g1.rearrange("(k p) n -> p k n", p=P))
                load(wg2[:], W_g2.rearrange("(k p) n -> p k n", p=P))
                load(ws1[:], W_s1.rearrange("(k p) n -> p k n", p=P))
                load(bpre0_c, b_pre0.rearrange("(p a) -> p a", a=1))
                load(bg1_c, b_g1.rearrange("(k p) -> p k", p=P))
                load(bg2_c, b_g2.rearrange("(k p) -> p k", p=P))
                load(bnd0_r[:], b_nd0.rearrange("(a n) -> a n", a=1).to_broadcast([P, MUL]))
                load(bo0_r[:], b_o0.rearrange("(a n) -> a n", a=1).to_broadcast([P, MUL]))
                load(outg_r[:], out_g.rearrange("(a n) -> a n", a=1).to_broadcast([P, D]))
                load(outb_r[:], out_b.rearrange("(a n) -> a n", a=1).to_broadcast([P, D]))
                for j in range(NSUB):
                    load(wf2[HID * j:HID * (j + 1), :], W_f2)
                    load(ws2[HID * j:HID * (j + 1), :], W_s2)
                for c in range(NSUB):
                    load(w1[:, c, :].rearrange("p (e h) -> p e h", e=NX),
                         W1[:, c * P:(c + 1) * P, :].rearrange("e p h -> p e h"))
                load(w2[:], W2.rearrange("e h d -> (e h) d").rearrange("(k p) d -> p k d", p=P))
                load(wg[:], Wg.rearrange("(k p) n -> p k n", p=P))
                load(lng_c, ln_g.rearrange("(k p) -> p k", p=P))
                load(lnb_c, ln_b.rearrange("(k p) -> p k", p=P))
                load(b1_c, b1.rearrange("e h -> (e h)").rearrange("(k p) -> p k", p=P))
                act.wait_ge(z_pool, 1)
                for j in range(NSUB):
                    act.dma_start(wf1[HID * j:HID * (j + 1), HID * j:HID * (j + 1)], W_f1).then_inc(w_in, 16)
                    n += 16
            assert n == W_TOTAL, n


        @block.tensor
        def _(pe):
            pe.wait_ge(w_in, W_TOTAL)
            pe.wait_ge(z_pool, 4)
            nc.tensor.transpose(psum[0][:, 0:P], wpre0[:], ident[:]).then_inc(z_pe, 1)
            for k in range(NSUB):
                for c in range(NSUB):
                    nc.tensor.matmul(psum[1][:, k:k + 1], w1[:, c, k * P:(k + 1) * P], lnb_c[:, c:c + 1],
                                     start=(c == 0), stop=(c == NSUB - 1))
            for c in range(NSUB):
                last = nc.tensor.matmul(psum[2][:, 0:NX], lnb_c[:, c:c + 1].to_broadcast([P, P]), wg[:, c, :],
                                        start=(c == 0), stop=(c == NSUB - 1))
            last.then_inc(z_pe, 1)
            pe.wait_ge(z_dve, 2)
            nc.tensor.matmul(psum[3][:, 0:HID], wpre0T[:], wab[:, 0, :], start=True, stop=True)
            nc.tensor.matmul(psum[4][:, 0:1], wab[:].rearrange("p j h -> p (j h)"), bpre0_c,
                             start=True, stop=True).then_inc(z_pe, 1)

        @block.vector
        def _(dve):
            dve.wait_ge(w_in, W_TOTAL)
            dve.wait_ge(z_pool, 4)
            nc.vector.tensor_tensor(wab[:], ws1[:, 0:1, :].to_broadcast([P, NSUB, HID]),
                                    ws1[:, 1:2, :].to_broadcast([P, NSUB, HID]), ALU.add).then_inc(z_dve, 1)
            for j in range(NSUB):
                nc.vector.tensor_scalar(wc[:, j, HID * j:HID * (j + 1)], ws1[:, 2, :], 1.0 / 3.0, None, ALU.mult)
            nc.vector.tensor_scalar(ws2[:, 3 * MUL:D], ws2[:, 3 * MUL:D], 1.0 / math.sqrt(3.0), None, ALU.mult)
            dve.wait_ge(z_pe, 1)
            nc.vector.tensor_copy(wpre0T[:], psum[0][:, 0:P]).then_inc(z_dve, 1)
            dve.wait_ge(z_pe, 2)
            nc.vector.tensor_tensor(b1p_c, psum[1][:, 0:NSUB], b1_c, ALU.add)
            nc.vector.tensor_copy(bgate_r[:], psum[2][:, 0:NX])
            for c in range(NSUB):
                nc.vector.tensor_scalar(w1[:, c, :], w1[:, c, :], lng_c[:, c:c + 1], None, ALU.mult)
                nc.vector.tensor_scalar(wg[:, c, :], wg[:, c, :], lng_c[:, c:c + 1], None, ALU.mult)
            dve.wait_ge(z_pe, 3)
            nc.vector.tensor_copy(wq[:], psum[3][:, 0:HID])
            nc.vector.tensor_copy(bq_c, psum[4][:, 0:1]).then_inc(z_dve, 1)

        SETUP_DVE = 3

        @block.sync
        def _(sp):
            sp.wait_ge(z_pool, 1)
            sp.dma_start(ea32[0:EP, :], edge_attr_32.rearrange("(p t) h -> p (t h)", p=EP)).then_inc(e_in, 16)
            sp.dma_start(ea4[0:EP, :], edge_attr_4.rearrange("(p t) h -> p (t h)", p=EP)).then_inc(e_in, 16)
            sp.dma_start(key_i[0:EP, :], src.rearrange("(p t) -> p t", p=EP)).then_inc(e_in, 16)
            sp.dma_start(gsrc_i[0:EP, :], src.rearrange("(p t) -> p t", p=EP)).then_inc(e_in, 16)
            sp.dma_start(gdst_i[0:EP, :], dst.rearrange("(p t) -> p t", p=EP)).then_inc(e_in, 16)

        E_TOTAL = 5 * 16

        a_x = [take(NSUB, D) for _ in range(2)]
        a_xT = [take(4, TILE) for _ in range(2)]
        a_sq = take(3, TILE)
        a_n1 = take(TILE)
        a_g = take(2, TILE)
        a_xg = take(4, TILE)
        a_row = [take(NSUB, ROW) for _ in range(2)]
        a_bn = take(NSUB, 6)
        a_mv = [take(NSUB, 2) for _ in range(2)]
        a_rn = [take(2, NSUB) for _ in range(2)]
        A_T, A_ND, A_P, A_G = psum[0:2], psum[2:4], psum[4:6], psum[6:8]

        x_in = [sem(f"a_x_in{b}") for b in range(2)]
        row_out = [sem(f"a_row_out{b}") for b in range(2)]
        s_bn, s_mv, s_rstd, s_nmr, s_xn = (sem(n) for n in ("a_bn", "a_mv", "a_rstd", "a_nmr", "a_xn"))
        s_var = sem("a_var")
        s_t, s_tact, s_tdve = sem("a_t"), sem("a_t_act"), sem("a_t_dve")
        s_p, s_pev = sem("a_p"), sem("a_p_ev")
        s_sq, s_n1 = sem("a_sq"), sem("a_n1")
        s_g1, s_silu, s_g2, s_g0, s_xg = (sem(n) for n in ("a_g1", "a_silu", "a_g2", "a_g0", "a_xg"))
        s_nd, s_ndev = sem("a_nd"), sem("a_nd_ev")

        @block.sync
        def _(sp):
            def load(s, k, b):
                after(sp, s_t, 4 * (s - 1))
                sp.dma_start(a_x[b], rows(x, s)).then_inc(x_in[b], 16)

            def step(s, k, b):
                if runs(s, -1):
                    load(s + 1, k + b, 1 - b)
                if runs(s, 1):
                    t, o = s - 1, 1 - b
                    sp.wait_ge(s_pev, 4 * s)
                    sp.wait_ge(s_ndev, 4 * s)
                    if isinstance(t, int) and t == NT - 1:
                        sp.wait_ge(row_out[1 - o], 48 * (NT // 2))
                    sp.dma_start(rows(by_src, t), a_row[o][:, :, 0:QP]).then_inc(row_out[o], 16)
                    sp.dma_start(rows(by_dst, t), a_row[o][:, :, HID:ROW]).then_inc(row_out[o], 16)
                    sp.dma_start(rows(acc, t), a_row[o][:, :, QP:ROW]).then_inc(row_out[o], 16)

            load(0, 0, 0)
            pipeline(sp, step, NT)

        @block.vector
        def _(dve):
            def statistics(s, k, b):
                dve.wait_ge(x_in[b], 16 * k + 16)
                for j in range(NSUB):
                    last = nc.vector.bn_stats(a_bn[:, j, :], a_x[b][:, j, :])
                last.then_inc(s_bn, 1)
                dve.wait_ge(s_bn, s + 1)
                if not isinstance(s, int) or s >= 2:
                    dve.wait_ge(s_xn, s - 1)
                settled(dve, dve_passed)
                for j in range(NSUB):
                    last = nc.vector.bn_aggr(a_mv[b][:, j, :], a_bn[:, j, :])
                last.then_inc(s_mv, 1)

            def shift(s, b):
                dve.wait_ge(s_rstd, s + 1)
                nc.vector.scalar_tensor_tensor(out=a_rn[b][:, 1, :], in0=a_mv[b][:, :, 0], scalar=-1.0,
                                               in1=a_rn[b][:, 0, :], op0=ALU.mult, op1=ALU.mult).then_inc(s_nmr, 1)

            def step(s, k, b):
                if runs(s, 0):
                    for c in (1, 3):
                        dve.wait_ge(s_t, 4 * s + c + 1)
                        nc.vector.tensor_copy(a_xT[b][:, c, :], A_T[1][:]).then_inc(s_tdve, 1)
                if runs(s, -1):
                    statistics(s + 1, k + b, 1 - b)
                if runs(s, 1):
                    o, ko = 1 - b, before(k, b)
                    after(dve, row_out[o], 48 * ko)
                    for j in range(NSUB):
                        dve.wait_ge(s_nd, 4 * (s - 1) + j + 1)
                        nc.vector.tensor_tensor(a_row[o][:, j, QP:QP + MUL], A_ND[j % 2][:, 0:MUL], bnd0_r[:], ALU.add)
                        nc.vector.tensor_copy(a_row[o][:, j, QP + MUL:ROW], A_ND[j % 2][:, MUL:D]).then_inc(s_ndev, 1)
                if runs(s, -1):
                    shift(s + 1, 1 - b)
                if runs(s, 0):
                    nc.vector.tensor_copy(stats[:, bass.ds(s, 1), :].rearrange("p a n -> p (a n)"),
                                          a_rn[b].rearrange("p a n -> p (a n)"))
                    dve.wait_ge(s_tact, 2 * s + 2)
                    dve.wait_ge(s_g2, 2 * s + 2)
                    after(dve, s_nd, 4 * s)
                    nc.vector.scalar_tensor_tensor(
                        out=a_xg[:, 1:4, :], in0=A_G[1][:, None, :].to_broadcast([P, 3, TILE]),
                        scalar=bg2_c[:, 1:2], in1=a_xT[b][:, 1:4, :], op0=ALU.add, op1=ALU.mult).then_inc(s_xg, 1)

            statistics(0, 0, 0)
            shift(0, 0)
            dve.wait_ge(s_nmr, 1)
            pipeline(dve, step, NT)

        @block.gpsimd
        def _(pool):
            def rstd(s, b):
                pool.wait_ge(s_mv, s + 1)
                nc.gpsimd.tensor_tensor(a_rn[b][:, 0, :], a_mv[b][:, :, 1], eps4[:], ALU.add).then_inc(s_var, 1)
                pool.wait_ge(s_var, s + 1)
                nc.gpsimd.tensor_tensor(a_rn[b][:, 0, :], a_rn[b][:, 0, :], mhalf[:], ALU.pow).then_inc(s_rstd, 1)

            def step(s, k, b):
                if runs(s, 0):
                    xT = a_xT[b]
                    pool.wait_ge(s_tdve, 2 * s + 2)
                    pool.wait_ge(s_tact, 2 * s + 2)
                    after(pool, s_n1, s)
                    nc.gpsimd.tensor_tensor(a_sq, xT[:, 1:4, :], xT[:, 1:4, :], ALU.mult).then_inc(s_sq, 1)
                    pool.wait_ge(s_sq, 3 * s + 1)
                    nc.gpsimd.tensor_tensor(a_sq[:, 0, :], a_sq[:, 0, :], a_sq[:, 1, :], ALU.add).then_inc(s_sq, 1)
                    pool.wait_ge(s_sq, 3 * s + 2)
                    nc.gpsimd.tensor_tensor(a_sq[:, 0, :], a_sq[:, 0, :], a_sq[:, 2, :], ALU.add).then_inc(s_sq, 1)
                if runs(s, -1):
                    rstd(s + 1, 1 - b)

            rstd(0, 0)
            pipeline(pool, step, NT - 1)

        @block.scalar
        def _(act):
            act.wait_ge(z_dve, SETUP_DVE)

            def normalise(s, b):
                act.wait_ge(s_nmr, s + 1)
                for j in range(NSUB):
                    last = nc.scalar.activation(a_x[b][:, j, :], a_x[b][:, j, :], ACT.Identity,
                                                bias=a_rn[b][:, 1, j:j + 1], scale=a_rn[b][:, 0, j:j + 1])
                last.then_inc(s_xn, 1)

            def step(s, k, b):
                after(act, s_xg, s - 1)
                for c in (0, 2):
                    act.wait_ge(s_t, 4 * s + c + 1)
                    nc.scalar.activation(a_xT[b][:, c, :], A_T[0][:], ACT.Copy).then_inc(s_tact, 1)
                after(act, row_out[b], 48 * k)
                for j in range(NSUB):
                    act.wait_ge(s_p, 4 * s + j + 1)
                    nc.scalar.activation(a_row[b][:, j, 0:QP], A_P[j % 2][:, 0:QP], ACT.Copy).then_inc(s_pev, 1)
                if runs(s, -1):
                    normalise(s + 1, 1 - b)
                act.wait_ge(s_sq, 3 * s + 3)
                after(act, s_g1, 2 * s)
                nc.scalar.activation(a_n1, a_sq[:, 0, :], ACT.Sqrt, scale=1.0 / 3.0).then_inc(s_n1, 1)
                for o in range(2):
                    act.wait_ge(s_g1, 2 * s + o + 1)
                    nc.scalar.activation(a_g[:, o, :], A_G[o][:], ACT.Silu, bias=bg1_c[:, o:o + 1]).then_inc(s_silu, 1)
                act.wait_ge(s_g2, 2 * s + 1)
                after(act, s_nd, 4 * s)
                nc.scalar.activation(a_xg[:, 0, :], A_G[0][:], ACT.Identity, bias=bg2_c[:, 0:1]).then_inc(s_g0, 1)

            normalise(0, 0)
            pipeline(act, step, NT - 1)

        @block.tensor
        def _(pe):
            pe.wait_ge(z_dve, SETUP_DVE)

            def node_features(t):
                pe.wait_ge(s_g0, t + 1)
                pe.wait_ge(s_xg, t + 1)
                for j in range(NSUB):
                    after(pe, s_ndev, 4 * t + j - 1)
                    for c in range(4):
                        last = nc.tensor.matmul(A_ND[j % 2][:, c * MUL:(c + 1) * MUL], a_xg[:, c, j * P:(j + 1) * P],
                                                wnd0[:] if c == 0 else wnd1[:], start=True, stop=True)
                    last.then_inc(s_nd, 1)

            def step(s, k, b):
                if runs(s, 0):
                    pe.wait_ge(s_xn, s + 1)
                    for c in range(4):
                        after(pe, s_tdve if c % 2 else s_tact, 2 * s + c // 2)
                        for j in range(NSUB):
                            v = a_x[b][:, j, 0:MUL] if c == 0 else a_x[b][:, j, MUL + c - 1:D:3]
                            last = nc.tensor.transpose(A_T[c % 2][:, j * P:(j + 1) * P], v, ident[:])
                        last.then_inc(s_t, 1)
                if runs(s, 1):
                    node_features(s - 1)
                if runs(s, 0):
                    xT = a_xT[b]
                    pe.wait_ge(s_tact, 2 * s + 2)
                    pe.wait_ge(s_tdve, 2 * s + 2)
                    for j in range(NSUB):
                        after(pe, s_pev, 4 * s + j - 1)
                        nc.tensor.matmul(A_P[j % 2][:, 0:HID], xT[:, 0, j * P:(j + 1) * P], wq[:], start=True, stop=True)
                        for c in range(3):
                            last = nc.tensor.matmul(A_P[j % 2][:, HID + c * MUL:HID + (c + 1) * MUL],
                                                    xT[:, 1 + c, j * P:(j + 1) * P], wpre1[:], start=True, stop=True)
                        last.then_inc(s_p, 1)
                    pe.wait_ge(s_n1, s + 1)
                    for o in range(2):
                        for c, v in enumerate((xT[:, 0, :], a_n1)):
                            last = nc.tensor.matmul(A_G[o][:], wg1[:, c, o * P:(o + 1) * P], v,
                                                    start=(c == 0), stop=(c == 1))
                        last.then_inc(s_g1, 1)
                    pe.wait_ge(s_silu, 2 * s + 2)
                    for o in range(2):
                        for c in range(2):
                            last = nc.tensor.matmul(A_G[o][:], wg2[:, c, o * P:(o + 1) * P], a_g[:, c, :],
                                                    start=(c == 0), stop=(c == 1))
                        last.then_inc(s_g2, 1)

            pipeline(pe, step, NT)

        at[0] = 0
        b_gs = [take(NSUB, QP) for _ in range(2)]
        b_gd = [take(NSUB, PX) for _ in range(2)]
        b_pr = [take(3, MUL) for _ in range(2)]
        b_ip = take(NSUB, MUL)
        b_ipT = take(TILE)
        b_q = take(NSUB, HID)
        b_ea = take(P)
        b_eaT = take(P)
        b_hp = take(2 * P)
        b_ln = take(2 * P)
        b_hh = take(2 * P)
        b_wa = [take(D) for _ in range(2)]
        b_w = take(4, MUL)
        b_y = [take(8, MUL) for _ in range(2)]
        b_s = [take(NSUB, P) for _ in range(2)]
        b_sl = take(NSUB, P)
        b_sm = [take(4, P) for _ in range(2)]
        b_out = [take(D) for _ in range(2)]
        b_key = [take(NSUB) for _ in range(2)]
        b_cnt = take(NSUB)
        b_sh = [take(NSUB, 4) for _ in range(2)]
        b_gsi = [sb(f"b_gsi{b}", [P, NSUB], U32) for b in range(2)]
        b_gdi = [sb(f"b_gdi{b}", [P, NSUB], U32) for b in range(2)]
        b_sci = [sb(f"b_sci{b}", [P, NSUB], U32) for b in range(2)]
        B_A, B_B, B_AGG, B_T, B_H = psum[0:2], psum[2:4], psum[4:6], psum[6], psum[7]

        gather = [[sem(f"b_gather{b}{j}") for j in range(NSUB)] for b in range(2)]
        added = sem("b_added")
        q_idx, q_ea, q_pr, q_ip, q_ipt, q_ipe = (sem(f"b_{n}") for n in ("idx", "ea", "pr", "ip", "ipt", "ipe"))
        q_eat, q_eae, q_h, q_hp, q_act, q_hh = (sem(f"b_{n}") for n in ("eat", "eae", "h", "hp", "act", "hh"))
        q_ab, q_ae, q_w, q_y, q_sm, q_agg, q_oe = (sem(f"b_{n}") for n in ("ab", "ae", "w", "y", "sm", "agg", "oe"))
        q_q, q_sh = sem("b_q"), sem("b_sh")
        q_tr, q_s, q_sl, q_cnt, q_sci = (sem(f"b_{n}") for n in ("tr", "s", "sl", "cnt", "sci"))

        @block.vector
        def _(dve):
            dve.wait_ge(e_in, E_TOTAL)
            wait_all(dve, row_out, 48 * (NT // 2))

            def indices(s, k, b):
                after(dve, q_sci, s - 1)
                nc.vector.tensor_copy(b_gsi[b][:], gsrc_i[:, bass.ds(s * NSUB, NSUB)])
                nc.vector.tensor_copy(b_gdi[b][:], gdst_i[:, bass.ds(s * NSUB, NSUB)])
                nc.vector.tensor_copy(b_key[b], key_i[:, bass.ds(s * NSUB, NSUB)]).then_inc(q_idx, 1)

            def factors(s, b):
                after(dve, q_sm, 4 * (s - 1))
                nc.vector.tensor_copy(b_sh[b].rearrange("p j m -> p (j m)"),
                                      ea4[:, bass.ds(s * NSUB * 4, NSUB * 4)]).then_inc(q_sh, 1)

            def products(s, k, b, j):
                dve.wait_ge(gather[b][j], 32 * k + 32)
                after(dve, q_ip, 4 * s + j - 1)
                if j == 0:
                    after(dve, q_ipt, s)
                nc.vector.tensor_tensor(b_pr[j % 2].rearrange("p c u -> p (c u)"), b_gs[b][:, j, HID:QP],
                                        b_gd[b][:, j, 0:3 * MUL], ALU.mult).then_inc(q_pr, 1)
                dve.wait_ge(q_pr, 4 * s + j + 1)
                nc.vector.tensor_reduce(out=b_ip[:, j, :], in_=b_pr[j % 2].rearrange("p c u -> p u c"),
                                        axis=AX.X, op=ALU.add).then_inc(q_ip, 1)

            def collect_q(s, b):
                after(dve, q_h, s)
                nc.vector.tensor_copy(b_q, b_gs[b][:, :, 0:HID]).then_inc(q_q, 1)

            def shared_targets(s, k, b):
                dve.wait_ge(q_tr, s + 1)
                nc.vector.tensor_tensor(b_s[b], B_T[:].rearrange("p (j e) -> p j e", j=NSUB),
                                        b_key[b][:, :, None].to_broadcast([P, NSUB, P]), ALU.is_equal).then_inc(q_s, 1)
                dve.wait_ge(q_s, s + 1)
                nc.vector.tensor_tensor(b_sl, b_s[b], lower[:, None, :].to_broadcast([P, NSUB, P]),
                                        ALU.mult).then_inc(q_sl, 1)
                dve.wait_ge(q_sl, s + 1)
                nc.vector.tensor_reduce(out=b_cnt, in_=b_sl, axis=AX.X, op=ALU.add).then_inc(q_cnt, 1)
                dve.wait_ge(q_cnt, s + 1)
                after(dve, added, 64 * (s - 1))
                nc.vector.scalar_tensor_tensor(out=b_sci[b][:], in0=b_cnt, scalar=float(FAR), in1=b_key[b],
                                               op0=ALU.mult, op1=ALU.add).then_inc(q_sci, 1)

            def softplus_end(s, k, b):
                dve.wait_ge(q_act, 3 * s + 3)
                after(dve, q_ab, 4 * s)
                nc.vector.scalar_tensor_tensor(out=b_hh, in0=b_hp, scalar=0.0, in1=b_ln,
                                               op0=ALU.max, op1=ALU.add).then_inc(q_hh, 1)

            def messages(t, o, j):
                n = 4 * t + j
                feat = b_gd[o][:, j, 3 * MUL:PX].rearrange("p (c u) -> p c u", u=MUL)
                y = b_y[j % 2]
                dve.wait_ge(q_ae, n + 1)
                dve.wait_ge(q_ab, n + 1)
                after(dve, q_y, n)
                nc.vector.tensor_tensor(b_w.rearrange("p c u -> p (c u)"), b_wa[j % 2], B_B[j % 2][:],
                                        ALU.mult).then_inc(q_w, 1)
                dve.wait_ge(q_w, n + 1)
                after(dve, q_agg, n - 1)
                nc.vector.tensor_tensor(y[:, 0:8:7, :], b_w[:, 0:2, :],
                                        feat[:, 0:1, :].to_broadcast([P, 2, MUL]), ALU.mult)
                nc.vector.tensor_tensor(y[:, 1:7, :].rearrange("p (k c) u -> p k c u", k=2),
                                        b_w[:, 2:4, None, :].to_broadcast([P, 2, 3, MUL]),
                                        feat[:, None, 1:4, :].to_broadcast([P, 2, 3, MUL]), ALU.mult).then_inc(q_y, 1)

            def step(s, k, b):
                t, o = s - 1, 1 - b
                if runs(s, -1):
                    indices(s + 1, k + b, o)
                for j in range(NSUB):
                    if runs(s, 1) and j < 3:
                        messages(t, o, j)
                    if runs(s, 0):
                        products(s, k, b, j)
                if runs(s, 0):
                    collect_q(s, b)
                if runs(s, 1):
                    messages(t, o, 3)
                if runs(s, 0):
                    shared_targets(s, k, b)
                    softplus_end(s, k, b)
                    factors(s, b)

            indices(0, 0, 0)
            pipeline(dve, step, ET)

        @block.gpsimd
        def _(pool):
            wait_all(pool, row_out, 48 * (NT // 2))

            def fetch(s, k, b, j):
                if j == 0:
                    pool.wait_ge(q_idx, s + 1)
                if not isinstance(s, int) or s >= 2:
                    pool.wait_ge(q_y, 4 * (s - 2) + j + 1)
                settled(pool, pool_passed)
                nc.gpsimd.indirect_dma_start(
                    out=b_gs[b][:, j, :], out_offset=None, in_=by_src[:, :],
                    in_offset=bass.IndirectOffsetOnAxis(ap=b_gsi[b][:, j:j + 1], axis=0)).then_inc(gather[b][j], 16)
                nc.gpsimd.indirect_dma_start(
                    out=b_gd[b][:, j, :], out_offset=None, in_=by_dst[:, :],
                    in_offset=bass.IndirectOffsetOnAxis(ap=b_gdi[b][:, j:j + 1], axis=0)).then_inc(gather[b][j], 16)

            def step(s, k, b):
                for j in range(NSUB):
                    if runs(s, -1):
                        fetch(s + 1, k + b, 1 - b, j)
                    if runs(s, 1):
                        t, o = s - 1, 1 - b
                        n = 4 * t + j
                        pool.wait_ge(q_oe, n + 1)
                        pool.wait_ge(q_sci, t + 1)
                        after(pool, added, 16 * n)
                        settled(pool, pool_passed)
                        nc.gpsimd.indirect_dma_start(
                            out=acc[:, :], out_offset=bass.IndirectOffsetOnAxis(ap=b_sci[o][:, j:j + 1], axis=0),
                            in_=b_out[j % 2], in_offset=None, bounds_check=N - 1, oob_is_err=False,
                            compute_op=ALU.add).then_inc(added, 16)

            for j in range(NSUB):
                fetch(0, 0, 0, j)
            pipeline(pool, step, ET)

        @block.scalar
        def _(act):
            wait_all(act, row_out, 48 * (NT // 2))
            nc.scalar.preload_act_table_set("natural_log_exp_and_others")

            def hidden(s, k, b):
                act.wait_ge(q_ipt, s + 1)
                after(act, q_h, s)
                nc.scalar.activation(b_ipT, B_T[:], ACT.Copy).then_inc(q_ipe, 1)
                act.wait_ge(q_eat, s + 1)
                nc.scalar.activation(b_eaT, B_H[:, 0:P], ACT.Copy).then_inc(q_eae, 1)
                act.wait_ge(q_h, s + 1)
                after(act, q_hh, s)
                nc.scalar.activation(b_hp[:, 0:P], B_H[:, P:2 * P], ACT.Copy)
                nc.scalar.activation(b_hp[:, P:2 * P], B_H[:, 2 * P:3 * P], ACT.Identity,
                                     bias=bq_c).then_inc(q_hp, 1)
                act.wait_ge(q_hp, s + 1)
                nc.scalar.activation(b_ln, b_hp, ACT.Abs).then_inc(q_act, 1)
                act.wait_ge(q_act, 3 * s + 1)
                nc.scalar.activation(b_ln, b_ln, ACT.Exp, scale=-1.0).then_inc(q_act, 1)
                act.wait_ge(q_act, 3 * s + 2)
                nc.scalar.activation(b_ln, b_ln, ACT.Ln, bias=half_c, scale=0.5).then_inc(q_act, 1)

            def weights(t, o, j):
                n = 4 * t + j
                act.wait_ge(q_ab, n + 1)
                after(act, q_w, n - 1)
                nc.scalar.activation(b_wa[j % 2], B_A[j % 2][:], ACT.Copy).then_inc(q_ae, 1)

            def scaled(t, o, j):
                n = 4 * t + j
                act.wait_ge(q_s, t + 1)
                act.wait_ge(q_sh, t + 1)
                after(act, q_agg, n - 1)
                for m in range(4):
                    last = nc.scalar.activation(b_sm[j % 2][:, m, :], b_s[o][:, j, :], ACT.Copy,
                                                scale=b_sh[o][:, j, m:m + 1])
                last.then_inc(q_sm, 1)

            def sums(t, o, j):
                n = 4 * t + j
                act.wait_ge(q_agg, n + 1)
                after(act, added, 16 * (n - 1))
                nc.scalar.activation(b_out[j % 2], B_AGG[j % 2][:], ACT.Copy).then_inc(q_oe, 1)

            def step(s, k, b):
                t, o = s - 1, 1 - b
                if runs(s, 0):
                    after(act, q_eat, s)
                    if isinstance(s, int) and s == 0:
                        act.wait_ge(e_in, E_TOTAL)
                    nc.scalar.activation(b_ea, ea32[:, bass.ds(s * P, P)], ACT.Copy).then_inc(q_ea, 1)
                if runs(s, 1):
                    weights(t, o, 0)
                    scaled(t, o, 0)
                    for j in range(1, NSUB):
                        weights(t, o, j)
                        scaled(t, o, j)
                        sums(t, o, j - 1)
                if runs(s, 0):
                    hidden(s, k, b)
                if runs(s, 1):
                    sums(t, o, NSUB - 1)

            pipeline(act, step, ET)

        @block.tensor
        def _(pe):
            wait_all(pe, row_out, 48 * (NT // 2))

            def hidden(s, k, b):
                after(pe, q_s, s)
                for j in range(NSUB):
                    pe.wait_ge(q_ip, 4 * s + j + 1)
                    last = nc.tensor.transpose(B_T[:, j * P:(j + 1) * P], b_ip[:, j, :], ident[:])
                last.then_inc(q_ipt, 1)
                pe.wait_ge(q_ea, s + 1)
                after(pe, q_hp, s)
                nc.tensor.transpose(B_H[:, 0:P], b_ea, ident[:]).then_inc(q_eat, 1)
                pe.wait_ge(q_eae, s + 1)
                nc.tensor.matmul(B_H[:, P:2 * P], wf1[:], b_eaT, start=True, stop=True)
                pe.wait_ge(q_ipe, s + 1)
                for j in range(NSUB):
                    nc.tensor.matmul(B_H[:, 2 * P:3 * P], wc[:, j, :], b_ipT[:, j * P:(j + 1) * P],
                                     start=(j == 0), stop=False)
                pe.wait_ge(q_q, s + 1)
                nc.tensor.matmul(B_H[:, 2 * P:3 * P], b_q.rearrange("p j h -> p (j h)"), ident[:],
                                 start=False, stop=True).then_inc(q_h, 1)
                for j in range(NSUB):
                    last = nc.tensor.transpose(B_T[:, j * P:(j + 1) * P], b_key[b][:, j:j + 1].to_broadcast([P, P]),
                                               ident[:])
                last.then_inc(q_tr, 1)

            def weights(t, j):
                n = 4 * t + j
                if j == 0:
                    pe.wait_ge(q_hh, t + 1)
                after(pe, q_ae, n - 1)
                after(pe, q_w, n - 1)
                part = slice(HID * j, HID * (j + 1))
                nc.tensor.matmul(B_A[j % 2][:], b_hh[part, 0:P], wf2[part, :], start=True, stop=True)
                nc.tensor.matmul(B_B[j % 2][:], b_hh[part, P:2 * P], ws2[part, :], start=True, stop=True).then_inc(q_ab, 1)

            def aggregate(t, j):
                n = 4 * t + j
                pe.wait_ge(q_sm, n + 1)
                pe.wait_ge(q_y, n + 1)
                after(pe, q_oe, n - 1)
                y, sm = b_y[j % 2], b_sm[j % 2]
                agg = B_AGG[j % 2][:].rearrange("p (c u) -> p c u", u=MUL)
                nc.tensor.matmul(agg, sm[:, 0, :], y[:, 0:4, :], start=True, stop=False)
                for c in range(3):
                    last = nc.tensor.matmul(agg[:, 0:c + 2:c + 1, :], sm[:, 1 + c, :], y[:, 4 + c:8:3 - c, :],
                                            start=False, stop=(c == 2))
                last.then_inc(q_agg, 1)

            def step(s, k, b):
                t = s - 1
                if runs(s, 1):
                    weights(t, 0)
                    weights(t, 1)
                    aggregate(t, 0)
                    weights(t, 2)
                    aggregate(t, 1)
                    weights(t, 3)
                    aggregate(t, 2)
                if runs(s, 0):
                    hidden(s, k, b)
                if runs(s, 1):
                    aggregate(t, 3)

            pipeline(pe, step, ET)

        at[0] = 0
        c_h = [take(NSUB, D) for _ in range(2)]
        c_x = [take(NSUB, D) for _ in range(2)]
        c_hT = take(4, TILE)
        c_x2 = [take(NSUB, D) for _ in range(2)]
        c_xh = take(NSUB, D)
        c_xhT = take(4, TILE)
        c_g = [take(TILE) for _ in range(2)]
        c_hg = take(4, TILE)
        c_xn = [take(D) for _ in range(2)]
        c_z = [take(NSUB, D) for _ in range(2)]
        c_r = [take(NSUB, D) for _ in range(2)]
        c_sc = [take(2, NSUB) for _ in range(2)]
        c_bn, c_bz = take(NSUB, 6), take(NSUB, 6)
        c_mv = [take(NSUB, 2) for _ in range(2)]
        c_st = [take(4, NSUB) for _ in range(2)]
        c_tmp = take(NSUB)
        c_mz = [take(NSUB, 2) for _ in range(2)]
        c_rz = [take(2, NSUB) for _ in range(2)]
        c_lg, c_mx, c_o1, c_o2 = (take(NSUB, NX) for _ in range(4))
        c_if = take(NSUB, 2)
        c_d, c_th = take(NSUB), take(NSUB)
        c_w12 = take(2, NSUB)
        c_mi = sb("c_mi", [P, NSUB, NX], U32)
        c_cT = sb("c_cT", [NX, TILE])
        C_T, C_O, C_HB, C_EX, C_L = psum[0:2], psum[2:4], psum[4:6], psum[6], psum[7]

        c_in = [sem(f"c_in{b}") for b in range(2)]
        c_out = [sem(f"c_out{b}") for b in range(2)]
        (t1, t1act, t1dve, u_sc, u_xs, u_xb, u_o, u_x2, u_bn, u_mv, u_pool, u_nm, u_xh, u_t2, t2act, t2dve) = (
            sem(f"c_{n}") for n in ("t1", "t1act", "t1dve", "sc", "xs", "xb", "o", "x2", "bn", "mv", "pool", "nm",
                                    "xh", "t2", "t2act", "t2dve"))
        (v_l, v_lg, v_d, v_th, v_chain, v_cf, v_ct, v_cte, v_h, v_ge, v_ex, v_hg, v_w2, v_xn, v_z, v_bz, v_mz, v_pz,
         v_nz, v_zh, v_r, v_zg, v_fin) = (
            sem(f"c_{n}") for n in ("l", "lg", "d", "th", "chain", "cf", "ct", "cte", "h", "ge", "ex", "hg", "w2",
                                    "xn", "z", "bz", "mz", "pz", "nz", "zh", "r", "zg", "fin"))

        @block.sync
        def _(sp):
            sp.wait_ge(added, 16 * EC)

            def load(s, k, b):
                after(sp, t1, 4 * (s - 1))
                after(sp, u_x2, 4 * (s - 1))
                sp.dma_start(c_h[b], rows(acc, s)).then_inc(c_in[b], 16)
                sp.dma_start(c_x[b], rows(x, s)).then_inc(c_in[b], 16)

            def step(s, k, b):
                if runs(s, -1):
                    load(s + 1, k + b, 1 - b)
                if runs(s, 2):
                    t = s - 2
                    sp.wait_ge(v_fin, s - 1)
                    if isinstance(t, int) and t == NT - 1:
                        sp.wait_ge(c_out[1 - b], 16 * (NT // 2))
                    sp.dma_start(rows(out, t), c_z[b]).then_inc(c_out[b], 16)

            load(0, 0, 0)
            pipeline(sp, step, NT + 1)
            for b in range(2):
                sp.wait_ge(c_out[b], 16 * (NT // 2))

        @block.vector
        def _(dve):
            dve.wait_ge(added, 16 * EC)

            def copy_chunks(sem_in, sem_out, n, to):
                for c in (1, 3):
                    dve.wait_ge(sem_in, 4 * n + c + 1)
                    nc.vector.tensor_copy(to[:, c, :], C_T[1][:]).then_inc(sem_out, 1)

            def scale(s, b):
                after(dve, u_xs, s - 1)
                at_s = stats[:, bass.ds(s, 1), :].rearrange("p a n -> p (a n)")
                nc.vector.tensor_scalar(c_sc[b][:, 0, :], at_s[:, 0:NSUB], 1.0, None, ALU.add)
                nc.vector.tensor_copy(c_sc[b][:, 1, :], at_s[:, NSUB:2 * NSUB]).then_inc(u_sc, 1)

            def residual(s, b):
                dve.wait_ge(u_xb, s + 1)
                after(dve, u_xh, s - 1)
                after(dve, v_r, s - 1)
                after(dve, v_xn, 4 * (s - 1))
                for j in range(NSUB):
                    dve.wait_ge(u_o, 4 * s + j + 1)
                    x2v = c_x2[b][:, j, MUL:D].rearrange("p (u c) -> p c u", c=3)
                    xv = c_x[b][:, j, MUL:D].rearrange("p (u c) -> p c u", c=3)
                    ov = C_O[j % 2][:, MUL:D].rearrange("p (c u) -> p c u", c=3)
                    nc.vector.tensor_tensor(c_x2[b][:, j, 0:MUL], C_O[j % 2][:, 0:MUL], c_x[b][:, j, 0:MUL], ALU.add)
                    nc.vector.tensor_tensor(x2v, ov, xv, ALU.add).then_inc(u_x2, 1)
                for j in range(NSUB):
                    dve.wait_ge(u_x2, 4 * s + j + 1)
                    last = nc.vector.bn_stats(c_bn[:, j, :], c_x2[b][:, j, :])
                last.then_inc(u_bn, 1)
                dve.wait_ge(u_bn, s + 1)
                settled(dve, dve_passed)
                for j in range(NSUB):
                    last = nc.vector.bn_aggr(c_mv[b][:, j, :], c_bn[:, j, :])
                last.then_inc(u_mv, 1)

            def shifts(s, b):
                dve.wait_ge(u_pool, 7 * s + 7)
                nc.vector.scalar_tensor_tensor(
                    out=c_st[b][:, 2:4, :], in0=c_st[b][:, 0:2, :], scalar=-1.0,
                    in1=c_mv[b][:, None, :, 0].to_broadcast([P, 2, NSUB]), op0=ALU.mult, op1=ALU.mult).then_inc(u_nm, 1)

            def top2(t):
                dve.wait_ge(v_l, t + 1)
                nc.vector.tensor_tensor(c_lg, C_L[:, 0:NSUB * NX].rearrange("p (j e) -> p j e", j=NSUB),
                                        bgate_r[:, None, :].to_broadcast([P, NSUB, NX]), ALU.add).then_inc(v_lg, 1)
                dve.wait_ge(v_lg, t + 1)
                settled(dve, dve_passed)
                for j in range(NSUB):
                    last = nc.vector.max(out=c_mx[:, j, :], in_=c_lg[:, j, :])
                last.then_inc(v_chain, 1)
                dve.wait_ge(v_chain, 4 * t + 1)
                after(dve, v_th, t)
                nc.vector.tensor_tensor(c_d, c_mx[:, :, 0], c_mx[:, :, 1], ALU.subtract).then_inc(v_d, 1)
                for j in range(NSUB):
                    last = nc.vector.max_index(out=c_mi[:, j, :], in_max=c_mx[:, j, :], in_values=c_lg[:, j, :])
                last.then_inc(v_chain, 1)
                dve.wait_ge(v_chain, 4 * t + 2)
                nc.vector.tensor_copy(c_if, c_mi[:, :, 0:2]).then_inc(v_chain, 1)
                dve.wait_ge(v_chain, 4 * t + 3)
                after(dve, v_ct, t)
                for i, o in enumerate((c_o1, c_o2)):
                    nc.vector.tensor_tensor(o, iota8[:, None, :].to_broadcast([P, NSUB, NX]),
                                            c_if[:, :, i:i + 1].to_broadcast([P, NSUB, NX]), ALU.is_equal)
                dve.wait_ge(v_th, t + 1)
                nc.vector.tensor_scalar(c_w12[:, 0, :], c_th, 0.5, 0.5, ALU.mult, ALU.add)
                nc.vector.tensor_scalar(c_w12[:, 1, :], c_th, -0.5, 0.5, ALU.mult, ALU.add).then_inc(v_chain, 1)
                dve.wait_ge(v_chain, 4 * t + 4)
                for i, o in enumerate((c_o1, c_o2)):
                    last = nc.vector.tensor_tensor(o, o, c_w12[:, i, :, None].to_broadcast([P, NSUB, NX]), ALU.mult)
                last.then_inc(v_cf, 1)
                dve.wait_ge(v_cf, 2 * t + 1)
                nc.vector.tensor_tensor(c_o1, c_o1, c_o2, ALU.add).then_inc(v_cf, 1)

            def experts(t):
                for q in range(4):
                    dve.wait_ge(v_ge, 4 * t + q + 1)
                    dve.wait_ge(v_ex, 4 * t + q + 1)
                    nc.vector.tensor_tensor(c_hg[:, q, :], C_EX[:], c_g[q % 2], ALU.mult).then_inc(v_hg, 1)

            def second_residual(t, o, k):
                after(dve, c_out[o], 16 * k)
                for j in range(NSUB):
                    dve.wait_ge(v_w2, 4 * t + j + 1)
                    dve.wait_ge(v_xn, 4 * t + j + 1)
                    nc.vector.tensor_tensor(c_z[o][:, j, :], C_O[j % 2][:], c_xn[j % 2], ALU.add).then_inc(v_z, 1)
                for j in range(NSUB):
                    dve.wait_ge(v_z, 4 * t + j + 1)
                    last = nc.vector.bn_stats(c_bz[:, j, :], c_z[o][:, j, :])
                last.then_inc(v_bz, 1)
                dve.wait_ge(v_bz, t + 1)
                settled(dve, dve_passed)
                for j in range(NSUB):
                    last = nc.vector.bn_aggr(c_mz[o][:, j, :], c_bz[:, j, :])
                last.then_inc(v_mz, 1)

            def shift_z(t, b):
                dve.wait_ge(v_pz, 2 * t + 2)
                nc.vector.scalar_tensor_tensor(out=c_rz[b][:, 1, :], in0=c_mz[b][:, :, 0], scalar=-1.0,
                                               in1=c_rz[b][:, 0, :], op0=ALU.mult, op1=ALU.mult).then_inc(v_nz, 1)

            def finish(t, b):
                dve.wait_ge(v_zg, t + 1)
                nc.vector.tensor_tensor(c_z[b], c_z[b], c_r[b], ALU.add).then_inc(v_fin, 1)

            def step(s, k, b):
                if runs(s, 2):
                    shift_z(s - 2, b)
                if runs(s, 0):
                    copy_chunks(t1, t1dve, s, c_hT)
                    residual(s, b)
                if runs(s, -1):
                    scale(s + 1, 1 - b)
                if runs(s, 1):
                    copy_chunks(u_t2, t2dve, s - 1, c_xhT)
                if runs(s, 0):
                    shifts(s, b)
                if runs(s, 1):
                    top2(s - 1)
                if runs(s, 2):
                    finish(s - 2, b)
                if runs(s, 1):
                    experts(s - 1)
                    second_residual(s - 1, 1 - b, before(k, b))

            scale(0, 0)
            pipeline(dve, step, NT + 1)

        @block.gpsimd
        def _(pool):
            pool.wait_ge(added, 16 * EC)
            pool.wait_ge(z_dve, SETUP_DVE)

            def moments(s, b):
                var, st = c_mv[b][:, :, 1], c_st[b]
                ops = [lambda: nc.gpsimd.tensor_tensor(c_tmp, var, eps4[:], ALU.add),
                       lambda: nc.gpsimd.tensor_tensor(st[:, 0, :], c_tmp, mhalf[:], ALU.pow),
                       lambda: nc.gpsimd.tensor_tensor(c_tmp, st[:, 0, :], st[:, 0, :], ALU.mult),
                       lambda: nc.gpsimd.tensor_tensor(c_tmp, c_tmp, var, ALU.mult),
                       lambda: nc.gpsimd.tensor_tensor(c_tmp, c_tmp, eps4[:], ALU.add),
                       lambda: nc.gpsimd.tensor_tensor(c_tmp, c_tmp, mhalf[:], ALU.pow),
                       lambda: nc.gpsimd.tensor_tensor(st[:, 1, :], c_tmp, st[:, 0, :], ALU.mult)]
                pool.wait_ge(u_mv, s + 1)
                after(pool, v_xn, 4 * (s - 1))
                for i, op in enumerate(ops):
                    op().then_inc(u_pool, 1)
                    pool.wait_ge(u_pool, 7 * s + i + 1)

            def step(s, k, b):
                if runs(s, 0):
                    pool.wait_ge(u_xs, s + 1)
                    nc.gpsimd.tensor_tensor(c_x[b][:, :, 0:MUL], c_x[b][:, :, 0:MUL],
                                            bo0_r[:, None, :].to_broadcast([P, NSUB, MUL]), ALU.add).then_inc(u_xb, 1)
                    moments(s, b)
                if runs(s, 2):
                    pool.wait_ge(v_zh, s - 1)
                    nc.gpsimd.tensor_tensor(c_z[b], c_z[b], outg_r[:, None, :].to_broadcast([P, NSUB, D]),
                                            ALU.mult).then_inc(v_zg, 1)
                if runs(s, 1):
                    o = 1 - b
                    after(pool, v_fin, s - 2)
                    nc.gpsimd.tensor_tensor(c_r[o], c_x2[o], outb_r[:, None, :].to_broadcast([P, NSUB, D]),
                                            ALU.add).then_inc(v_r, 1)
                    pool.wait_ge(v_mz, s)
                    after(pool, v_zh, s - 2)
                    nc.gpsimd.tensor_tensor(c_rz[o][:, 0, :], c_mz[o][:, :, 1], eps4[:], ALU.add).then_inc(v_pz, 1)
                    pool.wait_ge(v_pz, 2 * s - 1)
                    nc.gpsimd.tensor_tensor(c_rz[o][:, 0, :], c_rz[o][:, 0, :], mhalf[:], ALU.pow).then_inc(v_pz, 1)

            pipeline(pool, step, NT + 1)

        @block.scalar
        def _(act):
            act.wait_ge(added, 16 * EC)
            nc.scalar.preload_act_table_set("gelu_apprx_tanh_and_others")

            def copy_chunks(sem_in, sem_out, n, to):
                for c in (0, 2):
                    act.wait_ge(sem_in, 4 * n + c + 1)
                    nc.scalar.activation(to[:, c, :], C_T[0][:], ACT.Copy).then_inc(sem_out, 1)

            def scale_x(s, k, b):
                act.wait_ge(c_in[b], 32 * k + 32)
                act.wait_ge(u_sc, s + 1)
                for j in range(NSUB):
                    last = nc.scalar.activation(c_x[b][:, j, :], c_x[b][:, j, :], ACT.Identity,
                                                bias=c_sc[b][:, 1, j:j + 1], scale=c_sc[b][:, 0, j:j + 1])
                last.then_inc(u_xs, 1)

            def normalise(s, b):
                act.wait_ge(u_nm, s + 1)
                after(act, u_t2, 4 * s)
                for j in range(NSUB):
                    last = nc.scalar.activation(c_xh[:, j, :], c_x2[b][:, j, :], ACT.Identity,
                                                bias=c_st[b][:, 3, j:j + 1], scale=c_st[b][:, 1, j:j + 1])
                last.then_inc(u_xh, 1)

            def first_norm(t, o, j):
                after(act, v_z, 4 * t + j - 1)
                nc.scalar.activation(c_xn[j % 2], c_x2[o][:, j, :], ACT.Identity,
                                     bias=c_st[o][:, 2, j:j + 1], scale=c_st[o][:, 0, j:j + 1]).then_inc(v_xn, 1)

            def gelu(t, q):
                act.wait_ge(v_h, 4 * t + q + 1)
                after(act, v_hg, 4 * t + q - 1)
                nc.scalar.activation(c_g[q % 2], C_HB[q % 2][:], ACT.Gelu_apprx_tanh,
                                     bias=b1p_c[:, q:q + 1]).then_inc(v_ge, 1)

            def step(s, k, b):
                t, o = s - 1, 1 - b
                if runs(s, 0):
                    copy_chunks(t1, t1act, s, c_hT)
                if runs(s, 2):
                    act.wait_ge(v_nz, s - 1)
                    for j in range(NSUB):
                        last = nc.scalar.activation(c_z[b][:, j, :], c_z[b][:, j, :], ACT.Identity,
                                                    bias=c_rz[b][:, 1, j:j + 1], scale=c_rz[b][:, 0, j:j + 1])
                    last.then_inc(v_zh, 1)
                if runs(s, 1):
                    copy_chunks(u_t2, t2act, t, c_xhT)
                    act.wait_ge(v_d, t + 1)
                    after(act, v_cf, 2 * t)
                    nc.scalar.activation(c_th, c_d, ACT.Tanh, scale=0.5).then_inc(v_th, 1)
                    gelu(t, 0)
                    act.wait_ge(v_ct, t + 1)
                    after(act, v_w2, 4 * t)
                    nc.scalar.activation(c_cT[:], C_L[0:NX, :], ACT.Copy).then_inc(v_cte, 1)
                    gelu(t, 1)
                    gelu(t, 2)
                    first_norm(t, o, 0)
                    first_norm(t, o, 1)
                    gelu(t, 3)
                if runs(s, 0):
                    normalise(s, b)
                if runs(s, -1):
                    scale_x(s + 1, k + b, o)
                if runs(s, 1):
                    first_norm(t, o, 2)
                    first_norm(t, o, 3)

            scale_x(0, 0, 0)
            pipeline(act, step, NT + 1)

        @block.tensor
        def _(pe):
            pe.wait_ge(added, 16 * EC)

            def project(s, k, b):
                pe.wait_ge(c_in[b], 32 * k + 32)
                for c in range(4):
                    if c < 2:
                        after(pe, t2dve if c % 2 else t2act, 2 * (s - 1))
                    after(pe, t1dve if c % 2 else t1act, 2 * s + c // 2)
                    for j in range(NSUB):
                        last = nc.tensor.transpose(C_T[c % 2][:, j * P:(j + 1) * P], c_h[b][:, j, c * P:(c + 1) * P],
                                                   ident[:])
                    last.then_inc(t1, 1)
                pe.wait_ge(t1act, 2 * s + 2)
                pe.wait_ge(t1dve, 2 * s + 2)
                for j in range(NSUB):
                    if j < 2:
                        after(pe, v_z, 4 * (s - 1) + j - 1)
                    after(pe, u_x2, 4 * s + j - 1)
                    for c in range(4):
                        last = nc.tensor.matmul(C_O[j % 2][:, c * MUL:(c + 1) * MUL], c_hT[:, c, j * P:(j + 1) * P],
                                                wo0[:] if c == 0 else wo1[:], start=True, stop=True)
                    last.then_inc(u_o, 1)

            def transpose_x(s):
                t = s - 1
                pe.wait_ge(u_xh, t + 1)
                for c in range(4):
                    if runs(s, 0):
                        pe.wait_ge(t1dve if c % 2 else t1act, 2 * s + 2)
                    after(pe, t2dve if c % 2 else t2act, 2 * t + c // 2)
                    for j in range(NSUB):
                        last = nc.tensor.transpose(C_T[c % 2][:, j * P:(j + 1) * P], c_xh[:, j, c * P:(c + 1) * P],
                                                   ident[:])
                    last.then_inc(u_t2, 1)
                pe.wait_ge(t2act, 2 * t + 2)
                pe.wait_ge(t2dve, 2 * t + 2)

            def logits(t):
                after(pe, v_cte, t)
                for j in range(NSUB):
                    for c in range(4):
                        last = nc.tensor.matmul(C_L[:, j * NX:(j + 1) * NX], c_xhT[:, c, j * P:(j + 1) * P], wg[:, c, :],
                                                start=(c == 0), stop=(c == 3))
                last.then_inc(v_l, 1)

            def hidden(t, q):
                after(pe, v_ge, 4 * t + q - 1)
                for c in range(4):
                    last = nc.tensor.matmul(C_HB[q % 2][:], w1[:, c, q * P:(q + 1) * P], c_xhT[:, c, :],
                                            start=(c == 0), stop=(c == 3))
                last.then_inc(v_h, 1)

            def spread(t, q):
                after(pe, v_hg, 4 * t + q)
                nc.tensor.matmul(C_EX[:], sel[:, q * P:(q + 1) * P], c_cT[:], start=True, stop=True).then_inc(v_ex, 1)

            def step(s, k, b):
                t = s - 1
                if runs(s, 0):
                    project(s, k, b)
                if runs(s, 1):
                    transpose_x(s)
                    logits(t)
                    hidden(t, 0)
                    hidden(t, 1)
                    pe.wait_ge(v_cf, 2 * t + 2)
                    for j in range(NSUB):
                        last = nc.tensor.transpose(C_L[0:NX, j * P:(j + 1) * P], c_o1[:, j, :], ident[:])
                    last.then_inc(v_ct, 1)
                    pe.wait_ge(v_cte, t + 1)
                    spread(t, 0)
                    hidden(t, 2)
                    spread(t, 1)
                    hidden(t, 3)
                    spread(t, 2)
                    spread(t, 3)
                    pe.wait_ge(v_hg, 4 * t + 4)
                    for j in range(NSUB):
                        if j < 2:
                            if runs(s, 0):
                                pe.wait_ge(u_x2, 4 * s + j + 3)
                            else:
                                pe.wait_ge(v_z, 4 * (t - 1) + j + 3)
                        else:
                            pe.wait_ge(v_z, 4 * t + j - 1)
                        nc.tensor.matmul(C_O[j % 2][:], c_cT[:, j * P:(j + 1) * P], b2s[:], start=True, stop=False)
                        for q in range(4):
                            last = nc.tensor.matmul(C_O[j % 2][:], c_hg[:, q, j * P:(j + 1) * P], w2[:, q, :],
                                                    start=False, stop=(q == 3))
                        last.then_inc(v_w2, 1)

            pipeline(pe, step, NT)


_INS = ['x', 'src', 'dst', 'edge_attr_32', 'edge_attr_4',
        'L0_gnn_W_pre0', 'L0_gnn_b_pre0', 'L0_gnn_W_pre1', 'L0_gnn_W_nd0', 'L0_gnn_b_nd0', 'L0_gnn_W_nd1',
        'L0_gnn_W_g1', 'L0_gnn_b_g1', 'L0_gnn_W_g2', 'L0_gnn_b_g2', 'L0_gnn_W_f1', 'L0_gnn_W_f2',
        'L0_gnn_W_s1', 'L0_gnn_W_s2', 'L0_gnn_W_o0', 'L0_gnn_b_o0', 'L0_gnn_W_o1',
        'L0_ffn_Wg', 'L0_ffn_W1', 'L0_ffn_b1', 'L0_ffn_W2', 'L0_ffn_b2',
        'L0_ffn_ln_g', 'L0_ffn_ln_b', 'L0_ffn_out_g', 'L0_ffn_out_b']


def kernel(**inputs):
    import numpy as _np
    import concourse.bacc as _bacc
    from concourse import mybir as _mybir
    from concourse.bass_utils import run_bass_kernel_spmd as _run

    nc = _bacc.Bacc("TRN2", target_bir_lowering=False, num_devices=1)
    arrays, args = {}, []
    for name in _INS:
        a = _np.ascontiguousarray(inputs[name])
        arrays[f"in_{name}"] = a
        args.append(nc.dram_tensor(f"in_{name}", a.shape, _mybir.dt.from_np(a.dtype), kind="ExternalInput").ap())
    args.append(nc.dram_tensor("out_x", (N, D), FP32, kind="ExternalOutput").ap())
    gnn_ffn_kernel(nc, *args)
    r = _run(nc, [arrays], core_ids=[0])
    return r.results[0]["out_x"]
```

```python
from contextlib import ExitStack
import math

import concourse.bass as bass
from concourse import mybir

FP32 = mybir.dt.float32
FP32R = mybir.dt.float32r
I32 = mybir.dt.int32
U32 = mybir.dt.uint32
ALU = mybir.AluOpType
ACT = mybir.ActivationFunctionType
AX = mybir.AxisListType

P = 128
N, D = 10000, 512
MUL = 128
NSUB = 4
TILE = NSUB * P
NT = -(-N // TILE)
E = 10000
EP = 125
EC = E // EP
ET = EC // NSUB
HID = 32
NX, EH = 8, 64
QP = HID + 3 * MUL
PX = 3 * MUL + D
ROW = HID + PX
EPS = 1e-5
FAR = 1 << 20
PAD_KEY = 1 << 14
assert EP * EC == E and NT == ET and NT % 2 == 0 and PAD_KEY > N


def after(engine, semaphore, value):
    if not isinstance(value, int) or value > 0:
        engine.wait_ge(semaphore, value)


def pipeline(engine, step, last, tail=2):
    for s in range(4):
        step(s, s // 2, s % 2)
    with engine.Fori(2, (NT - tail) // 2) as k:
        for b in range(2):
            step(2 * k + b, k, b)
    for s in range(NT - tail, last + 1):
        step(s, s // 2, s % 2)


def runs(s, lag):
    return not isinstance(s, int) or 0 <= s - lag < NT


def settled(engine, passed):
    engine.sem_inc(passed, 1)


def wait_all(engine, semaphores, value):
    for semaphore in semaphores:
        engine.wait_ge(semaphore, value)


def base(s):
    return min(TILE * s, N - TILE) if isinstance(s, int) else TILE * s


def before(k, b):
    return k if b else k - 1


def gnn_ffn_kernel(nc, x, src, dst, edge_attr_32, edge_attr_4,
                   W_pre0, b_pre0, W_pre1, W_nd0, b_nd0, W_nd1, W_g1, b_g1, W_g2, b_g2,
                   W_f1, W_f2, W_s1, W_s2, W_o0, b_o0, W_o1,
                   Wg, W1, b1, W2, b2, ln_g, ln_b, out_g, out_b, out):
    by_src = nc.dram_tensor("by_src", [N, QP], FP32, kind="Internal").ap()
    by_dst = nc.dram_tensor("by_dst", [N, PX], FP32, kind="Internal").ap()
    acc = nc.dram_tensor("acc", [N + P, D], FP32, kind="Internal").ap()

    def rows(dram, s):
        return dram[bass.ds(base(s), TILE), :].rearrange("(p j) d -> p j d", j=NSUB)

    ctx = ExitStack()
    with ctx:
        def sb(name, shape, dtype=FP32):
            return ctx.enter_context(nc.sbuf_tensor(name, shape, dtype))

        def sem(name):
            return ctx.enter_context(nc.semaphore(name))

        ident = sb("ident", [P, P])
        lower = sb("lower", [P, P])
        sel = sb("sel", [3 * NX, NX * EH], FP32R)
        b2s = sb("b2s", [3 * NX, D], FP32R)
        middle = sb("middle", [3 * NX, 1])
        iota_i = sb("iota_i", [P, NX], I32)
        iota8 = sb("iota8", [P, NX])
        mhalf = sb("mhalf", [P, NSUB])
        spare_i = sb("spare_i", [P, NSUB], I32)
        spare = sb("spare", [P, NSUB])
        zeros = sb("zeros", [P, D])
        eps4 = sb("eps4", [P, NSUB])
        wpre0 = sb("wpre0", [P, MUL])
        wpre0T = sb("wpre0T", [P, MUL])
        wpre1 = sb("wpre1", [P, MUL])
        wnd0 = sb("wnd0", [P, MUL])
        wnd1 = sb("wnd1", [P, MUL])
        wo0 = sb("wo0", [P, MUL])
        wo1 = sb("wo1", [P, MUL])
        wg1 = sb("wg1", [P, 2, 2 * MUL])
        wg2 = sb("wg2", [P, 2, 2 * MUL])
        ws1 = sb("ws1", [P, 3, HID])
        wab = sb("wab", [P, NSUB, HID])
        wq = sb("wq", [P, HID])
        wc = sb("wc", [P, NSUB, P])
        wf1 = sb("wf1", [P, P])
        w1_hi, w1_lo = (sb(f"w1_{p}", [P, NSUB, NX * EH], FP32R) for p in ("hi", "lo"))
        w2_hi, w2_lo = (sb(f"w2_{p}", [P, NSUB, D], FP32R) for p in ("hi", "lo"))
        wg_parts = sb("wg_parts", [P, NSUB, P], FP32R)
        bgate_c = sb("bgate_c", [2 * NX, 1])
        fold = sb("fold", [2 * NX, NX])
        cols = sb("cols", [P, 24])
        bpre0_c, bq_c = cols[:, 0:1], cols[:, 1:2]
        bg1_c, bg2_c, half_c = cols[:, 2:4], cols[:, 4:6], cols[:, 6:7]
        lng_c, lnb_c, b1_c, b1p_c = cols[:, 8:12], cols[:, 12:16], cols[:, 16:20], cols[:, 20:24]
        bnd0_r = sb("bnd0_r", [P, MUL])
        bo0_r = sb("bo0_r", [P, MUL])
        outg_r = sb("outg_r", [P, D])
        outb_r = sb("outb_r", [P, D])
        stats = sb("stats", [P, NT, 2 * NSUB])
        ea32 = sb("ea32", [P, EC * HID])
        ea4 = sb("ea4", [P, EC * 4])
        key_i = sb("key_i", [P, EC], I32)
        gsrc_i = sb("gsrc_i", [P, EC], I32)
        gdst_i = sb("gdst_i", [P, EC], I32)

        ARENA = 21400
        arena = sb("arena", [P, ARENA])
        at = [0]

        def take(*shape):
            n = math.prod(shape)
            v = arena[:, at[0]:at[0] + n]
            at[0] += n
            assert at[0] <= ARENA, at
            if len(shape) == 2:
                v = v.rearrange("p (a b) -> p a b", a=shape[0])
            return v

        def parts(w_hi, w_lo, a_hi, a_lo):
            return ((w_hi, a_hi), (w_hi, a_lo), (w_lo, a_hi))

        xhT_hi, xhT_lo = (sb(f"xhT_{p}", [P, 4, TILE], FP32R) for p in ("hi", "lo"))
        hg_hi, hg_lo = (sb(f"hg_{p}", [P, 4, TILE], FP32R) for p in ("hi", "lo"))

        wf2_hi, wf2_lo = xhT_hi[:, 0, :], xhT_lo[:, 0, :]
        ws2_hi, ws2_lo = xhT_hi[:, 1, :], xhT_lo[:, 1, :]
        hh_hi, hh_lo = hg_hi[:, 1, 0:2 * P], hg_lo[:, 1, 0:2 * P]

        SETUP_AT = 13400
        at[0] = SETUP_AT
        w1, w2 = take(NSUB, NX * EH), take(NSUB, D)
        b2_raw, sel_a, sel_c = (take(D)[0:3 * NX, :] for _ in range(3))
        wg = take(NSUB, P)
        wf2, ws2 = take(D), take(D)

        psum = [ctx.enter_context(nc.psum_tensor(f"bank{i}", [P, 512], FP32)) for i in range(8)]

        block = ctx.enter_context(nc.Block())

        w_in = sem("w_in")
        e_in = sem("e_in")
        z_pool = sem("z_pool")
        z_scaled, z_hi2 = sem("z_scaled"), sem("z_hi2")
        z_hi, z_lo = sem("z_hi"), sem("z_lo")
        dve_passed, pool_passed = sem("dve_passed"), sem("pool_passed")
        z_dve = sem("z_dve")
        z_pe = sem("z_pe")
        loads = [(wpre0, W_pre0), (wpre1, W_pre1), (wnd0, W_nd0), (wnd1, W_nd1),
                 (wo0, W_o0), (wo1, W_o1)]

        @block.gpsimd
        def _(pool):
            nc.gpsimd.memset(sel_a, 1.0)
            nc.gpsimd.memset(sel_c, 1.0)
            nc.gpsimd.memset(wg, 0.0)
            nc.gpsimd.memset(bgate_c[:], 0.0)
            for tile, value in ((ident, 0.0), (lower, 0.0), (middle, -1.0), (mhalf, -0.5), (eps4, EPS),
                                (ea32, 0.0), (ea4, 0.0), (wf1, 0.0), (wc, 0.0)):
                last = nc.gpsimd.memset(tile[:], value)
            nc.gpsimd.memset(half_c, 0.5)
            nc.gpsimd.memset(zeros[:], 0.0)
            nc.gpsimd.iota(spare_i[:], pattern=[[0, NSUB]], base=N, channel_multiplier=1)
            nc.gpsimd.memset(key_i[:], PAD_KEY)
            nc.gpsimd.memset(gsrc_i[:], 0)
            nc.gpsimd.memset(gdst_i[:], 0).then_inc(z_pool, 1)
            nc.gpsimd.iota(iota_i[:], pattern=[[1, NX]], base=0, channel_multiplier=0).then_inc(z_pool, 1)
            pool.wait_ge(z_pool, 2)
            nc.gpsimd.affine_select(out=ident[:], in_=ident[:], compare_op=ALU.not_equal, fill=1.0,
                                    base=0, pattern=[[-1, P]], channel_multiplier=1)
            nc.gpsimd.affine_select(out=lower[:], in_=lower[:], compare_op=ALU.is_ge, fill=1.0,
                                    base=0, pattern=[[1, P]], channel_multiplier=-1)
            nc.gpsimd.tensor_copy(iota8[:], iota_i[:])
            nc.gpsimd.tensor_copy(spare[:], spare_i[:])
            nc.gpsimd.affine_select(out=middle[:], in_=middle[:], compare_op=ALU.is_ge, fill=0.0,
                                    base=-NX, pattern=[[0, 1]], channel_multiplier=1)
            for tile, first in ((sel_a, 0), (sel_c, 2 * NX)):
                last = nc.gpsimd.affine_select(out=tile, in_=tile, compare_op=ALU.is_ge, fill=0.0,
                                               base=EH * first, pattern=[[1, NX * EH]], channel_multiplier=-EH)
            last.then_inc(z_pool, 1)
            pool.wait_ge(z_pool, 3)
            nc.gpsimd.affine_select(out=middle[:], in_=middle[:], compare_op=ALU.is_ge, fill=0.0,
                                    base=2 * NX - 1, pattern=[[0, 1]], channel_multiplier=-1)
            for tile, first in ((sel_a, 0), (sel_c, 2 * NX)):
                last = nc.gpsimd.affine_select(out=tile, in_=tile, compare_op=ALU.is_ge, fill=0.0,
                                               base=EH - 1 - EH * first, pattern=[[-1, NX * EH]], channel_multiplier=EH)
            last.then_inc(z_pool, 1)
            pool.wait_ge(z_hi, 1)
            nc.gpsimd.tensor_tensor(w1_lo[:], w1, w1_hi[:].bitcast(FP32), ALU.subtract)
            nc.gpsimd.tensor_tensor(wg_parts[:, :, NX:2 * NX], wg[:, :, 0:NX], wg_parts[:, :, 0:NX].bitcast(FP32),
                                    ALU.subtract).then_inc(z_lo, 1)

        W_TOTAL = 16 * (len(loads) + 10 + 2 * NSUB + NSUB + 5 + 3 + NSUB)

        @block.scalar
        def _(act):
            n = 0

            def load(dst_ap, src_ap):
                nonlocal n
                act.dma_start(dst_ap, src_ap).then_inc(w_in, 16)
                n += 16

            with nc.allow_non_contiguous_dma(reason="bias columns, once"):
                for tile, dram in loads:
                    load(tile[:], dram)
                load(wg1[:], W_g1.rearrange("(k p) n -> p k n", p=P))
                load(wg2[:], W_g2.rearrange("(k p) n -> p k n", p=P))
                load(ws1[:], W_s1.rearrange("(k p) n -> p k n", p=P))
                load(bpre0_c, b_pre0.rearrange("(p a) -> p a", a=1))
                load(bg1_c, b_g1.rearrange("(k p) -> p k", p=P))
                load(bg2_c, b_g2.rearrange("(k p) -> p k", p=P))
                load(bnd0_r[:], b_nd0.rearrange("(a n) -> a n", a=1).to_broadcast([P, MUL]))
                load(bo0_r[:], b_o0.rearrange("(a n) -> a n", a=1).to_broadcast([P, MUL]))
                load(outg_r[:], out_g.rearrange("(a n) -> a n", a=1).to_broadcast([P, D]))
                load(outb_r[:], out_b.rearrange("(a n) -> a n", a=1).to_broadcast([P, D]))
                for j in range(NSUB):
                    load(wf2[HID * j:HID * (j + 1), :], W_f2)
                    load(ws2[HID * j:HID * (j + 1), :], W_s2)
                for c in range(NSUB):
                    load(w1[:, c, :].rearrange("p (e h) -> p e h", e=NX),
                         W1[:, c * P:(c + 1) * P, :].rearrange("e p h -> p e h"))
                load(w2, W2.rearrange("e h d -> (e h) d").rearrange("(k p) d -> p k d", p=P))
                for r in range(3):
                    load(b2_raw[r * NX:(r + 1) * NX, :], b2)
                load(lng_c, ln_g.rearrange("(k p) -> p k", p=P))
                load(lnb_c, ln_b.rearrange("(k p) -> p k", p=P))
                load(b1_c, b1.rearrange("e h -> (e h)").rearrange("(k p) -> p k", p=P))
                act.wait_ge(z_pool, 1)
                load(wg[:, :, 0:NX], Wg.rearrange("(k p) n -> p k n", p=P))
                for j in range(NSUB):
                    act.dma_start(wf1[HID * j:HID * (j + 1), HID * j:HID * (j + 1)], W_f1).then_inc(w_in, 16)
                    n += 16
            assert n == W_TOTAL, n


        @block.tensor
        def _(pe):
            pe.wait_ge(w_in, W_TOTAL)
            pe.wait_ge(z_pool, 4)
            nc.tensor.transpose(psum[0][:, 0:P], wpre0[:], ident[:]).then_inc(z_pe, 1)
            for k in range(NSUB):
                for c in range(NSUB):
                    nc.tensor.matmul(psum[1][:, k:k + 1], w1[:, c, k * P:(k + 1) * P], lnb_c[:, c:c + 1],
                                     start=(c == 0), stop=(c == NSUB - 1))
            for c in range(NSUB):
                last = nc.tensor.matmul(psum[2][0:NX, 0:1], wg[:, c, 0:NX], lnb_c[:, c:c + 1],
                                        start=(c == 0), stop=(c == NSUB - 1))
            last.then_inc(z_pe, 1)
            pe.wait_ge(z_dve, 2)
            nc.tensor.matmul(psum[3][:, 0:HID], wpre0T[:], wab[:, 0, :], start=True, stop=True)
            nc.tensor.matmul(psum[4][:, 0:1], wab[:].rearrange("p j h -> p (j h)"), bpre0_c,
                             start=True, stop=True).then_inc(z_pe, 1)

        @block.vector
        def _(dve):
            dve.wait_ge(w_in, W_TOTAL)
            dve.wait_ge(z_pool, 4)
            nc.vector.tensor_tensor(wab[:], ws1[:, 0:1, :].to_broadcast([P, NSUB, HID]),
                                    ws1[:, 1:2, :].to_broadcast([P, NSUB, HID]), ALU.add).then_inc(z_dve, 1)
            nc.vector.tensor_copy(w2_hi[:], w2)
            nc.vector.tensor_tensor(sel[:], sel_a, sel_c, ALU.add)
            b2_hi = hg_hi[0:3 * NX, 0, :]
            nc.vector.tensor_copy(b2_hi, b2_raw).then_inc(z_hi2, 1)
            for j in range(NSUB):
                nc.vector.tensor_scalar(wc[:, j, HID * j:HID * (j + 1)], ws1[:, 2, :], 1.0 / 3.0, None, ALU.mult)
            nc.vector.tensor_scalar(ws2[:, 3 * MUL:D], ws2[:, 3 * MUL:D], 1.0 / math.sqrt(3.0), None, ALU.mult)
            nc.vector.tensor_copy(wf2_hi, wf2).then_inc(z_hi2, 1)
            dve.wait_ge(z_hi2, 2)
            nc.vector.tensor_copy(ws2_hi, ws2).then_inc(z_hi2, 1)
            nc.vector.tensor_tensor(wf2_lo, wf2, wf2_hi.bitcast(FP32), ALU.subtract)
            nc.vector.tensor_tensor(w2_lo[:], w2, w2_hi[:].bitcast(FP32), ALU.subtract)
            nc.vector.scalar_tensor_tensor(out=b2s[:], in0=b2_hi.bitcast(FP32), scalar=middle[:, 0:1], in1=b2_raw,
                                           op0=ALU.mult, op1=ALU.add)
            dve.wait_ge(z_hi2, 3)
            nc.vector.tensor_tensor(ws2_lo, ws2, ws2_hi.bitcast(FP32), ALU.subtract)
            dve.wait_ge(z_pe, 1)
            nc.vector.tensor_copy(wpre0T[:], psum[0][:, 0:P]).then_inc(z_dve, 1)
            dve.wait_ge(z_pe, 2)
            nc.vector.tensor_tensor(b1p_c, psum[1][:, 0:NSUB], b1_c, ALU.add)
            nc.vector.tensor_copy(bgate_c[0:NX, :], psum[2][0:NX, 0:1])
            nc.vector.tensor_tensor(fold[:], ident[0:2 * NX, 0:NX], ident[0:2 * NX, NX:2 * NX], ALU.add)
            for c in range(NSUB):
                nc.vector.tensor_scalar(w1[:, c, :], w1[:, c, :], lng_c[:, c:c + 1], None, ALU.mult)
                last = nc.vector.tensor_scalar(wg[:, c, 0:NX], wg[:, c, 0:NX], lng_c[:, c:c + 1], None, ALU.mult)
            last.then_inc(z_scaled, 1)
            dve.wait_ge(z_scaled, 1)
            nc.vector.tensor_copy(w1_hi[:], w1)
            nc.vector.tensor_copy(wg_parts[:], wg).then_inc(z_hi, 1)
            dve.wait_ge(z_pe, 3)
            nc.vector.tensor_copy(wq[:], psum[3][:, 0:HID])
            nc.vector.tensor_copy(bq_c, psum[4][:, 0:1]).then_inc(z_dve, 1)

        SETUP_DVE = 3

        @block.sync
        def _(sp):
            sp.wait_ge(z_pool, 1)
            sp.dma_start(acc[N:N + P, :], zeros[:]).then_inc(e_in, 16)
            sp.dma_start(ea32[0:EP, :], edge_attr_32.rearrange("(p t) h -> p (t h)", p=EP)).then_inc(e_in, 16)
            sp.dma_start(ea4[0:EP, :], edge_attr_4.rearrange("(p t) h -> p (t h)", p=EP)).then_inc(e_in, 16)
            sp.dma_start(key_i[0:EP, :], src.rearrange("(p t) -> p t", p=EP)).then_inc(e_in, 16)
            sp.dma_start(gsrc_i[0:EP, :], src.rearrange("(p t) -> p t", p=EP)).then_inc(e_in, 16)
            sp.dma_start(gdst_i[0:EP, :], dst.rearrange("(p t) -> p t", p=EP)).then_inc(e_in, 16)

        E_TOTAL = 6 * 16

        at[0] = 0
        a_x = [take(NSUB, D) for _ in range(2)]
        a_xT = [take(4, TILE) for _ in range(2)]
        a_sq = take(3, TILE)
        a_n1 = take(TILE)
        a_g = take(2, TILE)
        a_xg = take(4, TILE)
        a_bn = take(NSUB, 6)
        a_mv = [take(NSUB, 2) for _ in range(2)]
        a_rn = [take(2, NSUB) for _ in range(2)]
        assert at[0] <= SETUP_AT
        a_qp = [take(NSUB, QP) for _ in range(2)]
        a_ft = [take(NSUB, D) for _ in range(2)]
        A_T, A_ND, A_P, A_G = psum[0:2], psum[2:4], psum[4:6], psum[6:8]

        x_in = [sem(f"a_x_in{b}") for b in range(2)]
        qp_out = [sem(f"a_qp_out{b}") for b in range(2)]
        ft_out = [sem(f"a_ft_out{b}") for b in range(2)]
        row_out = qp_out + ft_out
        s_bn, s_mv, s_rstd, s_nmr, s_xn = (sem(n) for n in ("a_bn", "a_mv", "a_rstd", "a_nmr", "a_xn"))
        s_var = sem("a_var")
        s_t, s_tact, s_tdve = sem("a_t"), sem("a_t_act"), sem("a_t_dve")
        s_p, s_pact, s_pdve = sem("a_p"), sem("a_p_act"), sem("a_p_dve")
        s_sq, s_n1 = sem("a_sq"), sem("a_n1")
        s_g1, s_silu, s_g2, s_g0, s_xg = (sem(n) for n in ("a_g1", "a_silu", "a_g2", "a_g0", "a_xg"))
        s_nd, s_ndev = sem("a_nd"), sem("a_nd_ev")


        @block.sync
        def _(sp):
            def load(s, k, b):
                after(sp, s_t, 4 * (s - 1))
                sp.dma_start(a_x[b], rows(x, s)).then_inc(x_in[b], 16)

            def step(s, k, b):
                if runs(s, -2):
                    load(s + 2, k + 1, b)
                if runs(s, 2):
                    t = s - 2
                    sp.wait_ge(s_ndev, 4 * (s - 1))
                    if isinstance(t, int) and t == NT - 1:
                        sp.wait_ge(ft_out[1 - b], 32 * (NT // 2))
                    sp.dma_start(rows(by_dst, t)[:, :, 3 * MUL:PX], a_ft[b]).then_inc(ft_out[b], 16)
                    sp.dma_start(rows(acc, t), a_ft[b]).then_inc(ft_out[b], 16)
                if runs(s, 0):
                    sp.wait_ge(s_pact, 2 * s + 2)
                    sp.wait_ge(s_pdve, 2 * s + 2)
                    if isinstance(s, int) and s == NT - 1:
                        sp.wait_ge(qp_out[1 - b], 32 * (NT // 2))
                    sp.dma_start(rows(by_src, s), a_qp[b]).then_inc(qp_out[b], 16)
                    sp.dma_start(rows(by_dst, s)[:, :, 0:3 * MUL], a_qp[b][:, :, HID:QP]).then_inc(qp_out[b], 16)

            load(0, 0, 0)
            load(1, 0, 1)
            pipeline(sp, step, NT + 1, tail=4)

        @block.vector
        def _(dve):
            def statistics(s, k, b):
                dve.wait_ge(x_in[b], 16 * k + 16)
                for j in range(NSUB):
                    last = nc.vector.bn_stats(a_bn[:, j, :], a_x[b][:, j, :])
                last.then_inc(s_bn, 1)
                dve.wait_ge(s_bn, s + 1)
                if not isinstance(s, int) or s >= 2:
                    dve.wait_ge(s_xn, s - 1)
                settled(dve, dve_passed)
                for j in range(NSUB):
                    last = nc.vector.bn_aggr(a_mv[b][:, j, :], a_bn[:, j, :])
                last.then_inc(s_mv, 1)

            def shift(s, b):
                dve.wait_ge(s_rstd, s + 1)
                nc.vector.scalar_tensor_tensor(out=a_rn[b][:, 1, :], in0=a_mv[b][:, :, 0], scalar=-1.0,
                                               in1=a_rn[b][:, 0, :], op0=ALU.mult, op1=ALU.mult).then_inc(s_nmr, 1)

            def transposed(s, b, c):
                dve.wait_ge(s_t, 4 * s + c + 1)
                nc.vector.tensor_copy(a_xT[b][:, c, :], A_T[1][:]).then_inc(s_tdve, 1)

            def features(u, j, b):
                dve.wait_ge(s_nd, 4 * u + j + 1)
                nc.vector.tensor_tensor(a_ft[b][:, j, 0:MUL], A_ND[j % 2][:, 0:MUL], bnd0_r[:], ALU.add)
                nc.vector.tensor_copy(a_ft[b][:, j, MUL:D], A_ND[j % 2][:, MUL:D]).then_inc(s_ndev, 1)

            def step(s, k, b):
                t, u, o = s - 1, s - 2, 1 - b
                if runs(s, 0):
                    after(dve, s_xg, s - 1)
                    transposed(s, b, 1)
                if runs(s, -1):
                    statistics(s + 1, k + b, o)
                if runs(s, 0):
                    transposed(s, b, 3)
                if runs(s, 2):
                    after(dve, ft_out[b], 32 * (k - 1))
                    features(u, 0, b)
                    features(u, 1, b)
                if runs(s, -1):
                    shift(s + 1, o)
                if runs(s, 2):
                    features(u, 2, b)
                    features(u, 3, b)
                if runs(s, 0):
                    nc.vector.tensor_copy(stats[:, bass.ds(s, 1), :].rearrange("p a n -> p (a n)"),
                                          a_rn[b].rearrange("p a n -> p (a n)"))
                if runs(s, 1):
                    dve.wait_ge(s_tact, 2 * t + 2)
                    dve.wait_ge(s_g2, 2 * t + 2)
                    after(dve, s_nd, 4 * t)
                    nc.vector.scalar_tensor_tensor(
                        out=a_xg[:, 1:4, :], in0=A_G[1][:, None, :].to_broadcast([P, 3, TILE]),
                        scalar=bg2_c[:, 1:2], in1=a_xT[o][:, 1:4, :], op0=ALU.add, op1=ALU.mult).then_inc(s_xg, 1)
                if runs(s, 0):
                    if isinstance(s, int) and s == 0:
                        dve.wait_ge(z_lo, 1)
                    after(dve, qp_out[b], 32 * k)
                    for j in (1, 3):
                        dve.wait_ge(s_p, 4 * s + j + 1)
                        nc.vector.tensor_copy(a_qp[b][:, j, :], A_P[1][:, 0:QP]).then_inc(s_pdve, 1)

            statistics(0, 0, 0)
            shift(0, 0)
            dve.wait_ge(s_nmr, 1)
            pipeline(dve, step, NT + 1)

        @block.gpsimd
        def _(pool):
            def rstd(s, b):
                pool.wait_ge(s_mv, s + 1)
                nc.gpsimd.tensor_tensor(a_rn[b][:, 0, :], a_mv[b][:, :, 1], eps4[:], ALU.add).then_inc(s_var, 1)
                pool.wait_ge(s_var, s + 1)
                nc.gpsimd.tensor_tensor(a_rn[b][:, 0, :], a_rn[b][:, 0, :], mhalf[:], ALU.pow).then_inc(s_rstd, 1)

            def step(s, k, b):
                if runs(s, -1):
                    rstd(s + 1, 1 - b)
                xT = a_xT[b]
                pool.wait_ge(s_tdve, 2 * s + 2)
                pool.wait_ge(s_tact, 2 * s + 2)
                after(pool, s_n1, s)
                nc.gpsimd.tensor_tensor(a_sq, xT[:, 1:4, :], xT[:, 1:4, :], ALU.mult).then_inc(s_sq, 1)
                pool.wait_ge(s_sq, 3 * s + 1)
                nc.gpsimd.tensor_tensor(a_sq[:, 0, :], a_sq[:, 0, :], a_sq[:, 1, :], ALU.add).then_inc(s_sq, 1)
                pool.wait_ge(s_sq, 3 * s + 2)
                nc.gpsimd.tensor_tensor(a_sq[:, 0, :], a_sq[:, 0, :], a_sq[:, 2, :], ALU.add).then_inc(s_sq, 1)

            rstd(0, 0)
            pipeline(pool, step, NT - 1)

        @block.scalar
        def _(act):
            act.wait_ge(z_dve, SETUP_DVE)

            def normalise(s, b):
                act.wait_ge(s_nmr, s + 1)
                for j in range(NSUB):
                    last = nc.scalar.activation(a_x[b][:, j, :], a_x[b][:, j, :], ACT.Identity,
                                                bias=a_rn[b][:, 1, j:j + 1], scale=a_rn[b][:, 0, j:j + 1])
                last.then_inc(s_xn, 1)

            def transposed(s, b, c):
                act.wait_ge(s_t, 4 * s + c + 1)
                nc.scalar.activation(a_xT[b][:, c, :], A_T[0][:], ACT.Copy).then_inc(s_tact, 1)

            def step(s, k, b):
                t, o = s - 1, 1 - b
                if runs(s, 0):
                    after(act, s_xg, s - 1)
                    transposed(s, b, 0)
                if runs(s, 1):
                    after(act, s_g2, 2 * t)
                    for o_ in range(2):
                        act.wait_ge(s_g1, 2 * t + o_ + 1)
                        nc.scalar.activation(a_g[:, o_, :], A_G[o_][:], ACT.Silu,
                                             bias=bg1_c[:, o_:o_ + 1]).then_inc(s_silu, 1)
                if runs(s, 0):
                    transposed(s, b, 2)
                if runs(s, -1):
                    normalise(s + 1, o)
                if runs(s, 1):
                    act.wait_ge(s_g2, 2 * t + 1)
                    after(act, s_nd, 4 * t)
                    nc.scalar.activation(a_xg[:, 0, :], A_G[0][:], ACT.Identity, bias=bg2_c[:, 0:1]).then_inc(s_g0, 1)
                if runs(s, 0):
                    if isinstance(s, int) and s == 0:
                        act.wait_ge(z_lo, 1)
                    after(act, qp_out[b], 32 * k)
                    for j in (0, 2):
                        act.wait_ge(s_p, 4 * s + j + 1)
                        nc.scalar.activation(a_qp[b][:, j, :], A_P[0][:, 0:QP], ACT.Copy).then_inc(s_pact, 1)
                    act.wait_ge(s_sq, 3 * s + 3)
                    after(act, s_g1, 2 * s)
                    nc.scalar.activation(a_n1, a_sq[:, 0, :], ACT.Sqrt, scale=1.0 / 3.0).then_inc(s_n1, 1)

            normalise(0, 0)
            pipeline(act, step, NT)

        @block.tensor
        def _(pe):
            pe.wait_ge(z_dve, SETUP_DVE)

            def transpose_x(s, b, chunks):
                for c in chunks:
                    if c == 0:
                        pe.wait_ge(s_xn, s + 1)
                    after(pe, s_tdve if c % 2 else s_tact, 2 * s + c // 2)
                    for j in range(NSUB):
                        v = a_x[b][:, j, 0:MUL] if c == 0 else a_x[b][:, j, MUL + c - 1:D:3]
                        last = nc.tensor.transpose(A_T[c % 2][:, j * P:(j + 1) * P], v, ident[:])
                    last.then_inc(s_t, 1)

            def gate_hidden(t, xT):
                if not isinstance(t, int) or t > 0:
                    pe.wait_ge(s_g0, t)
                    pe.wait_ge(s_xg, t)
                for c, v in enumerate((xT[:, 0, :], a_n1)):
                    if c == 1:
                        pe.wait_ge(s_n1, t + 1)
                    for o in range(2):
                        last = nc.tensor.matmul(A_G[o][:], wg1[:, c, o * P:(o + 1) * P], v,
                                                start=(c == 0), stop=(c == 1))
                        if c == 1:
                            last.then_inc(s_g1, 1)

            def gate(t):
                pe.wait_ge(s_silu, 2 * t + 2)
                for o in range(2):
                    for c in range(2):
                        last = nc.tensor.matmul(A_G[o][:], wg2[:, c, o * P:(o + 1) * P], a_g[:, c, :],
                                                start=(c == 0), stop=(c == 1))
                    last.then_inc(s_g2, 1)

            def node_features(t):
                pe.wait_ge(s_g0, t + 1)
                pe.wait_ge(s_xg, t + 1)
                for j in range(NSUB):
                    after(pe, s_ndev, 4 * t + j - 1)
                    for c in range(4):
                        last = nc.tensor.matmul(A_ND[j % 2][:, c * MUL:(c + 1) * MUL], a_xg[:, c, j * P:(j + 1) * P],
                                                wnd0[:] if c == 0 else wnd1[:], start=True, stop=True)
                    last.then_inc(s_nd, 1)

            def q_p1(s, xT):
                pe.wait_ge(s_tact, 2 * s + 2)
                pe.wait_ge(s_tdve, 2 * s + 2)
                for j in range(NSUB):
                    after(pe, s_pdve if j % 2 else s_pact, 2 * s + j // 2)
                    nc.tensor.matmul(A_P[j % 2][:, 0:HID], xT[:, 0, j * P:(j + 1) * P], wq[:], start=True, stop=True)
                    for c in range(3):
                        last = nc.tensor.matmul(A_P[j % 2][:, HID + c * MUL:HID + (c + 1) * MUL],
                                                xT[:, 1 + c, j * P:(j + 1) * P], wpre1[:], start=True, stop=True)
                    last.then_inc(s_p, 1)

            def step(s, k, b):
                if runs(s, 0):
                    transpose_x(s, b, (0, 1))
                if runs(s, 1):
                    gate_hidden(s - 1, a_xT[1 - b])
                if runs(s, 0):
                    transpose_x(s, b, (2, 3))
                if runs(s, 2):
                    node_features(s - 2)
                if runs(s, 1):
                    gate(s - 1)
                if runs(s, 0):
                    q_p1(s, a_xT[b])

            pipeline(pe, step, NT + 1)

        at[0] = 0
        b_gs = [take(NSUB, QP) for _ in range(2)]
        b_gd = [take(NSUB, PX) for _ in range(2)]
        b_pr = [take(3, MUL) for _ in range(2)]
        b_ipT = take(TILE)
        b_q = take(NSUB, HID)
        b_ea = take(P)
        b_eaT = take(P)
        b_hp = take(2 * P)
        b_ln = take(2 * P)
        b_hh = take(2 * P)
        b_wa = [take(D) for _ in range(2)]
        b_w = take(4, MUL)
        b_xs = [take(8, MUL) for _ in range(2)]
        b_y = take(8, MUL)
        b_msg = [take(4, MUL) for _ in range(2)]
        b_s = [take(NSUB, P) for _ in range(2)]
        b_sl = take(NSUB, P)
        b_out = [take(D) for _ in range(2)]
        b_key = [take(NSUB) for _ in range(2)]
        b_cnt = take(NSUB)
        b_idx = take(NSUB)
        b_sh = [take(NSUB, 4) for _ in range(2)]
        b_gsi = [sb(f"b_gsi{b}", [P, NSUB], U32) for b in range(2)]
        b_gdi = [sb(f"b_gdi{b}", [P, NSUB], U32) for b in range(2)]
        b_sci = [sb(f"b_sci{b}", [P, NSUB], U32) for b in range(2)]
        B_A, B_B, B_AGG, B_T, B_H = psum[0:2], psum[2:4], psum[4:6], psum[6], psum[7]

        gather = [[sem(f"b_gather{b}{j}") for j in range(NSUB)] for b in range(2)]
        added = sem("b_added")
        q_idx, q_ea, q_pr, q_ipt, q_ipe = (sem(f"b_{n}") for n in ("idx", "ea", "pr", "ipt", "ipe"))
        q_eat, q_eae, q_h, q_hp, q_act, q_hh = (sem(f"b_{n}") for n in ("eat", "eae", "h", "hp", "act", "hh"))
        q_ab, q_ae, q_w, q_y, q_agg, q_oe = (sem(f"b_{n}") for n in ("ab", "ae", "w", "y", "agg", "oe"))
        q_hi = sem("b_hi")
        q_dot, q_xs, q_msg = sem("b_dot"), sem("b_xs"), sem("b_msg")
        q_q, q_sh, q_far = sem("b_q"), sem("b_sh"), sem("b_far")
        q_tr, q_s, q_sl, q_cnt, q_sci = (sem(f"b_{n}") for n in ("tr", "s", "sl", "cnt", "sci"))

        @block.vector
        def _(dve):
            dve.wait_ge(e_in, E_TOTAL)
            wait_all(dve, row_out, 32 * (NT // 2))

            def indices(s, k, b):
                after(dve, q_sci, s - 1)
                nc.vector.tensor_copy(b_gsi[b][:], gsrc_i[:, bass.ds(s * NSUB, NSUB)])
                nc.vector.tensor_copy(b_gdi[b][:], gdst_i[:, bass.ds(s * NSUB, NSUB)])
                nc.vector.tensor_copy(b_key[b], key_i[:, bass.ds(s * NSUB, NSUB)]).then_inc(q_idx, 1)

            def factors(s, b):
                after(dve, q_xs, 4 * (s - 1))
                nc.vector.tensor_copy(b_sh[b].rearrange("p j m -> p (j m)"),
                                      ea4[:, bass.ds(s * NSUB * 4, NSUB * 4)]).then_inc(q_sh, 1)

            def products(s, k, b, j):
                dve.wait_ge(gather[b][j], 32 * k + 32)
                after(dve, q_ipt, 4 * s + j - 1)
                nc.vector.tensor_tensor(b_pr[j % 2].rearrange("p c u -> p (c u)"), b_gs[b][:, j, HID:QP],
                                        b_gd[b][:, j, 0:3 * MUL], ALU.mult).then_inc(q_pr, 1)

            def collect_q(s, b):
                after(dve, q_h, s)
                nc.vector.tensor_copy(b_q, b_gs[b][:, :, 0:HID]).then_inc(q_q, 1)

            def shared_targets(s, b):
                dve.wait_ge(q_tr, s + 1)
                after(dve, q_agg, 4 * (s - 1))
                nc.vector.tensor_tensor(b_s[b], B_T[:].rearrange("p (j e) -> p j e", j=NSUB),
                                        b_key[b][:, :, None].to_broadcast([P, NSUB, P]), ALU.is_equal).then_inc(q_s, 1)
                dve.wait_ge(q_s, s + 1)
                nc.vector.tensor_tensor(b_sl, b_s[b], lower[:, None, :].to_broadcast([P, NSUB, P]),
                                        ALU.mult).then_inc(q_sl, 1)

            def add_indices(s, b):
                dve.wait_ge(q_sl, s + 1)
                nc.vector.tensor_reduce(out=b_cnt, in_=b_sl, axis=AX.X, op=ALU.add).then_inc(q_cnt, 1)
                dve.wait_ge(q_cnt, s + 1)
                nc.vector.scalar_tensor_tensor(out=b_idx, in0=b_cnt, scalar=float(FAR), in1=b_key[b],
                                               op0=ALU.mult, op1=ALU.add).then_inc(q_far, 1)
                dve.wait_ge(q_far, s + 1)
                after(dve, added, 64 * (s - 1))
                nc.vector.tensor_tensor(b_sci[b][:], b_idx, spare[:], ALU.min).then_inc(q_sci, 1)

            def softplus_end(s, k, b):
                dve.wait_ge(q_act, 3 * s + 3)
                nc.vector.scalar_tensor_tensor(out=b_hh, in0=b_hp, scalar=0.0, in1=b_ln,
                                               op0=ALU.max, op1=ALU.add)
                after(dve, q_ab, 4 * s)
                nc.vector.scalar_tensor_tensor(out=hh_hi, in0=b_hp, scalar=0.0, in1=b_ln,
                                               op0=ALU.max, op1=ALU.add).then_inc(q_hi, 1)
                dve.wait_ge(q_hi, s + 1)
                nc.vector.tensor_tensor(hh_lo, b_hh, hh_hi.bitcast(FP32), ALU.subtract).then_inc(q_hh, 1)

            def message(t, o, j, meanwhile):
                n = 4 * t + j
                feat = b_gd[o][:, j, 3 * MUL:PX].rearrange("p (c u) -> p c u", u=MUL)
                xs = b_xs[j % 2]

                def dot(m):
                    if m == 0:
                        dve.wait_ge(q_sh, t + 1)
                        op = nc.vector.tensor_scalar(xs[:, 1, :], feat[:, 1, :], b_sh[o][:, j, 1:2], None, ALU.mult)
                    else:
                        dve.wait_ge(q_dot, 3 * n + m)
                        op = nc.vector.scalar_tensor_tensor(
                            out=xs[:, 1, :], in0=feat[:, 1 + m, :], scalar=b_sh[o][:, j, 1 + m:2 + m],
                            in1=xs[:, 1, :], op0=ALU.mult, op1=ALU.add)
                    op.then_inc(q_dot, 1)

                dot(0)
                meanwhile[0]()
                dot(1)
                dve.wait_ge(q_ae, n + 1)
                dve.wait_ge(q_ab, n + 1)
                nc.vector.tensor_tensor(b_w.rearrange("p c u -> p (c u)"), b_wa[j % 2], B_B[j % 2][:],
                                        ALU.mult).then_inc(q_w, 1)
                dot(2)
                dve.wait_ge(q_w, n + 1)
                dve.wait_ge(q_xs, n + 1)
                terms = b_y.rearrange("p (k c) u -> p k c u", k=2)
                nc.vector.tensor_tensor(terms[:, :, 1:4, :], b_w[:, 1:3, None, :].to_broadcast([P, 2, 3, MUL]),
                                        xs[:, 2:8, :].rearrange("p (k c) u -> p k c u", k=2), ALU.mult)
                dve.wait_ge(q_dot, 3 * n + 3)
                nc.vector.tensor_tensor(b_y[:, 0:8:4, :], b_w[:, 0:4:3, :], xs[:, 0:2, :], ALU.mult).then_inc(q_y, 1)
                meanwhile[1]()
                dve.wait_ge(q_y, n + 1)
                after(dve, q_agg, n - 1)
                nc.vector.tensor_tensor(b_msg[j % 2], b_y[:, 0:4, :], b_y[:, 4:8, :], ALU.add).then_inc(q_msg, 1)

            def step(s, k, b):
                t, o = s - 1, 1 - b

                def prepare(*blocks):
                    if runs(s, 0):
                        for j in blocks:
                            products(s, k, b, j)
                            if j == 3:
                                collect_q(s, b)

                def nothing():
                    pass

                if runs(s, -1):
                    indices(s + 1, k + b, o)
                if runs(s, 0):
                    factors(s, b)
                prepare(0, 1)
                if runs(s, 1):
                    message(t, o, 0, (nothing, lambda: prepare(2)))
                    message(t, o, 1, (lambda: prepare(3), nothing))
                    message(t, o, 2, (nothing, nothing))
                else:
                    prepare(2, 3)
                if runs(s, 0):
                    shared_targets(s, b)
                    softplus_end(s, k, b)
                if runs(s, 1):
                    message(t, o, 3, (nothing, nothing))
                if runs(s, 0):
                    add_indices(s, b)

            indices(0, 0, 0)
            pipeline(dve, step, ET)

        @block.gpsimd
        def _(pool):
            wait_all(pool, row_out, 32 * (NT // 2))

            def fetch(s, k, b, j):
                if j == 0:
                    pool.wait_ge(q_idx, s + 1)
                if not isinstance(s, int) or s >= 2:
                    pool.wait_ge(q_y, 4 * (s - 2) + j + 1)
                settled(pool, pool_passed)
                nc.gpsimd.indirect_dma_start(
                    out=b_gs[b][:, j, :], out_offset=None, in_=by_src[:, :],
                    in_offset=bass.IndirectOffsetOnAxis(ap=b_gsi[b][:, j:j + 1], axis=0)).then_inc(gather[b][j], 16)
                nc.gpsimd.indirect_dma_start(
                    out=b_gd[b][:, j, :], out_offset=None, in_=by_dst[:, :],
                    in_offset=bass.IndirectOffsetOnAxis(ap=b_gdi[b][:, j:j + 1], axis=0)).then_inc(gather[b][j], 16)

            def add(t, b, j):
                n = 4 * t + j
                pool.wait_ge(q_oe, n + 1)
                pool.wait_ge(q_sci, t + 1)
                after(pool, added, 16 * n)
                settled(pool, pool_passed)
                nc.gpsimd.indirect_dma_start(
                    out=acc[:, :], out_offset=bass.IndirectOffsetOnAxis(ap=b_sci[b][:, j:j + 1], axis=0),
                    in_=b_out[j % 2], in_offset=None, compute_op=ALU.add).then_inc(added, 16)

            def step(s, k, b):
                for j in range(NSUB):
                    if j == 0 and runs(s, 2):
                        add(s - 2, b, NSUB - 1)
                    if runs(s, -1):
                        fetch(s + 1, k + b, 1 - b, j)
                    if j < NSUB - 1 and runs(s, 1):
                        add(s - 1, 1 - b, j)

            for j in range(NSUB):
                fetch(0, 0, 0, j)
            pipeline(pool, step, ET + 1)

        @block.scalar
        def _(act):
            wait_all(act, row_out, 32 * (NT // 2))
            nc.scalar.preload_act_table_set("natural_log_exp_and_others")

            def edge_hidden(s):
                act.wait_ge(q_eat, s + 1)
                nc.scalar.activation(b_eaT, B_H[:, 0:P], ACT.Copy).then_inc(q_eae, 1)
                act.wait_ge(q_ipt, 4 * s + 4)
                after(act, q_h, s)
                nc.scalar.activation(b_ipT, B_T[:], ACT.Copy).then_inc(q_ipe, 1)

            def hidden(s):
                act.wait_ge(q_h, s + 1)
                after(act, q_hh, s)
                nc.scalar.activation(b_hp[:, 0:P], B_H[:, P:2 * P], ACT.Copy)
                nc.scalar.activation(b_hp[:, P:2 * P], B_H[:, 2 * P:3 * P], ACT.Identity,
                                     bias=bq_c).then_inc(q_hp, 1)
                act.wait_ge(q_hp, s + 1)
                nc.scalar.activation(b_ln, b_hp, ACT.Abs).then_inc(q_act, 1)
                act.wait_ge(q_act, 3 * s + 1)
                nc.scalar.activation(b_ln, b_ln, ACT.Exp, scale=-1.0).then_inc(q_act, 1)
                act.wait_ge(q_act, 3 * s + 2)
                nc.scalar.activation(b_ln, b_ln, ACT.Ln, bias=half_c, scale=0.5).then_inc(q_act, 1)

            def weights(t, o, j):
                n = 4 * t + j
                act.wait_ge(q_ab, n + 1)
                after(act, q_w, n - 1)
                nc.scalar.activation(b_wa[j % 2], B_A[j % 2][:], ACT.Copy).then_inc(q_ae, 1)

            def scaled(t, o, ko, j):
                n = 4 * t + j
                feat = b_gd[o][:, j, 3 * MUL:PX]
                act.wait_ge(gather[o][j], 32 * ko + 32)
                act.wait_ge(q_sh, t + 1)
                after(act, q_y, n - 1)
                for m in range(4):
                    nc.scalar.activation(b_xs[j % 2][:, m + (m > 0), :], feat[:, 0:MUL], ACT.Copy,
                                         scale=b_sh[o][:, j, m:m + 1])
                nc.scalar.activation(b_xs[j % 2][:, 5:8, :].rearrange("p c u -> p (c u)"), feat[:, MUL:D], ACT.Copy,
                                     scale=b_sh[o][:, j, 0:1]).then_inc(q_xs, 1)

            def sums(t, o, j):
                n = 4 * t + j
                act.wait_ge(q_agg, n + 1)
                after(act, added, 16 * (n - 1))
                nc.scalar.activation(b_out[j % 2], B_AGG[j % 2][:], ACT.Copy).then_inc(q_oe, 1)

            def step(s, k, b):
                t, o = s - 1, 1 - b
                if runs(s, 0):
                    after(act, q_eat, s)
                    if isinstance(s, int) and s == 0:
                        act.wait_ge(e_in, E_TOTAL)
                    nc.scalar.activation(b_ea, ea32[:, bass.ds(s * P, P)], ACT.Copy).then_inc(q_ea, 1)
                if runs(s, 1):
                    ko = before(k, b)
                    weights(t, o, 0)
                if runs(s, 2):
                    sums(t - 1, b, NSUB - 1)
                if runs(s, 1):
                    weights(t, o, 1)
                    scaled(t, o, ko, 1)
                    weights(t, o, 2)
                    scaled(t, o, ko, 2)
                    sums(t, o, 0)
                if runs(s, 0):
                    edge_hidden(s)
                if runs(s, 1):
                    weights(t, o, 3)
                    sums(t, o, 1)
                if runs(s, 0):
                    hidden(s)
                if runs(s, 1):
                    scaled(t, o, ko, 3)
                    sums(t, o, 2)
                if runs(s, 0):
                    scaled(s, b, k, 0)

            pipeline(act, step, ET + 1)

        @block.tensor
        def _(pe):
            wait_all(pe, row_out, 32 * (NT // 2))

            def sum_products(s, j):
                if j == 0:
                    after(pe, q_s, s)
                pe.wait_ge(q_pr, 4 * s + j + 1)
                for c in range(3):
                    last = nc.tensor.matmul(B_T[:, j * P:(j + 1) * P], b_pr[j % 2][:, c, :], ident[:],
                                            start=(c == 0), stop=(c == 2))
                last.then_inc(q_ipt, 1)

            def transpose_attr(s):
                pe.wait_ge(q_ea, s + 1)
                after(pe, q_hp, s)
                nc.tensor.transpose(B_H[:, 0:P], b_ea, ident[:]).then_inc(q_eat, 1)

            def hidden(s, b):
                pe.wait_ge(q_eae, s + 1)
                nc.tensor.matmul(B_H[:, P:2 * P], wf1[:], b_eaT, start=True, stop=True)
                pe.wait_ge(q_ipe, s + 1)
                for j in range(NSUB):
                    nc.tensor.matmul(B_H[:, 2 * P:3 * P], wc[:, j, :], b_ipT[:, j * P:(j + 1) * P],
                                     start=(j == 0), stop=False)
                pe.wait_ge(q_q, s + 1)
                nc.tensor.matmul(B_H[:, 2 * P:3 * P], b_q.rearrange("p j h -> p (j h)"), ident[:],
                                 start=False, stop=True).then_inc(q_h, 1)

            def transpose_keys(s, b):
                for j in range(NSUB):
                    last = nc.tensor.transpose(B_T[:, j * P:(j + 1) * P], b_key[b][:, j:j + 1].to_broadcast([P, P]),
                                               ident[:])
                last.then_inc(q_tr, 1)

            def weights(t, j):
                n = 4 * t + j
                if j == 0:
                    pe.wait_ge(q_hh, t + 1)
                after(pe, q_ae, n - 1)
                after(pe, q_w, n - 1)
                part = slice(HID * j, HID * (j + 1))
                for bank, columns, w_hi, w_lo in ((B_A, slice(0, P), wf2_hi, wf2_lo),
                                                  (B_B, slice(P, 2 * P), ws2_hi, ws2_lo)):
                    for i, (w, hh) in enumerate(parts(w_hi, w_lo, hh_hi, hh_lo)):
                        last = nc.tensor.matmul(bank[j % 2][:], hh[part, columns], w[part, :],
                                                start=(i == 0), stop=(i == 2))
                last.then_inc(q_ab, 1)

            def aggregate(t, o, j):
                n = 4 * t + j
                pe.wait_ge(q_s, t + 1)
                pe.wait_ge(q_msg, n + 1)
                after(pe, q_oe, n - 1)
                nc.tensor.matmul(B_AGG[j % 2][:], b_s[o][:, j, :], b_msg[j % 2].rearrange("p c u -> p (c u)"),
                                 start=True, stop=True).then_inc(q_agg, 1)

            def step(s, k, b):
                t, o = s - 1, 1 - b
                if runs(s, 1):
                    weights(t, 0)
                    weights(t, 1)
                if runs(s, 2):
                    aggregate(t - 1, b, NSUB - 1)
                if runs(s, 0):
                    sum_products(s, 0)
                    sum_products(s, 1)
                if runs(s, 1):
                    weights(t, 2)
                    aggregate(t, o, 0)
                if runs(s, 0):
                    sum_products(s, 2)
                    sum_products(s, 3)
                    transpose_attr(s)
                if runs(s, 1):
                    weights(t, 3)
                    aggregate(t, o, 1)
                if runs(s, 0):
                    hidden(s, b)
                    transpose_keys(s, b)
                if runs(s, 1):
                    aggregate(t, o, 2)

            pipeline(pe, step, ET + 1)

        at[0] = 0
        c_h = [take(NSUB, D) for _ in range(2)]
        c_x = [take(NSUB, D) for _ in range(2)]
        c_hT = take(4, TILE)
        c_x2 = [take(NSUB, D) for _ in range(2)]
        c_z = [take(NSUB, D) for _ in range(2)]
        c_g = take(4, TILE)
        c_sc = [take(2, NSUB) for _ in range(2)]
        c_bn, c_bz = take(NSUB, 6), take(NSUB, 6)
        c_mv = [take(NSUB, 2) for _ in range(2)]
        c_st = [take(4, NSUB) for _ in range(2)]
        c_var = take(2, NSUB)
        c_mz = [take(NSUB, 2) for _ in range(2)]
        c_rz = [take(2, NSUB) for _ in range(2)]
        c_lg, c_mx, c_o1, c_o2 = (take(NSUB, NX) for _ in range(4))
        c_if = take(NSUB, 2)
        c_d, c_th = take(NSUB), take(NSUB)
        c_w12 = take(2, NSUB)
        c_cf = take(NSUB, 3 * NX)
        c_mi = sb("c_mi", [P, NSUB, NX], U32)
        c_chi = sb("c_chi", [P, NSUB, NX], FP32R)
        c_lT = sb("c_lT", [2 * NX, TILE])
        c_cT = sb("c_cT", [3 * NX, TILE], FP32R)
        C_T, C_O, C_HB, C_L = psum[0:2], psum[2:4], psum[4:6], psum[7]
        C_EX = (psum[6], C_T[0], C_T[1], psum[6])

        c_in = [sem(f"c_in{b}") for b in range(2)]
        c_out = [sem(f"c_out{b}") for b in range(2)]
        (t1, t1act, t1dve, u_sc, u_xs, u_xb, u_o, u_x2, u_bn, u_mv, u_var, u_pow, u_nm, u_xh, u_t2, t2hi, t2lo) = (
            sem(f"c_{n}") for n in ("t1", "t1act", "t1dve", "sc", "xs", "xb", "o", "x2", "bn", "mv", "var", "pow",
                                    "nm", "xh", "t2", "t2hi", "t2lo"))
        (v_lt, v_lte, v_l, v_lg, v_d, v_th, v_chain, v_cf, v_ct, v_cte, v_h, v_ge, v_ex, v_mul, v_hi, v_lo, v_w2, v_xn, v_z,
         v_bz, v_mz, v_vz, v_pz, v_nz, v_zh, v_r, v_zg, v_fin) = (
            sem(f"c_{n}") for n in ("lt", "lte", "l", "lg", "d", "th", "chain", "cf", "ct", "cte", "h", "ge", "ex", "mul", "hi",
                                    "lo", "w2", "xn", "z", "bz", "mz", "vz", "pz", "nz", "zh", "r", "zg", "fin"))

        @block.sync
        def _(sp):
            sp.wait_ge(added, 16 * EC)

            def load(s, k, b):
                after(sp, u_t2, 4 * (s - 1))
                after(sp, u_x2, 4 * (s - 1))
                sp.dma_start(c_h[b], rows(acc, s)).then_inc(c_in[b], 16)
                sp.dma_start(c_x[b], rows(x, s)).then_inc(c_in[b], 16)

            def step(s, k, b):
                if runs(s, -1):
                    load(s + 1, k + b, 1 - b)
                if runs(s, 2):
                    t = s - 2
                    sp.wait_ge(v_fin, 4 * (s - 1))
                    if isinstance(t, int) and t == NT - 1:
                        sp.wait_ge(c_out[1 - b], 16 * (NT // 2))
                    sp.dma_start(rows(out, t), c_z[b]).then_inc(c_out[b], 16)

            load(0, 0, 0)
            pipeline(sp, step, NT + 1)
            for b in range(2):
                sp.wait_ge(c_out[b], 16 * (NT // 2))

        @block.vector
        def _(dve):
            dve.wait_ge(added, 16 * EC)

            def transposed(s, c):
                dve.wait_ge(t1, 4 * s + c + 1)
                nc.vector.tensor_copy(c_hT[:, c, :], C_T[1][:]).then_inc(t1dve, 1)

            def low_part(s, c):
                dve.wait_ge(t2hi, 4 * s + c + 1)
                nc.vector.tensor_tensor(xhT_lo[:, c, :], C_T[c % 2][:], xhT_hi[:, c, :].bitcast(FP32),
                                        ALU.subtract).then_inc(t2lo, 1)

            def scale(s, b):
                after(dve, u_xs, s - 1)
                at_s = stats[:, bass.ds(s, 1), :].rearrange("p a n -> p (a n)")
                nc.vector.tensor_scalar(c_sc[b][:, 0, :], at_s[:, 0:NSUB], 1.0, None, ALU.add)
                nc.vector.tensor_copy(c_sc[b][:, 1, :], at_s[:, NSUB:2 * NSUB]).then_inc(u_sc, 1)

            def residual(s, b, j):
                dve.wait_ge(u_o, 4 * s + j + 1)
                x2v = c_x2[b][:, j, MUL:D].rearrange("p (u c) -> p c u", c=3)
                xv = c_x[b][:, j, MUL:D].rearrange("p (u c) -> p c u", c=3)
                ov = C_O[j % 2][:, MUL:D].rearrange("p (c u) -> p c u", c=3)
                nc.vector.tensor_tensor(c_x2[b][:, j, 0:MUL], C_O[j % 2][:, 0:MUL], c_x[b][:, j, 0:MUL], ALU.add)
                nc.vector.tensor_tensor(x2v, ov, xv, ALU.add).then_inc(u_x2, 1)

            def x2_statistics(s, b, j):
                dve.wait_ge(u_x2, 4 * s + j + 1)
                nc.vector.bn_stats(c_bn[:, j, :], c_x2[b][:, j, :]).then_inc(u_bn, 1)

            def x2_variance(s, b):
                dve.wait_ge(u_bn, 4 * s + 4)
                settled(dve, dve_passed)
                for j in range(NSUB):
                    last = nc.vector.bn_aggr(c_mv[b][:, j, :], c_bn[:, j, :])
                last.then_inc(u_mv, 1)
                dve.wait_ge(u_mv, s + 1)
                nc.vector.tensor_scalar(c_var[:, 1, :], c_mv[b][:, :, 1], 1.0 + EPS, EPS * EPS, ALU.mult, ALU.add)
                nc.vector.tensor_scalar(c_var[:, 0, :], c_mv[b][:, :, 1], EPS, None, ALU.add).then_inc(u_var, 1)

            def shift(s, b, i):
                dve.wait_ge(u_pow, 2 * s + 2 - i)
                nc.vector.scalar_tensor_tensor(out=c_st[b][:, 2 + i, :], in0=c_st[b][:, i, :], scalar=-1.0,
                                               in1=c_mv[b][:, :, 0], op0=ALU.mult, op1=ALU.mult).then_inc(u_nm, 1)

            def top2(t):
                dve.wait_ge(v_l, t + 1)
                nc.vector.tensor_copy(c_lg, C_L[:, 0:NSUB * NX].rearrange("p (j e) -> p j e", j=NSUB)).then_inc(v_lg, 1)
                dve.wait_ge(v_lg, t + 1)
                settled(dve, dve_passed)
                for j in range(NSUB):
                    last = nc.vector.max(out=c_mx[:, j, :], in_=c_lg[:, j, :])
                last.then_inc(v_chain, 1)
                dve.wait_ge(v_chain, 6 * t + 1)
                nc.vector.tensor_tensor(c_d, c_mx[:, :, 0], c_mx[:, :, 1], ALU.subtract).then_inc(v_d, 1)
                for j in range(NSUB):
                    last = nc.vector.max_index(out=c_mi[:, j, :], in_max=c_mx[:, j, :], in_values=c_lg[:, j, :])
                last.then_inc(v_chain, 1)
                dve.wait_ge(v_chain, 6 * t + 2)
                nc.vector.tensor_copy(c_if, c_mi[:, :, 0:2]).then_inc(v_chain, 1)
                dve.wait_ge(v_chain, 6 * t + 3)
                for i, o in enumerate((c_o1, c_o2)):
                    nc.vector.tensor_tensor(o, iota8[:, None, :].to_broadcast([P, NSUB, NX]),
                                            c_if[:, :, i:i + 1].to_broadcast([P, NSUB, NX]), ALU.is_equal)
                dve.wait_ge(v_th, t + 1)
                nc.vector.tensor_scalar(c_w12[:, 0, :], c_th, 0.5, 0.5, ALU.mult, ALU.add)
                nc.vector.tensor_scalar(c_w12[:, 1, :], c_th, -0.5, 0.5, ALU.mult, ALU.add).then_inc(v_chain, 1)
                dve.wait_ge(v_chain, 6 * t + 4)
                for i, o in enumerate((c_o1, c_o2)):
                    last = nc.vector.tensor_tensor(o, o, c_w12[:, i, :, None].to_broadcast([P, NSUB, NX]), ALU.mult)
                last.then_inc(v_chain, 1)
                dve.wait_ge(v_chain, 6 * t + 5)
                nc.vector.tensor_tensor(c_o1, c_o1, c_o2, ALU.add).then_inc(v_chain, 1)
                dve.wait_ge(v_chain, 6 * t + 6)
                nc.vector.tensor_copy(c_chi[:], c_o1).then_inc(v_cf, 1)
                dve.wait_ge(v_cf, 2 * t + 1)
                for i in range(2):
                    nc.vector.tensor_copy(c_cf[:, :, i * NX:(i + 1) * NX], c_chi[:].bitcast(FP32))
                nc.vector.tensor_tensor(c_cf[:, :, 2 * NX:3 * NX], c_o1, c_chi[:].bitcast(FP32),
                                        ALU.subtract).then_inc(v_cf, 1)

            def weigh(t, q):
                dve.wait_ge(v_ge, 4 * t + q + 1)
                dve.wait_ge(v_ex, 4 * t + q + 1)
                nc.vector.tensor_tensor(c_g[:, q, :], C_EX[q][:], c_g[:, q, :], ALU.mult).then_inc(v_mul, 1)

            def second_residual(t, o, j):
                dve.wait_ge(v_w2, 4 * t + j + 1)
                dve.wait_ge(v_xn, 4 * t + j + 1)
                nc.vector.tensor_tensor(c_z[o][:, j, :], C_O[j % 2][:], c_z[o][:, j, :], ALU.add).then_inc(v_z, 1)

            def z_statistics(t, o, j):
                dve.wait_ge(v_z, 4 * t + j + 1)
                nc.vector.bn_stats(c_bz[:, j, :], c_z[o][:, j, :]).then_inc(v_bz, 1)

            def z_variance(t, o):
                dve.wait_ge(v_bz, 4 * t + 4)
                settled(dve, dve_passed)
                for j in range(NSUB):
                    last = nc.vector.bn_aggr(c_mz[o][:, j, :], c_bz[:, j, :])
                last.then_inc(v_mz, 1)
                dve.wait_ge(v_mz, t + 1)
                nc.vector.tensor_scalar(c_rz[o][:, 0, :], c_mz[o][:, :, 1], EPS, None, ALU.add).then_inc(v_vz, 1)

            def shift_z(t, b):
                dve.wait_ge(v_pz, t + 1)
                nc.vector.scalar_tensor_tensor(out=c_rz[b][:, 1, :], in0=c_mz[b][:, :, 0], scalar=-1.0,
                                               in1=c_rz[b][:, 0, :], op0=ALU.mult, op1=ALU.mult).then_inc(v_nz, 1)

            def finish(t, b, j):
                dve.wait_ge(v_zg, 4 * t + j + 1)
                dve.wait_ge(v_r, 4 * t + j + 1)
                nc.vector.tensor_tensor(c_z[b][:, j, :], c_z[b][:, j, :], c_x2[b][:, j, :], ALU.add).then_inc(v_fin, 1)

            def step(s, k, b):
                t, u, o = s - 1, s - 2, 1 - b
                if runs(s, 1):
                    low_part(t, 2)
                    low_part(t, 3)
                if runs(s, 2):
                    shift_z(u, b)
                if runs(s, 1):
                    top2(t)
                if runs(s, 0):
                    transposed(s, 1)
                if runs(s, 2):
                    for j in range(NSUB):
                        finish(u, b, j)
                if runs(s, 0):
                    transposed(s, 3)
                if runs(s, -1):
                    scale(s + 1, o)
                if runs(s, 1):
                    for q in range(4):
                        weigh(t, q)
                if runs(s, 0):
                    dve.wait_ge(u_xb, s + 1)
                    residual(s, b, 0)
                    for j in range(1, NSUB):
                        residual(s, b, j)
                        x2_statistics(s, b, j - 1)
                    x2_statistics(s, b, NSUB - 1)
                    x2_variance(s, b)
                if runs(s, 1):
                    second_residual(t, o, 0)
                if runs(s, 0):
                    shift(s, b, 1)
                if runs(s, 1):
                    second_residual(t, o, 1)
                    z_statistics(t, o, 0)
                if runs(s, 0):
                    shift(s, b, 0)
                if runs(s, 1):
                    second_residual(t, o, 2)
                    z_statistics(t, o, 1)
                if runs(s, 0):
                    low_part(s, 0)
                    low_part(s, 1)
                if runs(s, 1):
                    z_statistics(t, o, 2)
                    second_residual(t, o, 3)
                    z_statistics(t, o, 3)
                    z_variance(t, o)

            scale(0, 0)
            pipeline(dve, step, NT + 1)

        @block.gpsimd
        def _(pool):
            pool.wait_ge(added, 16 * EC)

            def add_bias(s, b):
                pool.wait_ge(u_xs, s + 1)
                nc.gpsimd.tensor_tensor(c_x[b][:, :, 0:MUL], c_x[b][:, :, 0:MUL],
                                        bo0_r[:, None, :].to_broadcast([P, NSUB, MUL]), ALU.add).then_inc(u_xb, 1)

            def gain(t, b, j):
                pool.wait_ge(v_zh, 4 * t + j + 1)
                nc.gpsimd.tensor_tensor(c_z[b][:, j, :], c_z[b][:, j, :], outg_r[:], ALU.mult).then_inc(v_zg, 1)

            def add_out_b(t, b, j):
                if j == 0:
                    pool.wait_ge(u_xh, t + 1)
                pool.wait_ge(v_xn, 4 * t + j + 1)
                nc.gpsimd.tensor_tensor(c_x2[b][:, j, :], c_x2[b][:, j, :], outb_r[:], ALU.add).then_inc(v_r, 1)

            def step(s, k, b):
                t, u, o = s - 1, s - 2, 1 - b
                if runs(s, 2):
                    pool.wait_ge(v_vz, u + 1)
                    nc.gpsimd.tensor_tensor(c_rz[b][:, 0, :], c_rz[b][:, 0, :], mhalf[:], ALU.pow).then_inc(v_pz, 1)
                    for j in range(NSUB):
                        gain(u, b, j)
                if runs(s, 1):
                    add_out_b(t, o, 0)
                    add_out_b(t, o, 1)
                    for q in range(4):
                        pool.wait_ge(v_hi, 4 * t + q + 1)
                        after(pool, v_w2, 4 * t)
                        nc.gpsimd.tensor_tensor(hg_lo[:, q, :], c_g[:, q, :], hg_hi[:, q, :].bitcast(FP32),
                                                ALU.subtract).then_inc(v_lo, 1)
                if runs(s, -1):
                    add_bias(s + 1, o)
                if runs(s, 0):
                    pool.wait_ge(u_var, s + 1)
                    for i in (1, 0):
                        nc.gpsimd.tensor_tensor(c_st[b][:, i, :], c_var[:, i, :], mhalf[:], ALU.pow).then_inc(u_pow, 1)
                if runs(s, 1):
                    add_out_b(t, o, 2)
                    add_out_b(t, o, 3)

            add_bias(0, 0)
            pipeline(pool, step, NT + 1)

        @block.scalar
        def _(act):
            act.wait_ge(added, 16 * EC)
            nc.scalar.preload_act_table_set("gelu_apprx_tanh_and_others")

            def transposed(s, c):
                act.wait_ge(t1, 4 * s + c + 1)
                nc.scalar.activation(c_hT[:, c, :], C_T[0][:], ACT.Copy).then_inc(t1act, 1)

            def high_part(s, c):
                act.wait_ge(u_t2, 4 * s + c + 1)
                nc.scalar.activation(xhT_hi[:, c, :], C_T[c % 2][:], ACT.Copy).then_inc(t2hi, 1)

            def scale_x(s, k, b):
                act.wait_ge(c_in[b], 32 * k + 32)
                act.wait_ge(u_sc, s + 1)
                for j in range(NSUB):
                    last = nc.scalar.activation(c_x[b][:, j, :], c_x[b][:, j, :], ACT.Identity,
                                                bias=c_sc[b][:, 1, j:j + 1], scale=c_sc[b][:, 0, j:j + 1])
                last.then_inc(u_xs, 1)

            def normalise(s, b):
                act.wait_ge(u_nm, 2 * s + 1)
                for j in range(NSUB):
                    last = nc.scalar.activation(c_h[b][:, j, :], c_x2[b][:, j, :], ACT.Identity,
                                                bias=c_st[b][:, 3, j:j + 1], scale=c_st[b][:, 1, j:j + 1])
                last.then_inc(u_xh, 1)

            def first_norm(t, o, ko, j):
                if j == 0:
                    act.wait_ge(u_nm, 2 * t + 2)
                    after(act, c_out[o], 16 * ko)
                nc.scalar.activation(c_z[o][:, j, :], c_x2[o][:, j, :], ACT.Identity,
                                     bias=c_st[o][:, 2, j:j + 1], scale=c_st[o][:, 0, j:j + 1]).then_inc(v_xn, 1)

            def normalise_z(u, b, j):
                act.wait_ge(v_nz, u + 1)
                nc.scalar.activation(c_z[b][:, j, :], c_z[b][:, j, :], ACT.Identity,
                                     bias=c_rz[b][:, 1, j:j + 1], scale=c_rz[b][:, 0, j:j + 1]).then_inc(v_zh, 1)

            def gelu(t, q):
                act.wait_ge(v_h, 4 * t + q + 1)
                after(act, v_lo, 4 * (t - 1) + q + 1)
                nc.scalar.activation(c_g[:, q, :], C_HB[q % 2][:], ACT.Gelu_apprx_tanh,
                                     bias=b1p_c[:, q:q + 1]).then_inc(v_ge, 1)

            def high_hidden(t, q):
                act.wait_ge(v_mul, 4 * t + q + 1)
                if q == 0:
                    after(act, v_w2, 4 * t)
                nc.scalar.activation(hg_hi[:, q, :], c_g[:, q, :], ACT.Copy).then_inc(v_hi, 1)

            def step(s, k, b):
                t, u, o = s - 1, s - 2, 1 - b
                ko = before(k, b)
                if runs(s, 1):
                    high_part(t, 2)
                    high_part(t, 3)
                if runs(s, 2):
                    normalise_z(u, b, 0)
                    normalise_z(u, b, 1)
                if runs(s, 1):
                    gelu(t, 0)
                if runs(s, 2):
                    normalise_z(u, b, 2)
                    normalise_z(u, b, 3)
                if runs(s, 1):
                    act.wait_ge(v_lt, t + 1)
                    nc.scalar.activation(c_lT[:], C_L[0:2 * NX, :], ACT.Identity, bias=bgate_c[:, 0:1]).then_inc(v_lte, 1)
                    first_norm(t, o, ko, 0)
                    gelu(t, 1)
                    act.wait_ge(v_d, t + 1)
                    nc.scalar.activation(c_th, c_d, ACT.Tanh, scale=0.5).then_inc(v_th, 1)
                if runs(s, 0):
                    transposed(s, 0)
                if runs(s, 1):
                    first_norm(t, o, ko, 1)
                    gelu(t, 2)
                    act.wait_ge(v_ct, t + 1)
                    nc.scalar.activation(c_cT[:], C_L[0:3 * NX, :], ACT.Copy).then_inc(v_cte, 1)
                if runs(s, 0):
                    transposed(s, 2)
                if runs(s, 1):
                    high_hidden(t, 0)
                    gelu(t, 3)
                    for q in range(1, 4):
                        high_hidden(t, q)
                    first_norm(t, o, ko, 2)
                    first_norm(t, o, ko, 3)
                if runs(s, -1):
                    scale_x(s + 1, k + b, o)
                if runs(s, 0):
                    normalise(s, b)
                    high_part(s, 0)
                    high_part(s, 1)

            scale_x(0, 0, 0)
            pipeline(act, step, NT + 1)

        @block.tensor
        def _(pe):
            pe.wait_ge(added, 16 * EC)

            def transpose_h(s, k, b, c):
                if c == 0:
                    pe.wait_ge(c_in[b], 32 * k + 32)
                    after(pe, t2lo, 4 * s)
                if c > 1:
                    pe.wait_ge(t1dve if c % 2 else t1act, 2 * s + 1)
                for j in range(NSUB):
                    last = nc.tensor.transpose(C_T[c % 2][:, j * P:(j + 1) * P], c_h[b][:, j, c * P:(c + 1) * P],
                                               ident[:])
                last.then_inc(t1, 1)

            def project(s, j):
                if j == 0:
                    pe.wait_ge(t1act, 2 * s + 2)
                    pe.wait_ge(t1dve, 2 * s + 2)
                    after(pe, v_z, 4 * (s - 1))
                if j > 1:
                    pe.wait_ge(u_x2, 4 * s + j - 1)
                for c in range(4):
                    last = nc.tensor.matmul(C_O[j % 2][:, c * MUL:(c + 1) * MUL], c_hT[:, c, j * P:(j + 1) * P],
                                            wo0[:] if c == 0 else wo1[:], start=True, stop=True)
                last.then_inc(u_o, 1)

            def transpose_x(s, b, c):
                if c == 0:
                    pe.wait_ge(u_xh, s + 1)
                    pe.wait_ge(t1act, 2 * s + 2)
                    after(pe, v_mul, 4 * s)
                if c > 1:
                    pe.wait_ge(t2lo, 4 * s + c - 1)
                for j in range(NSUB):
                    last = nc.tensor.transpose(C_T[c % 2][:, j * P:(j + 1) * P], c_h[b][:, j, c * P:(c + 1) * P],
                                               ident[:])
                last.then_inc(u_t2, 1)

            def logits(t):
                after(pe, v_cte, t)
                for c in range(4):
                    for i, xh in enumerate((xhT_hi, xhT_lo)):
                        last = nc.tensor.matmul(C_L[:], wg_parts[:, c, :], xh[:, c, :],
                                                start=(c == 0 and i == 0), stop=(c == 3 and i == 1))
                last.then_inc(v_lt, 1)

            def fold_logits(t):
                pe.wait_ge(v_lte, t + 1)
                for j in range(NSUB):
                    last = nc.tensor.matmul(C_L[:, j * NX:(j + 1) * NX], c_lT[:, j * P:(j + 1) * P], fold[:],
                                            start=True, stop=True)
                last.then_inc(v_l, 1)

            def hidden(t, q, chunks=range(4)):
                for c in chunks:
                    if c == 0:
                        after(pe, v_ge, 4 * t + q - 1)
                    if q == 0:
                        pe.wait_ge(t2lo, 4 * t + c + 1)
                    for i, (w, xh) in enumerate(parts(w1_hi, w1_lo, xhT_hi, xhT_lo)):
                        last = nc.tensor.matmul(C_HB[q % 2][:], w[:, c, q * P:(q + 1) * P], xh[:, c, :],
                                                start=(c == 0 and i == 0), stop=(c == 3 and i == 2))
                if chunks[-1] == 3:
                    last.then_inc(v_h, 1)

            def spread(t, q):
                if q == 0:
                    pe.wait_ge(v_cte, t + 1)
                if q == 3:
                    pe.wait_ge(v_mul, 4 * t + 1)
                nc.tensor.matmul(C_EX[q][:], sel[:, q * P:(q + 1) * P], c_cT[:], start=True, stop=True).then_inc(v_ex, 1)

            def expert_out(s, t, j):
                if j > 1:
                    pe.wait_ge(v_z, 4 * t + j - 1)
                elif runs(s, 0):
                    pe.wait_ge(u_x2, 4 * s + j + 3)
                else:
                    pe.wait_ge(v_z, 4 * (t - 1) + j + 3)
                tokens = slice(j * P, (j + 1) * P)
                nc.tensor.matmul(C_O[j % 2][:], c_cT[:, tokens], b2s[:], start=True, stop=False)
                for q in range(4):
                    if j == 0:
                        pe.wait_ge(v_lo, 4 * t + q + 1)
                    for i, (w, hg) in enumerate(parts(w2_hi, w2_lo, hg_hi, hg_lo)):
                        last = nc.tensor.matmul(C_O[j % 2][:], hg[:, q, tokens], w[:, q, :],
                                                start=False, stop=(q == 3 and i == 2))
                last.then_inc(v_w2, 1)

            def step(s, k, b):
                t = s - 1
                if runs(s, 1):
                    hidden(t, 0, (0,))
                    transpose_x(t, 1 - b, 2)
                    hidden(t, 0, (1,))
                    transpose_x(t, 1 - b, 3)
                    hidden(t, 1, (0, 1))
                    hidden(t, 0, (2, 3))
                    logits(t)
                    hidden(t, 1, (2, 3))
                    fold_logits(t)
                if runs(s, 0):
                    transpose_h(s, k, b, 0)
                    transpose_h(s, k, b, 1)
                if runs(s, 1):
                    hidden(t, 2)
                    pe.wait_ge(v_cf, 2 * t + 2)
                    for j in range(NSUB):
                        last = nc.tensor.transpose(C_L[0:3 * NX, j * P:(j + 1) * P], c_cf[:, j, :], ident[:])
                    last.then_inc(v_ct, 1)
                if runs(s, 0):
                    transpose_h(s, k, b, 2)
                    transpose_h(s, k, b, 3)
                if runs(s, 1):
                    spread(t, 0)
                    hidden(t, 3)
                    if runs(s, 0):
                        pe.wait_ge(t1act, 2 * s + 2)
                        pe.wait_ge(t1dve, 2 * s + 2)
                    spread(t, 1)
                    spread(t, 2)
                if runs(s, 0):
                    project(s, 0)
                if runs(s, 1):
                    spread(t, 3)
                if runs(s, 0):
                    for j in range(1, NSUB):
                        project(s, j)
                if runs(s, 1):
                    for j in range(NSUB - 1):
                        expert_out(s, t, j)
                if runs(s, 0):
                    transpose_x(s, b, 0)
                    transpose_x(s, b, 1)
                if runs(s, 1):
                    expert_out(s, t, NSUB - 1)

            pipeline(pe, step, NT)


_INS = ['x', 'src', 'dst', 'edge_attr_32', 'edge_attr_4',
        'L0_gnn_W_pre0', 'L0_gnn_b_pre0', 'L0_gnn_W_pre1', 'L0_gnn_W_nd0', 'L0_gnn_b_nd0', 'L0_gnn_W_nd1',
        'L0_gnn_W_g1', 'L0_gnn_b_g1', 'L0_gnn_W_g2', 'L0_gnn_b_g2', 'L0_gnn_W_f1', 'L0_gnn_W_f2',
        'L0_gnn_W_s1', 'L0_gnn_W_s2', 'L0_gnn_W_o0', 'L0_gnn_b_o0', 'L0_gnn_W_o1',
        'L0_ffn_Wg', 'L0_ffn_W1', 'L0_ffn_b1', 'L0_ffn_W2', 'L0_ffn_b2',
        'L0_ffn_ln_g', 'L0_ffn_ln_b', 'L0_ffn_out_g', 'L0_ffn_out_b']


def kernel(**inputs):
    import numpy as _np
    import concourse.bacc as _bacc
    from concourse import mybir as _mybir
    from concourse.bass_utils import run_bass_kernel_spmd as _run

    nc = _bacc.Bacc("TRN2", target_bir_lowering=False, num_devices=1)
    arrays, args = {}, []
    for name in _INS:
        a = _np.ascontiguousarray(inputs[name])
        arrays[f"in_{name}"] = a
        args.append(nc.dram_tensor(f"in_{name}", a.shape, _mybir.dt.from_np(a.dtype), kind="ExternalInput").ap())
    args.append(nc.dram_tensor("out_x", (N, D), FP32, kind="ExternalOutput").ap())
    gnn_ffn_kernel(nc, *args)
    r = _run(nc, [arrays], core_ids=[0])
    return r.results[0]["out_x"]
```

```python
from contextlib import ExitStack
import math

import concourse.bass as bass
from concourse import mybir

FP32 = mybir.dt.float32
FP32R = mybir.dt.float32r
I32 = mybir.dt.int32
U32 = mybir.dt.uint32
ALU = mybir.AluOpType
ACT = mybir.ActivationFunctionType
AX = mybir.AxisListType

P = 128
N, D = 10000, 512
MUL = 128
NSUB = 4
TILE = NSUB * P
NT = -(-N // TILE)
E = 10000
EP = 125
EC = E // EP
ET = EC // NSUB
HID = 32
NX, EH = 8, 64
QP = HID + 3 * MUL
PX = 3 * MUL + D
EPS = 1e-5
FAR = 1 << 20
PAD_KEY = 1 << 14
assert EP * EC == E and NT == ET and NT % 2 == 0 and PAD_KEY > N


def after(engine, semaphore, value):
    if not isinstance(value, int) or value > 0:
        engine.wait_ge(semaphore, value)


def pipeline(engine, step, last, tail=2):
    for s in range(4):
        step(s, s // 2, s % 2)
    with engine.Fori(2, (NT - tail) // 2) as k:
        for b in range(2):
            step(2 * k + b, k, b)
    for s in range(NT - tail, last + 1):
        step(s, s // 2, s % 2)


def runs(s, lag):
    return not isinstance(s, int) or 0 <= s - lag < NT


def settled(engine, passed):
    engine.sem_inc(passed, 1)


def wait_all(engine, semaphores, value):
    for semaphore in semaphores:
        engine.wait_ge(semaphore, value)


def base(s):
    return min(TILE * s, N - TILE) if isinstance(s, int) else TILE * s


def before(k, b):
    return k if b else k - 1


def gnn_ffn_kernel(nc, x, src, dst, edge_attr_32, edge_attr_4,
                   W_pre0, b_pre0, W_pre1, W_nd0, b_nd0, W_nd1, W_g1, b_g1, W_g2, b_g2,
                   W_f1, W_f2, W_s1, W_s2, W_o0, b_o0, W_o1,
                   Wg, W1, b1, W2, b2, ln_g, ln_b, out_g, out_b, out):
    by_src = nc.dram_tensor("by_src", [N, QP], FP32, kind="Internal").ap()
    by_dst = nc.dram_tensor("by_dst", [N, PX], FP32, kind="Internal").ap()
    acc = nc.dram_tensor("acc", [N + P, D], FP32, kind="Internal").ap()

    def rows(dram, s):
        return dram[bass.ds(base(s), TILE), :].rearrange("(p j) d -> p j d", j=NSUB)

    ctx = ExitStack()
    with ctx:
        def sb(name, shape, dtype=FP32):
            return ctx.enter_context(nc.sbuf_tensor(name, shape, dtype))

        def sem(name):
            return ctx.enter_context(nc.semaphore(name))

        ident = sb("ident", [P, P])
        lower = sb("lower", [P, P])
        sel = sb("sel", [3 * NX, NX * EH], FP32R)
        b2s = sb("b2s", [3 * NX, D], FP32R)
        middle = sb("middle", [3 * NX, 1])
        iota_i = sb("iota_i", [P, NX], I32)
        iota8 = sb("iota8", [P, NX])
        mhalf = sb("mhalf", [P, NSUB])
        rows_of = sb("rows_of", [P, NSUB])
        spare_i = sb("spare_i", [P, NSUB], I32)
        spare = sb("spare", [P, NSUB])
        zeros = sb("zeros", [P, D])
        eps4 = sb("eps4", [P, NSUB])
        wpre0 = sb("wpre0", [P, MUL])
        wpre0T = sb("wpre0T", [P, MUL])
        wpre1 = sb("wpre1", [P, MUL])
        wnd0 = sb("wnd0", [P, MUL])
        wnd1 = sb("wnd1", [P, MUL])
        wo0 = sb("wo0", [P, MUL])
        wo1 = sb("wo1", [P, MUL])
        wg1 = sb("wg1", [P, 2, 2 * MUL])
        wg2 = sb("wg2", [P, 2, 2 * MUL])
        ws1 = sb("ws1", [P, 3, HID])
        wab = sb("wab", [P, NSUB, HID])
        wq = sb("wq", [P, HID])
        wc = sb("wc", [P, NSUB, P])
        wf1 = sb("wf1", [P, P])
        w1_hi, w1_lo = (sb(f"w1_{p}", [P, NSUB, NX * EH], FP32R) for p in ("hi", "lo"))
        w2_hi, w2_lo = (sb(f"w2_{p}", [P, NSUB, D], FP32R) for p in ("hi", "lo"))
        wg_parts = sb("wg_parts", [P, NSUB, P], FP32R)
        bgate_c = sb("bgate_c", [2 * NX, 1])
        fold = sb("fold", [2 * NX, NX])
        cols = sb("cols", [P, 24])
        bpre0_c, bq_c = cols[:, 0:1], cols[:, 1:2]
        bg1_c, bg2_c, half_c = cols[:, 2:4], cols[:, 4:6], cols[:, 6:7]
        lng_c, lnb_c, b1_c, b1p_c = cols[:, 8:12], cols[:, 12:16], cols[:, 16:20], cols[:, 20:24]
        bnd0_r = sb("bnd0_r", [P, MUL])
        bo0_r = sb("bo0_r", [P, MUL])
        outg_r = sb("outg_r", [P, D])
        outb_r = sb("outb_r", [P, D])
        stats = sb("stats", [P, NT, 2 * NSUB])
        ea32 = sb("ea32", [P, EC * HID])
        ea4 = sb("ea4", [P, EC * 4])
        key_i = sb("key_i", [P, EC], I32)
        gsrc_i = sb("gsrc_i", [P, EC], I32)
        gdst_i = sb("gdst_i", [P, EC], I32)

        ARENA = 21400
        arena = sb("arena", [P, ARENA])
        at = [0]

        def take(*shape):
            n = math.prod(shape)
            v = arena[:, at[0]:at[0] + n]
            at[0] += n
            assert at[0] <= ARENA, at
            if len(shape) == 2:
                v = v.rearrange("p (a b) -> p a b", a=shape[0])
            return v

        def parts(w_hi, w_lo, a_hi, a_lo):
            return ((w_hi, a_hi), (w_hi, a_lo), (w_lo, a_hi))

        xhT_hi, xhT_lo = (sb(f"xhT_{p}", [P, 4, TILE], FP32R) for p in ("hi", "lo"))
        hg_hi, hg_lo = (sb(f"hg_{p}", [P, 4, TILE], FP32R) for p in ("hi", "lo"))

        wf2_hi, wf2_lo = xhT_hi[:, 0, :], xhT_lo[:, 0, :]
        ws2_hi, ws2_lo = xhT_hi[:, 1, :], xhT_lo[:, 1, :]
        hh_hi = hg_hi[:, 2, 0:2 * P]
        wg1_hi, wg1_lo, wg2_hi, wg2_lo = (part[:, c, :].rearrange("p (k n) -> p k n", k=2)
                                          for c in (2, 3) for part in (hg_hi, hg_lo))
        in_hi, in_lo = xhT_hi[:, 2:4, :], xhT_lo[:, 2:4, :]
        g_hi, g_lo = hg_hi[:, 0:2, :], hg_lo[:, 0:2, :]
        hb_hi, hb_lo = ([part[:, j // 2, j % 2 * 2 * P:(j % 2 + 1) * 2 * P] for j in range(NSUB)]
                        for part in (hg_hi, hg_lo))

        QP_AT, FT_AT, WG_AT = 13400, 16700, 20800
        at[0] = QP_AT
        b2_raw, sel_a, sel_c = (take(D)[0:3 * NX, :] for _ in range(3))
        wf2, ws2 = take(D), take(D)
        at[0] = FT_AT
        w1, w2 = take(NSUB, NX * EH), take(NSUB, D)
        at[0] = WG_AT
        wg = take(NSUB, P)

        psum = [ctx.enter_context(nc.psum_tensor(f"bank{i}", [P, 512], FP32)) for i in range(8)]

        block = ctx.enter_context(nc.Block())

        w_gate, w_edge, w_late = sem("w_gate"), sem("w_edge"), sem("w_late")
        e_in = sem("e_in")
        z_pool = sem("z_pool")
        z_hi, z_edge = sem("z_hi"), sem("z_edge")
        z_scaled, z_w1, z_lo, z_w2 = (sem(n) for n in ("z_scaled", "z_w1", "z_lo", "z_w2"))
        dve_passed, pool_passed = sem("dve_passed"), sem("pool_passed")
        z_dve = sem("z_dve")
        z_pe = sem("z_pe")
        @block.gpsimd
        def _(pool):
            nc.gpsimd.memset(sel_a, 1.0)
            nc.gpsimd.memset(sel_c, 1.0)
            nc.gpsimd.memset(rows_of[:], 1.0)
            nc.gpsimd.memset(wg, 0.0)
            nc.gpsimd.memset(bgate_c[:], 0.0)
            for tile, value in ((ident, 0.0), (lower, 0.0), (middle, -1.0), (mhalf, -0.5), (eps4, EPS),
                                (ea32, 0.0), (ea4, 0.0), (wf1, 0.0), (wc, 0.0)):
                last = nc.gpsimd.memset(tile[:], value)
            nc.gpsimd.memset(half_c, 0.5)
            nc.gpsimd.memset(zeros[:], 0.0)
            nc.gpsimd.iota(spare_i[:], pattern=[[0, NSUB]], base=N, channel_multiplier=1)
            nc.gpsimd.memset(key_i[:], PAD_KEY)
            nc.gpsimd.memset(gsrc_i[:], 0)
            nc.gpsimd.memset(gdst_i[:], 0).then_inc(z_pool, 1)
            nc.gpsimd.iota(iota_i[:], pattern=[[1, NX]], base=0, channel_multiplier=0).then_inc(z_pool, 1)
            pool.wait_ge(z_pool, 2)
            nc.gpsimd.affine_select(out=ident[:], in_=ident[:], compare_op=ALU.not_equal, fill=1.0,
                                    base=0, pattern=[[-1, P]], channel_multiplier=1)
            nc.gpsimd.affine_select(out=lower[:], in_=lower[:], compare_op=ALU.is_ge, fill=1.0,
                                    base=0, pattern=[[1, P]], channel_multiplier=-1)
            nc.gpsimd.tensor_copy(iota8[:], iota_i[:])
            nc.gpsimd.tensor_copy(spare[:], spare_i[:])
            nc.gpsimd.affine_select(out=middle[:], in_=middle[:], compare_op=ALU.is_ge, fill=0.0,
                                    base=-NX, pattern=[[0, 1]], channel_multiplier=1)
            nc.gpsimd.affine_select(out=rows_of[:], in_=rows_of[:], compare_op=ALU.is_ge, fill=0.0,
                                    base=0, pattern=[[-HID, NSUB]], channel_multiplier=1)
            for tile, first in ((sel_a, 0), (sel_c, 2 * NX)):
                last = nc.gpsimd.affine_select(out=tile, in_=tile, compare_op=ALU.is_ge, fill=0.0,
                                               base=EH * first, pattern=[[1, NX * EH]], channel_multiplier=-EH)
            last.then_inc(z_pool, 1)
            pool.wait_ge(z_pool, 3)
            nc.gpsimd.affine_select(out=middle[:], in_=middle[:], compare_op=ALU.is_ge, fill=0.0,
                                    base=2 * NX - 1, pattern=[[0, 1]], channel_multiplier=-1)
            nc.gpsimd.affine_select(out=rows_of[:], in_=rows_of[:], compare_op=ALU.is_ge, fill=0.0,
                                    base=HID - 1, pattern=[[HID, NSUB]], channel_multiplier=-1)
            for tile, first in ((sel_a, 0), (sel_c, 2 * NX)):
                last = nc.gpsimd.affine_select(out=tile, in_=tile, compare_op=ALU.is_ge, fill=0.0,
                                               base=EH - 1 - EH * first, pattern=[[-1, NX * EH]], channel_multiplier=EH)
            last.then_inc(z_pool, 1)

        GATE_LOADS, EDGE_LOADS, LATE_LOADS = 11, 2 * NSUB + 3, NSUB + 10

        @block.scalar
        def _(act):
            loads = [(wpre0[:], W_pre0), (ws1[:], W_s1.rearrange("(k p) n -> p k n", p=P)),
                     (bpre0_c, b_pre0.rearrange("(p a) -> p a", a=1)),
                     (wpre1[:], W_pre1), (wg1[:], W_g1.rearrange("(k p) n -> p k n", p=P)),
                     (bg1_c, b_g1.rearrange("(k p) -> p k", p=P)),
                     (wg2[:], W_g2.rearrange("(k p) n -> p k n", p=P)),
                     (bg2_c, b_g2.rearrange("(k p) -> p k", p=P)),
                     (wnd0[:], W_nd0), (wnd1[:], W_nd1),
                     (bnd0_r[:], b_nd0.rearrange("(a n) -> a n", a=1).to_broadcast([P, MUL]))]
            assert len(loads) == GATE_LOADS
            with nc.allow_non_contiguous_dma(reason="bias columns, once"):
                for tile, dram in loads:
                    act.dma_start(tile, dram).then_inc(w_gate, 16)

        def load_the_rest(sp):
            with nc.allow_non_contiguous_dma(reason="bias columns, once"):
                for j in range(NSUB):
                    sp.dma_start(wf2[HID * j:HID * (j + 1), :], W_f2).then_inc(w_edge, 16)
                    sp.dma_start(ws2[HID * j:HID * (j + 1), :], W_s2).then_inc(w_edge, 16)
                for r in range(3):
                    sp.dma_start(b2_raw[r * NX:(r + 1) * NX, :], b2).then_inc(w_edge, 16)
                loads = [(w1[:, c, :].rearrange("p (e h) -> p e h", e=NX),
                          W1[:, c * P:(c + 1) * P, :].rearrange("e p h -> p e h")) for c in range(NSUB)]
                loads += [(w2, W2.rearrange("e h d -> (e h) d").rearrange("(k p) d -> p k d", p=P)),
                          (lng_c, ln_g.rearrange("(k p) -> p k", p=P)),
                          (lnb_c, ln_b.rearrange("(k p) -> p k", p=P)),
                          (b1_c, b1.rearrange("e h -> (e h)").rearrange("(k p) -> p k", p=P)),
                          (wg[:, :, 0:NX], Wg.rearrange("(k p) n -> p k n", p=P)),
                          (wo0[:], W_o0), (wo1[:], W_o1),
                          (bo0_r[:], b_o0.rearrange("(a n) -> a n", a=1).to_broadcast([P, MUL])),
                          (outg_r[:], out_g.rearrange("(a n) -> a n", a=1).to_broadcast([P, D])),
                          (outb_r[:], out_b.rearrange("(a n) -> a n", a=1).to_broadcast([P, D]))]
                sp.wait_ge(z_pool, 1)
                for tile, dram in loads:
                    sp.dma_start(tile, dram).then_inc(w_late, 16)
                assert len(loads) == LATE_LOADS
                for j in range(NSUB):
                    sp.dma_start(wf1[HID * j:HID * (j + 1), HID * j:HID * (j + 1)], W_f1).then_inc(e_in, 16)
                sp.dma_start(acc[N:N + P, :], zeros[:]).then_inc(e_in, 16)
                sp.dma_start(ea32[0:EP, :], edge_attr_32.rearrange("(p t) h -> p (t h)", p=EP)).then_inc(e_in, 16)
                sp.dma_start(ea4[0:EP, :], edge_attr_4.rearrange("(p t) h -> p (t h)", p=EP)).then_inc(e_in, 16)
                sp.dma_start(key_i[0:EP, :], src.rearrange("(p t) -> p t", p=EP)).then_inc(e_in, 16)
                sp.dma_start(gsrc_i[0:EP, :], src.rearrange("(p t) -> p t", p=EP)).then_inc(e_in, 16)
                sp.dma_start(gdst_i[0:EP, :], dst.rearrange("(p t) -> p t", p=EP)).then_inc(e_in, 16)

        E_TOTAL = 16 * (NSUB + 6)

        @block.tensor
        def _(pe):
            pe.wait_ge(w_gate, 16 * GATE_LOADS)
            pe.wait_ge(z_pool, 4)
            nc.tensor.transpose(psum[0][:, 0:P], wpre0[:], ident[:]).then_inc(z_pe, 1)
            pe.wait_ge(z_dve, 2)
            nc.tensor.matmul(psum[3][:, 0:HID], wpre0T[:], wab[:, 0, :], start=True, stop=True)
            nc.tensor.matmul(psum[4][:, 0:1], wab[:].rearrange("p j h -> p (j h)"), bpre0_c,
                             start=True, stop=True).then_inc(z_pe, 1)

        SETUP_DVE = 3

        def prepare_q(dve):
            dve.wait_ge(w_gate, 16 * GATE_LOADS)
            dve.wait_ge(z_pool, 4)
            nc.vector.tensor_tensor(wab[:], ws1[:, 0:1, :].to_broadcast([P, NSUB, HID]),
                                    ws1[:, 1:2, :].to_broadcast([P, NSUB, HID]), ALU.add).then_inc(z_dve, 1)
            dve.wait_ge(z_pe, 1)
            nc.vector.tensor_copy(wpre0T[:], psum[0][:, 0:P]).then_inc(z_dve, 1)
            dve.wait_ge(z_pe, 2)
            nc.vector.tensor_copy(wq[:], psum[3][:, 0:HID])
            nc.vector.tensor_copy(bq_c, psum[4][:, 0:1]).then_inc(z_dve, 1)

        def prepare_edge_weights(dve):
            dve.wait_ge(w_edge, 16 * EDGE_LOADS)
            nc.vector.tensor_scalar(ws2[:, 3 * MUL:D], ws2[:, 3 * MUL:D], 1.0 / math.sqrt(3.0), None,
                                    ALU.mult).then_inc(z_hi, 1)
            b2_hi = xhT_hi[0:3 * NX, 3, :]
            nc.vector.tensor_copy(b2_hi, b2_raw)
            nc.vector.tensor_copy(wf2_hi, wf2)
            nc.vector.tensor_copy(wg1_hi, wg1[:])
            nc.vector.tensor_copy(wg2_hi, wg2[:])
            dve.wait_ge(z_hi, 1)
            nc.vector.tensor_copy(ws2_hi, ws2).then_inc(z_hi, 1)
            nc.vector.tensor_tensor(sel[:], sel_a, sel_c, ALU.add)
            for j in range(NSUB):
                nc.vector.tensor_scalar(wc[:, j, HID * j:HID * (j + 1)], ws1[:, 2, :], 1.0 / 3.0, None, ALU.mult)
            nc.vector.tensor_tensor(fold[:], ident[0:2 * NX, 0:NX], ident[0:2 * NX, NX:2 * NX], ALU.add)
            dve.wait_ge(z_hi, 2)
            nc.vector.tensor_tensor(wf2_lo, wf2, wf2_hi.bitcast(FP32), ALU.subtract)
            nc.vector.tensor_tensor(wg1_lo, wg1[:], wg1_hi.bitcast(FP32), ALU.subtract)
            nc.vector.tensor_tensor(wg2_lo, wg2[:], wg2_hi.bitcast(FP32), ALU.subtract)
            nc.vector.tensor_tensor(ws2_lo, ws2, ws2_hi.bitcast(FP32), ALU.subtract)
            nc.vector.scalar_tensor_tensor(out=b2s[:], in0=b2_hi.bitcast(FP32), scalar=middle[:, 0:1], in1=b2_raw,
                                           op0=ALU.mult, op1=ALU.add).then_inc(z_edge, 1)

        def products_with_ln_b(pe):
            pe.wait_ge(w_late, 16 * LATE_LOADS)
            for k in range(NSUB):
                for c in range(NSUB):
                    nc.tensor.matmul(psum[3][:, k:k + 1], w1[:, c, k * P:(k + 1) * P], lnb_c[:, c:c + 1],
                                     start=(c == 0), stop=(c == NSUB - 1))
            for c in range(NSUB):
                last = nc.tensor.matmul(psum[2][0:NX, 0:1], wg[:, c, 0:NX], lnb_c[:, c:c + 1],
                                        start=(c == 0), stop=(c == NSUB - 1))
            last.then_inc(z_pe, 1)

        def prepare_expert_weights(dve):
            dve.wait_ge(w_late, 16 * LATE_LOADS)
            dve.wait_ge(z_pe, 3)
            nc.vector.tensor_tensor(b1p_c, psum[3][:, 0:NSUB], b1_c, ALU.add)
            nc.vector.tensor_copy(bgate_c[0:NX, :], psum[2][0:NX, 0:1])
            for c in range(NSUB):
                nc.vector.tensor_scalar(w1[:, c, :], w1[:, c, :], lng_c[:, c:c + 1], None, ALU.mult)
                last = nc.vector.tensor_scalar(wg[:, c, 0:NX], wg[:, c, 0:NX], lng_c[:, c:c + 1], None, ALU.mult)
            last.then_inc(z_scaled, 1)
            dve.wait_ge(z_scaled, 1)
            nc.vector.tensor_copy(w1_hi[:], w1)
            nc.vector.tensor_copy(w2_hi[:], w2)
            nc.vector.tensor_copy(wg_parts[:], wg).then_inc(z_w1, 1)
            dve.wait_ge(z_w1, 1)
            nc.vector.tensor_tensor(wg_parts[:, :, NX:2 * NX], wg[:, :, 0:NX], wg_parts[:, :, 0:NX].bitcast(FP32),
                                    ALU.subtract)
            nc.vector.tensor_tensor(w2_lo[:], w2, w2_hi[:].bitcast(FP32), ALU.subtract).then_inc(z_w2, 1)

        def low_part_of_w1(pool):
            pool.wait_ge(z_w1, 1)
            nc.gpsimd.tensor_tensor(w1_lo[:], w1, w1_hi[:].bitcast(FP32), ALU.subtract).then_inc(z_lo, 1)

        at[0] = 0
        a_x = [take(NSUB, D) for _ in range(2)]
        a_xT = [take(4, TILE) for _ in range(2)]
        a_sq = take(3, TILE)
        a_n1 = take(TILE)
        a_g = take(2, TILE)
        a_xg = take(4, TILE)
        a_bn = take(NSUB, 6)
        a_mv = [take(NSUB, 2) for _ in range(2)]
        a_rn = [take(2, NSUB) for _ in range(2)]
        assert at[0] <= QP_AT
        a_qp = [take(NSUB, QP) for _ in range(2)]
        assert at[0] <= FT_AT
        a_ft = [take(NSUB, D) for _ in range(2)]
        assert at[0] <= WG_AT
        A_T, A_ND, A_P, A_G = psum[0:2], psum[2:4], psum[4:6], psum[6:8]

        x_in = [sem(f"a_x_in{b}") for b in range(2)]
        qp_out = [sem(f"a_qp_out{b}") for b in range(2)]
        ft_out = [sem(f"a_ft_out{b}") for b in range(2)]
        row_out = qp_out + ft_out
        s_bn, s_mv, s_rstd, s_nmr, s_xn = (sem(n) for n in ("a_bn", "a_mv", "a_rstd", "a_nmr", "a_xn"))
        s_var = sem("a_var")
        s_t, s_tact, s_tdve = sem("a_t"), sem("a_t_act"), sem("a_t_dve")
        s_p, s_pact, s_pdve = sem("a_p"), sem("a_p_act"), sem("a_p_dve")
        s_sq, s_n1 = sem("a_sq"), sem("a_n1")
        s_inhi, s_inlo, s_ghi, s_glo = (sem(n) for n in ("a_in_hi", "a_in_lo", "a_g_hi", "a_g_lo"))
        s_g1, s_silu, s_g2, s_g0, s_xg = (sem(n) for n in ("a_g1", "a_silu", "a_g2", "a_g0", "a_xg"))
        s_nd, s_ndev = sem("a_nd"), sem("a_nd_ev")


        @block.sync
        def _(sp):
            def load(s, k, b):
                after(sp, s_t, 4 * (s - 1))
                sp.dma_start(a_x[b], rows(x, s)).then_inc(x_in[b], 16)

            def step(s, k, b):
                if runs(s, -2):
                    load(s + 2, k + 1, b)
                if runs(s, 2):
                    t = s - 2
                    sp.wait_ge(s_ndev, 4 * (s - 1))
                    if isinstance(t, int) and t == NT - 1:
                        sp.wait_ge(ft_out[1 - b], 32 * (NT // 2))
                    sp.dma_start(rows(by_dst, t)[:, :, 3 * MUL:PX], a_ft[b]).then_inc(ft_out[b], 16)
                    sp.dma_start(rows(acc, t), a_ft[b]).then_inc(ft_out[b], 16)
                if runs(s, 0):
                    sp.wait_ge(s_pact, 2 * s + 2)
                    sp.wait_ge(s_pdve, 2 * s + 2)
                    if isinstance(s, int) and s == NT - 1:
                        sp.wait_ge(qp_out[1 - b], 32 * (NT // 2))
                    sp.dma_start(rows(by_src, s), a_qp[b]).then_inc(qp_out[b], 16)
                    sp.dma_start(rows(by_dst, s)[:, :, 0:3 * MUL], a_qp[b][:, :, HID:QP]).then_inc(qp_out[b], 16)

            load(0, 0, 0)
            load(1, 0, 1)
            load_the_rest(sp)
            pipeline(sp, step, NT + 1, tail=4)

        @block.vector
        def _(dve):
            def statistics(s, k, b):
                dve.wait_ge(x_in[b], 16 * k + 16)
                for j in range(NSUB):
                    last = nc.vector.bn_stats(a_bn[:, j, :], a_x[b][:, j, :])
                last.then_inc(s_bn, 1)
                dve.wait_ge(s_bn, s + 1)
                if not isinstance(s, int) or s >= 2:
                    dve.wait_ge(s_xn, s - 1)
                settled(dve, dve_passed)
                for j in range(NSUB):
                    last = nc.vector.bn_aggr(a_mv[b][:, j, :], a_bn[:, j, :])
                last.then_inc(s_mv, 1)

            def shift(s, b):
                dve.wait_ge(s_rstd, s + 1)
                nc.vector.scalar_tensor_tensor(out=a_rn[b][:, 1, :], in0=a_mv[b][:, :, 0], scalar=-1.0,
                                               in1=a_rn[b][:, 0, :], op0=ALU.mult, op1=ALU.mult).then_inc(s_nmr, 1)

            def transposed(s, b, c):
                dve.wait_ge(s_t, 4 * s + c + 1)
                nc.vector.tensor_copy(a_xT[b][:, c, :], A_T[1][:]).then_inc(s_tdve, 1)

            def input_low(s, b, c):
                dve.wait_ge(s_inhi, 2 * s + c + 1)
                nc.vector.tensor_tensor(in_lo[:, c, :], a_n1 if c else a_xT[b][:, 0, :], in_hi[:, c, :].bitcast(FP32),
                                        ALU.subtract).then_inc(s_inlo, 1)

            def hidden_low(t, c):
                dve.wait_ge(s_ghi, 2 * t + c + 1)
                nc.vector.tensor_tensor(g_lo[:, c, :], a_g[:, c, :], g_hi[:, c, :].bitcast(FP32),
                                        ALU.subtract).then_inc(s_glo, 1)

            def features(u, j, b):
                dve.wait_ge(s_nd, 4 * u + j + 1)
                nc.vector.tensor_tensor(a_ft[b][:, j, 0:MUL], A_ND[j % 2][:, 0:MUL], bnd0_r[:], ALU.add)
                nc.vector.tensor_copy(a_ft[b][:, j, MUL:D], A_ND[j % 2][:, MUL:D]).then_inc(s_ndev, 1)

            def step(s, k, b):
                t, u, o = s - 1, s - 2, 1 - b
                if runs(s, 0):
                    after(dve, s_xg, s - 1)
                    transposed(s, b, 1)
                if runs(s, -1):
                    statistics(s + 1, k + b, o)
                if runs(s, 0):
                    transposed(s, b, 3)
                if isinstance(s, int) and s == 2:
                    dve.wait_ge(z_lo, 1)
                    dve.wait_ge(z_w2, 1)
                if runs(s, 2):
                    after(dve, ft_out[b], 32 * (k - 1))
                    features(u, 0, b)
                    features(u, 1, b)
                if runs(s, -1):
                    shift(s + 1, o)
                if runs(s, 1):
                    hidden_low(t, 0)
                    hidden_low(t, 1)
                if runs(s, 2):
                    features(u, 2, b)
                    features(u, 3, b)
                if runs(s, 0):
                    input_low(s, b, 0)
                    nc.vector.tensor_copy(stats[:, bass.ds(s, 1), :].rearrange("p a n -> p (a n)"),
                                          a_rn[b].rearrange("p a n -> p (a n)"))
                if runs(s, 1):
                    dve.wait_ge(s_tact, 2 * t + 2)
                    dve.wait_ge(s_g2, 2 * t + 2)
                    after(dve, s_nd, 4 * t)
                    nc.vector.scalar_tensor_tensor(
                        out=a_xg[:, 1:4, :], in0=A_G[1][:, None, :].to_broadcast([P, 3, TILE]),
                        scalar=bg2_c[:, 1:2], in1=a_xT[o][:, 1:4, :], op0=ALU.add, op1=ALU.mult).then_inc(s_xg, 1)
                if runs(s, 0):
                    if isinstance(s, int) and s == 0:
                        prepare_edge_weights(dve)
                        dve.wait_ge(z_edge, 1)
                    after(dve, qp_out[b], 32 * k)
                    for j in (1, 3):
                        dve.wait_ge(s_p, 4 * s + j + 1)
                        nc.vector.tensor_copy(a_qp[b][:, j, :], A_P[1][:, 0:QP]).then_inc(s_pdve, 1)
                    input_low(s, b, 1)
                if isinstance(s, int) and s == 1:
                    prepare_expert_weights(dve)

            statistics(0, 0, 0)
            prepare_q(dve)
            shift(0, 0)
            dve.wait_ge(s_nmr, 1)
            pipeline(dve, step, NT + 1)

        @block.gpsimd
        def _(pool):
            def rstd(s, b):
                pool.wait_ge(s_mv, s + 1)
                nc.gpsimd.tensor_tensor(a_rn[b][:, 0, :], a_mv[b][:, :, 1], eps4[:], ALU.add).then_inc(s_var, 1)
                pool.wait_ge(s_var, s + 1)
                nc.gpsimd.tensor_tensor(a_rn[b][:, 0, :], a_rn[b][:, 0, :], mhalf[:], ALU.pow).then_inc(s_rstd, 1)

            def square(s, b, c):
                nc.gpsimd.tensor_tensor(a_sq[:, c, :], a_xT[b][:, 1 + c, :], a_xT[b][:, 1 + c, :],
                                        ALU.mult).then_inc(s_sq, 1)

            def step(s, k, b):
                pool.wait_ge(s_tdve, 2 * s + 1)
                after(pool, s_n1, s)
                square(s, b, 0)
                if runs(s, -1):
                    rstd(s + 1, 1 - b)
                pool.wait_ge(s_tact, 2 * s + 2)
                square(s, b, 1)
                pool.wait_ge(s_sq, 5 * s + 2)
                nc.gpsimd.tensor_tensor(a_sq[:, 0, :], a_sq[:, 0, :], a_sq[:, 1, :], ALU.add).then_inc(s_sq, 1)
                pool.wait_ge(s_tdve, 2 * s + 2)
                square(s, b, 2)
                pool.wait_ge(s_sq, 5 * s + 4)
                nc.gpsimd.tensor_tensor(a_sq[:, 0, :], a_sq[:, 0, :], a_sq[:, 2, :], ALU.add).then_inc(s_sq, 1)
                if isinstance(s, int) and s == 1:
                    low_part_of_w1(pool)

            rstd(0, 0)
            pipeline(pool, step, NT - 1)

        @block.scalar
        def _(act):
            act.wait_ge(z_dve, SETUP_DVE)

            def normalise(s, b):
                act.wait_ge(s_nmr, s + 1)
                for j in range(NSUB):
                    last = nc.scalar.activation(a_x[b][:, j, :], a_x[b][:, j, :], ACT.Identity,
                                                bias=a_rn[b][:, 1, j:j + 1], scale=a_rn[b][:, 0, j:j + 1])
                last.then_inc(s_xn, 1)

            def transposed(s, b, c):
                act.wait_ge(s_t, 4 * s + c + 1)
                nc.scalar.activation(a_xT[b][:, c, :], A_T[0][:], ACT.Copy).then_inc(s_tact, 1)

            def row(s, b, j):
                act.wait_ge(s_p, 4 * s + j + 1)
                nc.scalar.activation(a_qp[b][:, j, :], A_P[0][:, 0:QP], ACT.Copy).then_inc(s_pact, 1)

            def step(s, k, b):
                t, o = s - 1, 1 - b
                if runs(s, 0):
                    after(act, s_xg, s - 1)
                    transposed(s, b, 0)
                if runs(s, 1):
                    for c in range(2):
                        act.wait_ge(s_g1, 2 * t + c + 1)
                        after(act, s_glo, 2 * t - 1 + c)
                        nc.scalar.activation(a_g[:, c, :], A_G[c][:], ACT.Silu, bias=bg1_c[:, c:c + 1]).then_inc(s_silu, 1)
                if runs(s, 0):
                    transposed(s, b, 2)
                if runs(s, 1):
                    for c in range(2):
                        act.wait_ge(s_silu, 2 * t + c + 1)
                        after(act, s_g2, 2 * t)
                        nc.scalar.activation(g_hi[:, c, :], a_g[:, c, :], ACT.Copy).then_inc(s_ghi, 1)
                if runs(s, 0):
                    act.wait_ge(s_tact, 2 * s + 1)
                    after(act, s_g1, 2 * s)
                    nc.scalar.activation(in_hi[:, 0, :], a_xT[b][:, 0, :], ACT.Copy).then_inc(s_inhi, 1)
                if runs(s, -1):
                    normalise(s + 1, o)
                if runs(s, 1):
                    act.wait_ge(s_g2, 2 * t + 1)
                    after(act, s_nd, 4 * t)
                    nc.scalar.activation(a_xg[:, 0, :], A_G[0][:], ACT.Identity, bias=bg2_c[:, 0:1]).then_inc(s_g0, 1)
                if runs(s, 0):
                    if isinstance(s, int) and s == 0:
                        act.wait_ge(z_edge, 1)
                    after(act, qp_out[b], 32 * k)
                    row(s, b, 0)
                    nc.scalar.preload_act_table_set("sqrt_and_others")
                    act.wait_ge(s_sq, 5 * s + 5)
                    after(act, s_inlo, 2 * s)
                    nc.scalar.activation(a_n1, a_sq[:, 0, :], ACT.Sqrt, scale=1.0 / 3.0).then_inc(s_n1, 1)
                    act.wait_ge(s_n1, s + 1)
                    nc.scalar.activation(in_hi[:, 1, :], a_n1, ACT.Copy).then_inc(s_inhi, 1)
                    nc.scalar.preload_act_table_set("silu_and_others")
                    row(s, b, 2)

            normalise(0, 0)
            pipeline(act, step, NT)

        @block.tensor
        def _(pe):
            pe.wait_ge(z_dve, SETUP_DVE)

            def transpose_x(s, b, chunks):
                for c in chunks:
                    if c == 0:
                        pe.wait_ge(s_xn, s + 1)
                    after(pe, s_tdve if c % 2 else s_tact, 2 * s + c // 2)
                    for j in range(NSUB):
                        v = a_x[b][:, j, 0:MUL] if c == 0 else a_x[b][:, j, MUL + c - 1:D:3]
                        last = nc.tensor.transpose(A_T[c % 2][:, j * P:(j + 1) * P], v, ident[:])
                    last.then_inc(s_t, 1)

            def gate_hidden(t):
                if not isinstance(t, int) or t > 0:
                    pe.wait_ge(s_g0, t)
                    pe.wait_ge(s_xg, t)
                else:
                    pe.wait_ge(z_edge, 1)
                for c in range(2):
                    pe.wait_ge(s_inlo, 2 * t + c + 1)
                    for o in range(2):
                        for i, (w, v) in enumerate(parts(wg1_hi, wg1_lo, in_hi, in_lo)):
                            last = nc.tensor.matmul(A_G[o][:], w[:, c, o * P:(o + 1) * P], v[:, c, :],
                                                    start=(c == 0 and i == 0), stop=(c == 1 and i == 2))
                        if c == 1:
                            last.then_inc(s_g1, 1)

            def gate(t):
                pe.wait_ge(s_glo, 2 * t + 2)
                for o in range(2):
                    for c in range(2):
                        for i, (w, v) in enumerate(parts(wg2_hi, wg2_lo, g_hi, g_lo)):
                            last = nc.tensor.matmul(A_G[o][:], w[:, c, o * P:(o + 1) * P], v[:, c, :],
                                                    start=(c == 0 and i == 0), stop=(c == 1 and i == 2))
                    last.then_inc(s_g2, 1)

            def node_features(t):
                pe.wait_ge(s_g0, t + 1)
                pe.wait_ge(s_xg, t + 1)
                for j in range(NSUB):
                    after(pe, s_ndev, 4 * t + j - 1)
                    for c in range(4):
                        last = nc.tensor.matmul(A_ND[j % 2][:, c * MUL:(c + 1) * MUL], a_xg[:, c, j * P:(j + 1) * P],
                                                wnd0[:] if c == 0 else wnd1[:], start=True, stop=True)
                    last.then_inc(s_nd, 1)

            def q_p1(s, xT):
                pe.wait_ge(s_tact, 2 * s + 2)
                pe.wait_ge(s_tdve, 2 * s + 2)
                for j in range(NSUB):
                    after(pe, s_pdve if j % 2 else s_pact, 2 * s + j // 2)
                    nc.tensor.matmul(A_P[j % 2][:, 0:HID], xT[:, 0, j * P:(j + 1) * P], wq[:], start=True, stop=True)
                    for c in range(3):
                        last = nc.tensor.matmul(A_P[j % 2][:, HID + c * MUL:HID + (c + 1) * MUL],
                                                xT[:, 1 + c, j * P:(j + 1) * P], wpre1[:], start=True, stop=True)
                    last.then_inc(s_p, 1)

            def step(s, k, b):
                if isinstance(s, int) and s == 2:
                    pe.wait_ge(z_w1, 1)
                if runs(s, 0):
                    transpose_x(s, b, (0, 1))
                if runs(s, 1):
                    gate_hidden(s - 1)
                if runs(s, 0):
                    transpose_x(s, b, (2, 3))
                if runs(s, 2):
                    node_features(s - 2)
                if runs(s, 1):
                    gate(s - 1)
                if runs(s, 0):
                    q_p1(s, a_xT[b])
                if isinstance(s, int) and s == 1:
                    products_with_ln_b(pe)

            pipeline(pe, step, NT + 1)

        at[0] = 0
        b_gs = [take(NSUB, QP) for _ in range(2)]
        b_gd = [take(NSUB, PX) for _ in range(2)]
        b_pr = [take(3, MUL) for _ in range(2)]
        b_ipT = take(TILE)
        b_q = take(NSUB, HID)
        b_ea = take(P)
        b_eaT = take(P)
        b_hp = take(2 * P)
        b_ln = take(2 * P)
        b_hh = take(2 * P)
        b_wa = [take(D) for _ in range(2)]
        b_w = take(4, MUL)
        b_xs = [take(8, MUL) for _ in range(2)]
        b_y = take(8, MUL)
        b_msg = [take(4, MUL) for _ in range(2)]
        b_s = [take(NSUB, P) for _ in range(2)]
        b_sl = take(NSUB, P)
        b_out = [take(D) for _ in range(2)]
        b_key = [take(NSUB) for _ in range(2)]
        b_cnt = take(NSUB)
        b_idx = take(NSUB)
        b_sh = [take(NSUB, 4) for _ in range(2)]
        b_gsi = [sb(f"b_gsi{b}", [P, NSUB], U32) for b in range(2)]
        b_gdi = [sb(f"b_gdi{b}", [P, NSUB], U32) for b in range(2)]
        b_sci = [sb(f"b_sci{b}", [P, NSUB], U32) for b in range(2)]
        B_A, B_B, B_AGG, B_T, B_H = psum[0:2], psum[2:4], psum[4:6], psum[6], psum[7]

        gather = [[sem(f"b_gather{b}{j}") for j in range(NSUB)] for b in range(2)]
        added = sem("b_added")
        q_idx, q_ea, q_pr, q_ipt, q_ipe = (sem(f"b_{n}") for n in ("idx", "ea", "pr", "ipt", "ipe"))
        q_eat, q_eae, q_h, q_hp, q_act, q_hh = (sem(f"b_{n}") for n in ("eat", "eae", "h", "hp", "act", "hh"))
        q_ab, q_ae, q_w, q_y, q_agg, q_oe = (sem(f"b_{n}") for n in ("ab", "ae", "w", "y", "agg", "oe"))
        q_hi, q_hb = sem("b_hi"), sem("b_hb")
        q_dot, q_xs, q_msg = sem("b_dot"), sem("b_xs"), sem("b_msg")
        q_q, q_sh, q_far = sem("b_q"), sem("b_sh"), sem("b_far")
        q_tr, q_s, q_sl, q_cnt, q_sci = (sem(f"b_{n}") for n in ("tr", "s", "sl", "cnt", "sci"))

        @block.vector
        def _(dve):
            dve.wait_ge(e_in, E_TOTAL)
            wait_all(dve, row_out, 32 * (NT // 2))

            def factors(s, b):
                after(dve, q_xs, 4 * (s - 1))
                nc.vector.tensor_copy(b_sh[b].rearrange("p j m -> p (j m)"),
                                      ea4[:, bass.ds(s * NSUB * 4, NSUB * 4)]).then_inc(q_sh, 1)

            def products(s, k, b, j):
                dve.wait_ge(gather[b][j], 32 * k + 32)
                after(dve, q_ipt, 4 * s + j - 1)
                nc.vector.tensor_tensor(b_pr[j % 2].rearrange("p c u -> p (c u)"), b_gs[b][:, j, HID:QP],
                                        b_gd[b][:, j, 0:3 * MUL], ALU.mult).then_inc(q_pr, 1)

            def collect_q(s, b):
                after(dve, q_h, s)
                nc.vector.tensor_copy(b_q, b_gs[b][:, :, 0:HID]).then_inc(q_q, 1)

            def shared_targets(s, b):
                dve.wait_ge(q_tr, s + 1)
                after(dve, q_agg, 4 * (s - 1))
                nc.vector.tensor_tensor(b_s[b], B_T[:].rearrange("p (j e) -> p j e", j=NSUB),
                                        b_key[b][:, :, None].to_broadcast([P, NSUB, P]), ALU.is_equal).then_inc(q_s, 1)
                dve.wait_ge(q_s, s + 1)
                nc.vector.tensor_tensor(b_sl, b_s[b], lower[:, None, :].to_broadcast([P, NSUB, P]),
                                        ALU.mult).then_inc(q_sl, 1)

            def add_indices(s, b):
                dve.wait_ge(q_sl, s + 1)
                nc.vector.tensor_reduce(out=b_cnt, in_=b_sl, axis=AX.X, op=ALU.add).then_inc(q_cnt, 1)
                dve.wait_ge(q_cnt, s + 1)
                nc.vector.scalar_tensor_tensor(out=b_idx, in0=b_cnt, scalar=float(FAR), in1=b_key[b],
                                               op0=ALU.mult, op1=ALU.add).then_inc(q_far, 1)
                dve.wait_ge(q_far, s + 1)
                after(dve, added, 64 * (s - 1))
                nc.vector.tensor_tensor(b_sci[b][:], b_idx, spare[:], ALU.min).then_inc(q_sci, 1)

            def softplus_end(s, k, b):
                dve.wait_ge(q_act, 3 * s + 3)
                after(dve, q_hb, 4 * s)
                nc.vector.scalar_tensor_tensor(out=hh_hi, in0=b_hp, scalar=0.0, in1=b_ln,
                                               op0=ALU.max, op1=ALU.add)
                nc.vector.scalar_tensor_tensor(out=b_hh, in0=b_hp, scalar=0.0, in1=b_ln,
                                               op0=ALU.max, op1=ALU.add).then_inc(q_hi, 1)
                dve.wait_ge(q_hi, s + 1)
                nc.vector.tensor_tensor(b_hh, b_hh, hh_hi.bitcast(FP32), ALU.subtract).then_inc(q_hh, 1)

            def message(t, o, j, meanwhile):
                n = 4 * t + j
                feat = b_gd[o][:, j, 3 * MUL:PX].rearrange("p (c u) -> p c u", u=MUL)
                xs = b_xs[j % 2]

                def dot(m):
                    if m == 0:
                        dve.wait_ge(q_sh, t + 1)
                        op = nc.vector.tensor_scalar(xs[:, 1, :], feat[:, 1, :], b_sh[o][:, j, 1:2], None, ALU.mult)
                    else:
                        dve.wait_ge(q_dot, 3 * n + m)
                        op = nc.vector.scalar_tensor_tensor(
                            out=xs[:, 1, :], in0=feat[:, 1 + m, :], scalar=b_sh[o][:, j, 1 + m:2 + m],
                            in1=xs[:, 1, :], op0=ALU.mult, op1=ALU.add)
                    op.then_inc(q_dot, 1)

                dot(0)
                meanwhile[0]()
                dot(1)
                dve.wait_ge(q_ae, n + 1)
                dve.wait_ge(q_ab, n + 1)
                nc.vector.tensor_tensor(b_w.rearrange("p c u -> p (c u)"), b_wa[j % 2], B_B[j % 2][:],
                                        ALU.mult).then_inc(q_w, 1)
                dot(2)
                dve.wait_ge(q_w, n + 1)
                dve.wait_ge(q_xs, n + 1)
                terms = b_y.rearrange("p (k c) u -> p k c u", k=2)
                nc.vector.tensor_tensor(terms[:, :, 1:4, :], b_w[:, 1:3, None, :].to_broadcast([P, 2, 3, MUL]),
                                        xs[:, 2:8, :].rearrange("p (k c) u -> p k c u", k=2), ALU.mult)
                dve.wait_ge(q_dot, 3 * n + 3)
                nc.vector.tensor_tensor(b_y[:, 0:8:4, :], b_w[:, 0:4:3, :], xs[:, 0:2, :], ALU.mult).then_inc(q_y, 1)
                meanwhile[1]()
                dve.wait_ge(q_y, n + 1)
                after(dve, q_agg, n - 1)
                nc.vector.tensor_tensor(b_msg[j % 2], b_y[:, 0:4, :], b_y[:, 4:8, :], ALU.add).then_inc(q_msg, 1)

            def step(s, k, b):
                t, o = s - 1, 1 - b

                def prepare(*blocks):
                    if runs(s, 0):
                        for j in blocks:
                            products(s, k, b, j)
                            if j == 3:
                                collect_q(s, b)

                def nothing():
                    pass

                if runs(s, 0):
                    factors(s, b)
                prepare(0, 1)
                if runs(s, 1):
                    message(t, o, 0, (nothing, lambda: prepare(2)))
                    message(t, o, 1, (lambda: prepare(3), nothing))
                    message(t, o, 2, (nothing, nothing))
                else:
                    prepare(2, 3)
                if runs(s, 0):
                    shared_targets(s, b)
                    softplus_end(s, k, b)
                if runs(s, 1):
                    message(t, o, 3, (nothing, nothing))
                if runs(s, 0):
                    add_indices(s, b)

            pipeline(dve, step, ET)

        @block.gpsimd
        def _(pool):
            wait_all(pool, row_out, 32 * (NT // 2))

            def indices(s, b):
                after(pool, q_sci, s - 1)
                nc.gpsimd.tensor_copy(b_gsi[b][:], gsrc_i[:, bass.ds(s * NSUB, NSUB)])
                nc.gpsimd.tensor_copy(b_gdi[b][:], gdst_i[:, bass.ds(s * NSUB, NSUB)])
                nc.gpsimd.tensor_copy(b_key[b], key_i[:, bass.ds(s * NSUB, NSUB)]).then_inc(q_idx, 1)

            def fetch(s, k, b, j):
                if j == 0:
                    pool.wait_ge(q_idx, s + 1)
                if not isinstance(s, int) or s >= 2:
                    pool.wait_ge(q_y, 4 * (s - 2) + j + 1)
                settled(pool, pool_passed)
                nc.gpsimd.indirect_dma_start(
                    out=b_gs[b][:, j, :], out_offset=None, in_=by_src[:, :],
                    in_offset=bass.IndirectOffsetOnAxis(ap=b_gsi[b][:, j:j + 1], axis=0)).then_inc(gather[b][j], 16)
                nc.gpsimd.indirect_dma_start(
                    out=b_gd[b][:, j, :], out_offset=None, in_=by_dst[:, :],
                    in_offset=bass.IndirectOffsetOnAxis(ap=b_gdi[b][:, j:j + 1], axis=0)).then_inc(gather[b][j], 16)

            def add(t, b, j):
                n = 4 * t + j
                pool.wait_ge(q_oe, n + 1)
                pool.wait_ge(q_sci, t + 1)
                after(pool, added, 16 * n)
                settled(pool, pool_passed)
                nc.gpsimd.indirect_dma_start(
                    out=acc[:, :], out_offset=bass.IndirectOffsetOnAxis(ap=b_sci[b][:, j:j + 1], axis=0),
                    in_=b_out[j % 2], in_offset=None, compute_op=ALU.add).then_inc(added, 16)

            def step(s, k, b):
                if runs(s, -1):
                    indices(s + 1, 1 - b)
                for j in range(NSUB):
                    if j == 0 and runs(s, 2):
                        add(s - 2, b, NSUB - 1)
                    if runs(s, -1):
                        fetch(s + 1, k + b, 1 - b, j)
                    if j < NSUB - 1 and runs(s, 1):
                        add(s - 1, 1 - b, j)

            pool.wait_ge(e_in, E_TOTAL)
            indices(0, 0)
            for j in range(NSUB):
                fetch(0, 0, 0, j)
            pipeline(pool, step, ET + 1)

        @block.scalar
        def _(act):
            wait_all(act, row_out, 32 * (NT // 2))
            nc.scalar.preload_act_table_set("natural_log_exp_and_others")

            def edge_hidden(s):
                act.wait_ge(q_eat, s + 1)
                nc.scalar.activation(b_eaT, B_H[:, 0:P], ACT.Copy).then_inc(q_eae, 1)
                act.wait_ge(q_ipt, 4 * s + 4)
                after(act, q_h, s)
                nc.scalar.activation(b_ipT, B_T[:], ACT.Copy).then_inc(q_ipe, 1)

            def hidden(s):
                act.wait_ge(q_h, s + 1)
                after(act, q_hh, s)
                nc.scalar.activation(b_hp[:, 0:P], B_H[:, P:2 * P], ACT.Copy)
                nc.scalar.activation(b_hp[:, P:2 * P], B_H[:, 2 * P:3 * P], ACT.Identity,
                                     bias=bq_c).then_inc(q_hp, 1)
                act.wait_ge(q_hp, s + 1)
                nc.scalar.activation(b_ln, b_hp, ACT.Abs).then_inc(q_act, 1)
                act.wait_ge(q_act, 3 * s + 1)
                nc.scalar.activation(b_ln, b_ln, ACT.Exp, scale=-1.0).then_inc(q_act, 1)
                act.wait_ge(q_act, 3 * s + 2)
                nc.scalar.activation(b_ln, b_ln, ACT.Ln, bias=half_c, scale=0.5).then_inc(q_act, 1)

            def spread_hidden(s, blocks):
                if blocks[0] == 0:
                    act.wait_ge(q_hh, s + 1)
                    after(act, q_ab, 4 * s)
                for j in blocks:
                    nc.scalar.activation(hb_hi[j], hh_hi.bitcast(FP32), ACT.Copy, scale=rows_of[:, j:j + 1])
                    nc.scalar.activation(hb_lo[j], b_hh, ACT.Copy, scale=rows_of[:, j:j + 1]).then_inc(q_hb, 1)

            def weights(t, o, j):
                n = 4 * t + j
                act.wait_ge(q_ab, n + 1)
                after(act, q_w, n - 1)
                nc.scalar.activation(b_wa[j % 2], B_A[j % 2][:], ACT.Copy).then_inc(q_ae, 1)

            def scaled(t, o, ko, j):
                n = 4 * t + j
                feat = b_gd[o][:, j, 3 * MUL:PX]
                act.wait_ge(gather[o][j], 32 * ko + 32)
                act.wait_ge(q_sh, t + 1)
                after(act, q_y, n - 1)
                for m in range(4):
                    nc.scalar.activation(b_xs[j % 2][:, m + (m > 0), :], feat[:, 0:MUL], ACT.Copy,
                                         scale=b_sh[o][:, j, m:m + 1])
                nc.scalar.activation(b_xs[j % 2][:, 5:8, :].rearrange("p c u -> p (c u)"), feat[:, MUL:D], ACT.Copy,
                                     scale=b_sh[o][:, j, 0:1]).then_inc(q_xs, 1)

            def sums(t, o, j):
                n = 4 * t + j
                act.wait_ge(q_agg, n + 1)
                after(act, added, 16 * (n - 1))
                nc.scalar.activation(b_out[j % 2], B_AGG[j % 2][:], ACT.Copy).then_inc(q_oe, 1)

            def step(s, k, b):
                t, o = s - 1, 1 - b
                if runs(s, 0):
                    after(act, q_eat, s)
                    if isinstance(s, int) and s == 0:
                        act.wait_ge(e_in, E_TOTAL)
                    nc.scalar.activation(b_ea, ea32[:, bass.ds(s * P, P)], ACT.Copy).then_inc(q_ea, 1)
                if runs(s, 1):
                    ko = before(k, b)
                    weights(t, o, 0)
                if runs(s, 2):
                    sums(t - 1, b, NSUB - 1)
                if runs(s, 1):
                    weights(t, o, 1)
                    scaled(t, o, ko, 1)
                    weights(t, o, 2)
                    scaled(t, o, ko, 2)
                    sums(t, o, 0)
                if runs(s, 0):
                    edge_hidden(s)
                if runs(s, 1):
                    weights(t, o, 3)
                    scaled(t, o, ko, 3)
                    sums(t, o, 1)
                if runs(s, 0):
                    hidden(s)
                    spread_hidden(s, (0, 1))
                if runs(s, 1):
                    sums(t, o, 2)
                if runs(s, 0):
                    spread_hidden(s, (2, 3))
                    scaled(s, b, k, 0)

            pipeline(act, step, ET + 1)

        @block.tensor
        def _(pe):
            wait_all(pe, row_out, 32 * (NT // 2))

            def sum_products(s, j):
                if j == 0:
                    after(pe, q_s, s)
                pe.wait_ge(q_pr, 4 * s + j + 1)
                for c in range(3):
                    last = nc.tensor.matmul(B_T[:, j * P:(j + 1) * P], b_pr[j % 2][:, c, :], ident[:],
                                            start=(c == 0), stop=(c == 2))
                last.then_inc(q_ipt, 1)

            def transpose_attr(s):
                pe.wait_ge(q_ea, s + 1)
                after(pe, q_hp, s)
                nc.tensor.transpose(B_H[:, 0:P], b_ea, ident[:]).then_inc(q_eat, 1)

            def hidden(s, b):
                pe.wait_ge(q_eae, s + 1)
                nc.tensor.matmul(B_H[:, P:2 * P], wf1[:], b_eaT, start=True, stop=True)
                pe.wait_ge(q_ipe, s + 1)
                for j in range(NSUB):
                    nc.tensor.matmul(B_H[:, 2 * P:3 * P], wc[:, j, :], b_ipT[:, j * P:(j + 1) * P],
                                     start=(j == 0), stop=False)
                pe.wait_ge(q_q, s + 1)
                nc.tensor.matmul(B_H[:, 2 * P:3 * P], b_q.rearrange("p j h -> p (j h)"), ident[:],
                                 start=False, stop=True).then_inc(q_h, 1)

            def transpose_keys(s, b):
                for j in range(NSUB):
                    last = nc.tensor.transpose(B_T[:, j * P:(j + 1) * P], b_key[b][:, j:j + 1].to_broadcast([P, P]),
                                               ident[:])
                last.then_inc(q_tr, 1)

            def weights(t, j):
                n = 4 * t + j
                pe.wait_ge(q_hb, n + 1)
                after(pe, q_ae, n - 1)
                after(pe, q_w, n - 1)
                for bank, columns, w_hi, w_lo in ((B_A, slice(0, P), wf2_hi, wf2_lo),
                                                  (B_B, slice(P, 2 * P), ws2_hi, ws2_lo)):
                    for i, (w, hh) in enumerate(parts(w_hi, w_lo, hb_hi[j], hb_lo[j])):
                        last = nc.tensor.matmul(bank[j % 2][:], hh[:, columns], w,
                                                start=(i == 0), stop=(i == 2))
                last.then_inc(q_ab, 1)

            def aggregate(t, o, j):
                n = 4 * t + j
                pe.wait_ge(q_s, t + 1)
                pe.wait_ge(q_msg, n + 1)
                after(pe, q_oe, n - 1)
                nc.tensor.matmul(B_AGG[j % 2][:], b_s[o][:, j, :], b_msg[j % 2].rearrange("p c u -> p (c u)"),
                                 start=True, stop=True).then_inc(q_agg, 1)

            def step(s, k, b):
                t, o = s - 1, 1 - b
                if runs(s, 1):
                    weights(t, 0)
                    weights(t, 1)
                if runs(s, 2):
                    aggregate(t - 1, b, NSUB - 1)
                if runs(s, 0):
                    sum_products(s, 0)
                    sum_products(s, 1)
                if runs(s, 1):
                    weights(t, 2)
                    aggregate(t, o, 0)
                if runs(s, 0):
                    sum_products(s, 2)
                    sum_products(s, 3)
                    transpose_attr(s)
                if runs(s, 1):
                    weights(t, 3)
                    aggregate(t, o, 1)
                if runs(s, 0):
                    hidden(s, b)
                    transpose_keys(s, b)
                if runs(s, 1):
                    aggregate(t, o, 2)

            pipeline(pe, step, ET + 1)

        at[0] = 0
        c_h = [take(NSUB, D) for _ in range(2)]
        c_x = [take(NSUB, D) for _ in range(2)]
        c_hT = take(4, TILE)
        c_x2 = [take(NSUB, D) for _ in range(2)]
        c_z = [take(NSUB, D) for _ in range(2)]
        c_g = take(4, TILE)
        c_sc = [take(2, NSUB) for _ in range(2)]
        c_bn, c_bz = take(NSUB, 6), take(NSUB, 6)
        c_mv = [take(NSUB, 2) for _ in range(2)]
        c_st = [take(4, NSUB) for _ in range(2)]
        c_var = take(2, NSUB)
        c_mz = [take(NSUB, 2) for _ in range(2)]
        c_rz = [take(2, NSUB) for _ in range(2)]
        c_lg, c_mx, c_o1, c_o2 = (take(NSUB, NX) for _ in range(4))
        c_if = take(NSUB, 2)
        c_d, c_th = take(NSUB), take(NSUB)
        c_w12 = take(2, NSUB)
        c_cf = take(NSUB, 3 * NX)
        c_mi = sb("c_mi", [P, NSUB, NX], U32)
        c_chi = sb("c_chi", [P, NSUB, NX], FP32R)
        c_lT = sb("c_lT", [2 * NX, TILE])
        c_cT = sb("c_cT", [3 * NX, TILE], FP32R)
        C_T, C_O, C_HB, C_L = psum[0:2], psum[2:4], psum[4:6], psum[7]
        C_EX = (psum[6], C_T[0], C_T[1], psum[6])

        c_in = [sem(f"c_in{b}") for b in range(2)]
        c_out = [sem(f"c_out{b}") for b in range(2)]
        (t1, t1act, t1dve, u_sc, u_xs, u_xb, u_o, u_x2, u_bn, u_mv, u_var, u_pow, u_nm, u_xh, u_t2, t2hi, t2lo) = (
            sem(f"c_{n}") for n in ("t1", "t1act", "t1dve", "sc", "xs", "xb", "o", "x2", "bn", "mv", "var", "pow",
                                    "nm", "xh", "t2", "t2hi", "t2lo"))
        (v_lt, v_lte, v_l, v_lg, v_d, v_th, v_chain, v_cf, v_ct, v_cte, v_h, v_ge, v_ex, v_mul, v_hi, v_lo, v_w2, v_xn, v_z,
         v_bz, v_mz, v_vz, v_pz, v_nz, v_zh, v_r, v_zg, v_fin) = (
            sem(f"c_{n}") for n in ("lt", "lte", "l", "lg", "d", "th", "chain", "cf", "ct", "cte", "h", "ge", "ex", "mul", "hi",
                                    "lo", "w2", "xn", "z", "bz", "mz", "vz", "pz", "nz", "zh", "r", "zg", "fin"))

        @block.sync
        def _(sp):
            sp.wait_ge(added, 16 * EC)

            def load(s, k, b):
                after(sp, u_t2, 4 * (s - 1))
                after(sp, u_x2, 4 * (s - 1))
                sp.dma_start(c_h[b], rows(acc, s)).then_inc(c_in[b], 16)
                sp.dma_start(c_x[b], rows(x, s)).then_inc(c_in[b], 16)

            def step(s, k, b):
                if runs(s, -1):
                    load(s + 1, k + b, 1 - b)
                if runs(s, 2):
                    t = s - 2
                    sp.wait_ge(v_fin, 4 * (s - 1))
                    if isinstance(t, int) and t == NT - 1:
                        sp.wait_ge(c_out[1 - b], 16 * (NT // 2))
                    sp.dma_start(rows(out, t), c_z[b]).then_inc(c_out[b], 16)

            load(0, 0, 0)
            pipeline(sp, step, NT + 1)
            for b in range(2):
                sp.wait_ge(c_out[b], 16 * (NT // 2))

        @block.vector
        def _(dve):
            dve.wait_ge(added, 16 * EC)

            def transposed(s, c):
                dve.wait_ge(t1, 4 * s + c + 1)
                nc.vector.tensor_copy(c_hT[:, c, :], C_T[1][:]).then_inc(t1dve, 1)

            def low_part(s, c):
                dve.wait_ge(t2hi, 4 * s + c + 1)
                nc.vector.tensor_tensor(xhT_lo[:, c, :], C_T[c % 2][:], xhT_hi[:, c, :].bitcast(FP32),
                                        ALU.subtract).then_inc(t2lo, 1)

            def scale(s, b):
                after(dve, u_xs, s - 1)
                at_s = stats[:, bass.ds(s, 1), :].rearrange("p a n -> p (a n)")
                nc.vector.tensor_scalar(c_sc[b][:, 0, :], at_s[:, 0:NSUB], 1.0, None, ALU.add)
                nc.vector.tensor_copy(c_sc[b][:, 1, :], at_s[:, NSUB:2 * NSUB]).then_inc(u_sc, 1)

            def residual(s, b, j):
                dve.wait_ge(u_o, 4 * s + j + 1)
                x2v = c_x2[b][:, j, MUL:D].rearrange("p (u c) -> p c u", c=3)
                xv = c_x[b][:, j, MUL:D].rearrange("p (u c) -> p c u", c=3)
                ov = C_O[j % 2][:, MUL:D].rearrange("p (c u) -> p c u", c=3)
                nc.vector.tensor_tensor(c_x2[b][:, j, 0:MUL], C_O[j % 2][:, 0:MUL], c_x[b][:, j, 0:MUL], ALU.add)
                nc.vector.tensor_tensor(x2v, ov, xv, ALU.add).then_inc(u_x2, 1)

            def x2_statistics(s, b, j):
                dve.wait_ge(u_x2, 4 * s + j + 1)
                nc.vector.bn_stats(c_bn[:, j, :], c_x2[b][:, j, :]).then_inc(u_bn, 1)

            def x2_variance(s, b):
                dve.wait_ge(u_bn, 4 * s + 4)
                settled(dve, dve_passed)
                for j in range(NSUB):
                    last = nc.vector.bn_aggr(c_mv[b][:, j, :], c_bn[:, j, :])
                last.then_inc(u_mv, 1)
                dve.wait_ge(u_mv, s + 1)
                nc.vector.tensor_scalar(c_var[:, 1, :], c_mv[b][:, :, 1], 1.0 + EPS, EPS * EPS, ALU.mult, ALU.add)
                nc.vector.tensor_scalar(c_var[:, 0, :], c_mv[b][:, :, 1], EPS, None, ALU.add).then_inc(u_var, 1)

            def shift(s, b, i):
                dve.wait_ge(u_pow, 2 * s + 2 - i)
                nc.vector.scalar_tensor_tensor(out=c_st[b][:, 2 + i, :], in0=c_st[b][:, i, :], scalar=-1.0,
                                               in1=c_mv[b][:, :, 0], op0=ALU.mult, op1=ALU.mult).then_inc(u_nm, 1)

            def top2(t):
                dve.wait_ge(v_l, t + 1)
                nc.vector.tensor_copy(c_lg, C_L[:, 0:NSUB * NX].rearrange("p (j e) -> p j e", j=NSUB)).then_inc(v_lg, 1)
                dve.wait_ge(v_lg, t + 1)
                settled(dve, dve_passed)
                for j in range(NSUB):
                    last = nc.vector.max(out=c_mx[:, j, :], in_=c_lg[:, j, :])
                last.then_inc(v_chain, 1)
                dve.wait_ge(v_chain, 6 * t + 1)
                nc.vector.tensor_tensor(c_d, c_mx[:, :, 0], c_mx[:, :, 1], ALU.subtract).then_inc(v_d, 1)
                for j in range(NSUB):
                    last = nc.vector.max_index(out=c_mi[:, j, :], in_max=c_mx[:, j, :], in_values=c_lg[:, j, :])
                last.then_inc(v_chain, 1)
                dve.wait_ge(v_chain, 6 * t + 2)
                nc.vector.tensor_copy(c_if, c_mi[:, :, 0:2]).then_inc(v_chain, 1)
                dve.wait_ge(v_chain, 6 * t + 3)
                for i, o in enumerate((c_o1, c_o2)):
                    nc.vector.tensor_tensor(o, iota8[:, None, :].to_broadcast([P, NSUB, NX]),
                                            c_if[:, :, i:i + 1].to_broadcast([P, NSUB, NX]), ALU.is_equal)
                dve.wait_ge(v_th, t + 1)
                nc.vector.tensor_scalar(c_w12[:, 0, :], c_th, 0.5, 0.5, ALU.mult, ALU.add)
                nc.vector.tensor_scalar(c_w12[:, 1, :], c_th, -0.5, 0.5, ALU.mult, ALU.add).then_inc(v_chain, 1)
                dve.wait_ge(v_chain, 6 * t + 4)
                for i, o in enumerate((c_o1, c_o2)):
                    last = nc.vector.tensor_tensor(o, o, c_w12[:, i, :, None].to_broadcast([P, NSUB, NX]), ALU.mult)
                last.then_inc(v_chain, 1)
                dve.wait_ge(v_chain, 6 * t + 5)
                nc.vector.tensor_tensor(c_o1, c_o1, c_o2, ALU.add).then_inc(v_chain, 1)
                dve.wait_ge(v_chain, 6 * t + 6)
                nc.vector.tensor_copy(c_chi[:], c_o1).then_inc(v_cf, 1)
                dve.wait_ge(v_cf, 2 * t + 1)
                for i in range(2):
                    nc.vector.tensor_copy(c_cf[:, :, i * NX:(i + 1) * NX], c_chi[:].bitcast(FP32))
                nc.vector.tensor_tensor(c_cf[:, :, 2 * NX:3 * NX], c_o1, c_chi[:].bitcast(FP32),
                                        ALU.subtract).then_inc(v_cf, 1)

            def weigh(t, q):
                dve.wait_ge(v_ge, 4 * t + q + 1)
                dve.wait_ge(v_ex, 4 * t + q + 1)
                nc.vector.tensor_tensor(c_g[:, q, :], C_EX[q][:], c_g[:, q, :], ALU.mult).then_inc(v_mul, 1)

            def second_residual(t, o, j):
                dve.wait_ge(v_w2, 4 * t + j + 1)
                dve.wait_ge(v_xn, 4 * t + j + 1)
                nc.vector.tensor_tensor(c_z[o][:, j, :], C_O[j % 2][:], c_z[o][:, j, :], ALU.add).then_inc(v_z, 1)

            def z_statistics(t, o, j):
                dve.wait_ge(v_z, 4 * t + j + 1)
                nc.vector.bn_stats(c_bz[:, j, :], c_z[o][:, j, :]).then_inc(v_bz, 1)

            def z_variance(t, o):
                dve.wait_ge(v_bz, 4 * t + 4)
                settled(dve, dve_passed)
                for j in range(NSUB):
                    last = nc.vector.bn_aggr(c_mz[o][:, j, :], c_bz[:, j, :])
                last.then_inc(v_mz, 1)
                dve.wait_ge(v_mz, t + 1)
                nc.vector.tensor_scalar(c_rz[o][:, 0, :], c_mz[o][:, :, 1], EPS, None, ALU.add).then_inc(v_vz, 1)

            def shift_z(t, b):
                dve.wait_ge(v_pz, t + 1)
                nc.vector.scalar_tensor_tensor(out=c_rz[b][:, 1, :], in0=c_mz[b][:, :, 0], scalar=-1.0,
                                               in1=c_rz[b][:, 0, :], op0=ALU.mult, op1=ALU.mult).then_inc(v_nz, 1)

            def finish(t, b, j):
                dve.wait_ge(v_zg, 4 * t + j + 1)
                dve.wait_ge(v_r, 4 * t + j + 1)
                nc.vector.tensor_tensor(c_z[b][:, j, :], c_z[b][:, j, :], c_x2[b][:, j, :], ALU.add).then_inc(v_fin, 1)

            def step(s, k, b):
                t, u, o = s - 1, s - 2, 1 - b
                if runs(s, 1):
                    low_part(t, 2)
                    low_part(t, 3)
                if runs(s, 2):
                    shift_z(u, b)
                if runs(s, 1):
                    top2(t)
                if runs(s, 0):
                    transposed(s, 1)
                if runs(s, 2):
                    for j in range(NSUB):
                        finish(u, b, j)
                if runs(s, 0):
                    transposed(s, 3)
                if runs(s, -1):
                    scale(s + 1, o)
                if runs(s, 1):
                    for q in range(3):
                        weigh(t, q)
                if runs(s, 0):
                    dve.wait_ge(u_xb, s + 1)
                    residual(s, b, 0)
                if runs(s, 1):
                    weigh(t, 3)
                if runs(s, 0):
                    for j in range(1, NSUB):
                        residual(s, b, j)
                        x2_statistics(s, b, j - 1)
                    x2_statistics(s, b, NSUB - 1)
                    x2_variance(s, b)
                if runs(s, 1):
                    second_residual(t, o, 0)
                if runs(s, 0):
                    shift(s, b, 1)
                if runs(s, 1):
                    second_residual(t, o, 1)
                    z_statistics(t, o, 0)
                if runs(s, 0):
                    shift(s, b, 0)
                if runs(s, 1):
                    second_residual(t, o, 2)
                    z_statistics(t, o, 1)
                if runs(s, 0):
                    low_part(s, 0)
                    low_part(s, 1)
                if runs(s, 1):
                    z_statistics(t, o, 2)
                    second_residual(t, o, 3)
                    z_statistics(t, o, 3)
                    z_variance(t, o)

            scale(0, 0)
            pipeline(dve, step, NT + 1)

        @block.gpsimd
        def _(pool):
            pool.wait_ge(added, 16 * EC)

            def add_bias(s, b):
                pool.wait_ge(u_xs, s + 1)
                nc.gpsimd.tensor_tensor(c_x[b][:, :, 0:MUL], c_x[b][:, :, 0:MUL],
                                        bo0_r[:, None, :].to_broadcast([P, NSUB, MUL]), ALU.add).then_inc(u_xb, 1)

            def gain(t, b, j):
                pool.wait_ge(v_zh, 4 * t + j + 1)
                nc.gpsimd.tensor_tensor(c_z[b][:, j, :], c_z[b][:, j, :], outg_r[:], ALU.mult).then_inc(v_zg, 1)

            def add_out_b(t, b, j):
                if j == 0:
                    pool.wait_ge(u_xh, t + 1)
                pool.wait_ge(v_xn, 4 * t + j + 1)
                nc.gpsimd.tensor_tensor(c_x2[b][:, j, :], c_x2[b][:, j, :], outb_r[:], ALU.add).then_inc(v_r, 1)

            def step(s, k, b):
                t, u, o = s - 1, s - 2, 1 - b
                if runs(s, 2):
                    pool.wait_ge(v_vz, u + 1)
                    nc.gpsimd.tensor_tensor(c_rz[b][:, 0, :], c_rz[b][:, 0, :], mhalf[:], ALU.pow).then_inc(v_pz, 1)
                    for j in range(NSUB):
                        gain(u, b, j)
                if runs(s, 1):
                    add_out_b(t, o, 0)
                    add_out_b(t, o, 1)
                    for q in range(4):
                        pool.wait_ge(v_hi, 4 * t + q + 1)
                        after(pool, v_w2, 4 * t)
                        nc.gpsimd.tensor_tensor(hg_lo[:, q, :], c_g[:, q, :], hg_hi[:, q, :].bitcast(FP32),
                                                ALU.subtract).then_inc(v_lo, 1)
                if runs(s, -1):
                    add_bias(s + 1, o)
                if runs(s, 0):
                    pool.wait_ge(u_var, s + 1)
                    for i in (1, 0):
                        nc.gpsimd.tensor_tensor(c_st[b][:, i, :], c_var[:, i, :], mhalf[:], ALU.pow).then_inc(u_pow, 1)
                if runs(s, 1):
                    add_out_b(t, o, 2)
                    add_out_b(t, o, 3)

            add_bias(0, 0)
            pipeline(pool, step, NT + 1)

        @block.scalar
        def _(act):
            act.wait_ge(added, 16 * EC)
            nc.scalar.preload_act_table_set("gelu_apprx_tanh_and_others")

            def transposed(s, c):
                act.wait_ge(t1, 4 * s + c + 1)
                nc.scalar.activation(c_hT[:, c, :], C_T[0][:], ACT.Copy).then_inc(t1act, 1)

            def high_part(s, c):
                act.wait_ge(u_t2, 4 * s + c + 1)
                nc.scalar.activation(xhT_hi[:, c, :], C_T[c % 2][:], ACT.Copy).then_inc(t2hi, 1)

            def scale_x(s, k, b):
                act.wait_ge(c_in[b], 32 * k + 32)
                act.wait_ge(u_sc, s + 1)
                for j in range(NSUB):
                    last = nc.scalar.activation(c_x[b][:, j, :], c_x[b][:, j, :], ACT.Identity,
                                                bias=c_sc[b][:, 1, j:j + 1], scale=c_sc[b][:, 0, j:j + 1])
                last.then_inc(u_xs, 1)

            def normalise(s, b):
                act.wait_ge(u_nm, 2 * s + 1)
                for j in range(NSUB):
                    last = nc.scalar.activation(c_h[b][:, j, :], c_x2[b][:, j, :], ACT.Identity,
                                                bias=c_st[b][:, 3, j:j + 1], scale=c_st[b][:, 1, j:j + 1])
                last.then_inc(u_xh, 1)

            def first_norm(t, o, ko, j):
                if j == 0:
                    act.wait_ge(u_nm, 2 * t + 2)
                    after(act, c_out[o], 16 * ko)
                nc.scalar.activation(c_z[o][:, j, :], c_x2[o][:, j, :], ACT.Identity,
                                     bias=c_st[o][:, 2, j:j + 1], scale=c_st[o][:, 0, j:j + 1]).then_inc(v_xn, 1)

            def normalise_z(u, b, j):
                act.wait_ge(v_nz, u + 1)
                nc.scalar.activation(c_z[b][:, j, :], c_z[b][:, j, :], ACT.Identity,
                                     bias=c_rz[b][:, 1, j:j + 1], scale=c_rz[b][:, 0, j:j + 1]).then_inc(v_zh, 1)

            def gelu(t, q):
                act.wait_ge(v_h, 4 * t + q + 1)
                after(act, v_lo, 4 * (t - 1) + q + 1)
                nc.scalar.activation(c_g[:, q, :], C_HB[q % 2][:], ACT.Gelu_apprx_tanh,
                                     bias=b1p_c[:, q:q + 1]).then_inc(v_ge, 1)

            def high_hidden(t, q):
                act.wait_ge(v_mul, 4 * t + q + 1)
                if q == 0:
                    after(act, v_w2, 4 * t)
                nc.scalar.activation(hg_hi[:, q, :], c_g[:, q, :], ACT.Copy).then_inc(v_hi, 1)

            def step(s, k, b):
                t, u, o = s - 1, s - 2, 1 - b
                ko = before(k, b)
                if runs(s, 1):
                    high_part(t, 2)
                    high_part(t, 3)
                if runs(s, 2):
                    normalise_z(u, b, 0)
                    normalise_z(u, b, 1)
                if runs(s, 1):
                    gelu(t, 0)
                if runs(s, 2):
                    normalise_z(u, b, 2)
                    normalise_z(u, b, 3)
                if runs(s, 1):
                    act.wait_ge(v_lt, t + 1)
                    nc.scalar.activation(c_lT[:], C_L[0:2 * NX, :], ACT.Identity, bias=bgate_c[:, 0:1]).then_inc(v_lte, 1)
                    first_norm(t, o, ko, 0)
                    gelu(t, 1)
                    act.wait_ge(v_d, t + 1)
                    nc.scalar.activation(c_th, c_d, ACT.Tanh, scale=0.5).then_inc(v_th, 1)
                if runs(s, 0):
                    transposed(s, 0)
                if runs(s, 1):
                    first_norm(t, o, ko, 1)
                    gelu(t, 2)
                    act.wait_ge(v_ct, t + 1)
                    nc.scalar.activation(c_cT[:], C_L[0:3 * NX, :], ACT.Copy).then_inc(v_cte, 1)
                if runs(s, 0):
                    transposed(s, 2)
                if runs(s, 1):
                    high_hidden(t, 0)
                    gelu(t, 3)
                    for q in range(1, 4):
                        high_hidden(t, q)
                    first_norm(t, o, ko, 2)
                    first_norm(t, o, ko, 3)
                if runs(s, -1):
                    scale_x(s + 1, k + b, o)
                if runs(s, 0):
                    normalise(s, b)
                    high_part(s, 0)
                    high_part(s, 1)

            scale_x(0, 0, 0)
            pipeline(act, step, NT + 1)

        @block.tensor
        def _(pe):
            pe.wait_ge(added, 16 * EC)

            def transpose_h(s, k, b, c):
                if c == 0:
                    pe.wait_ge(c_in[b], 32 * k + 32)
                    after(pe, t2lo, 4 * s)
                if c > 1:
                    pe.wait_ge(t1dve if c % 2 else t1act, 2 * s + 1)
                for j in range(NSUB):
                    last = nc.tensor.transpose(C_T[c % 2][:, j * P:(j + 1) * P], c_h[b][:, j, c * P:(c + 1) * P],
                                               ident[:])
                last.then_inc(t1, 1)

            def project(s, j):
                if j == 0:
                    pe.wait_ge(t1act, 2 * s + 2)
                    pe.wait_ge(t1dve, 2 * s + 2)
                    after(pe, v_z, 4 * (s - 1))
                if j > 1:
                    pe.wait_ge(u_x2, 4 * s + j - 1)
                for c in range(4):
                    last = nc.tensor.matmul(C_O[j % 2][:, c * MUL:(c + 1) * MUL], c_hT[:, c, j * P:(j + 1) * P],
                                            wo0[:] if c == 0 else wo1[:], start=True, stop=True)
                last.then_inc(u_o, 1)

            def transpose_x(s, b, c):
                if c == 0:
                    pe.wait_ge(u_xh, s + 1)
                    pe.wait_ge(t1act, 2 * s + 2)
                    after(pe, v_mul, 4 * s)
                if c > 1:
                    pe.wait_ge(t2lo, 4 * s + c - 1)
                for j in range(NSUB):
                    last = nc.tensor.transpose(C_T[c % 2][:, j * P:(j + 1) * P], c_h[b][:, j, c * P:(c + 1) * P],
                                               ident[:])
                last.then_inc(u_t2, 1)

            def logits(t):
                after(pe, v_cte, t)
                for c in range(4):
                    for i, xh in enumerate((xhT_hi, xhT_lo)):
                        last = nc.tensor.matmul(C_L[:], wg_parts[:, c, :], xh[:, c, :],
                                                start=(c == 0 and i == 0), stop=(c == 3 and i == 1))
                last.then_inc(v_lt, 1)

            def fold_logits(t):
                pe.wait_ge(v_lte, t + 1)
                for j in range(NSUB):
                    last = nc.tensor.matmul(C_L[:, j * NX:(j + 1) * NX], c_lT[:, j * P:(j + 1) * P], fold[:],
                                            start=True, stop=True)
                last.then_inc(v_l, 1)

            def hidden(t, q, chunks=range(4)):
                for c in chunks:
                    if c == 0:
                        after(pe, v_ge, 4 * t + q - 1)
                    if q == 0:
                        pe.wait_ge(t2lo, 4 * t + c + 1)
                    for i, (w, xh) in enumerate(parts(w1_hi, w1_lo, xhT_hi, xhT_lo)):
                        last = nc.tensor.matmul(C_HB[q % 2][:], w[:, c, q * P:(q + 1) * P], xh[:, c, :],
                                                start=(c == 0 and i == 0), stop=(c == 3 and i == 2))
                if chunks[-1] == 3:
                    last.then_inc(v_h, 1)

            def spread(t, q):
                if q == 0:
                    pe.wait_ge(v_cte, t + 1)
                if q == 3:
                    pe.wait_ge(v_mul, 4 * t + 1)
                nc.tensor.matmul(C_EX[q][:], sel[:, q * P:(q + 1) * P], c_cT[:], start=True, stop=True).then_inc(v_ex, 1)

            def expert_out(s, t, j):
                if j > 1:
                    pe.wait_ge(v_z, 4 * t + j - 1)
                elif runs(s, 0):
                    pe.wait_ge(u_x2, 4 * s + j + 3)
                else:
                    pe.wait_ge(v_z, 4 * (t - 1) + j + 3)
                tokens = slice(j * P, (j + 1) * P)
                nc.tensor.matmul(C_O[j % 2][:], c_cT[:, tokens], b2s[:], start=True, stop=False)
                for q in range(4):
                    if j == 0:
                        pe.wait_ge(v_lo, 4 * t + q + 1)
                    for i, (w, hg) in enumerate(parts(w2_hi, w2_lo, hg_hi, hg_lo)):
                        last = nc.tensor.matmul(C_O[j % 2][:], hg[:, q, tokens], w[:, q, :],
                                                start=False, stop=(q == 3 and i == 2))
                last.then_inc(v_w2, 1)

            def step(s, k, b):
                t = s - 1
                if runs(s, 1):
                    hidden(t, 0, (0,))
                    transpose_x(t, 1 - b, 2)
                    hidden(t, 0, (1,))
                    transpose_x(t, 1 - b, 3)
                    hidden(t, 1, (0, 1))
                    hidden(t, 0, (2, 3))
                    logits(t)
                    hidden(t, 1, (2, 3))
                if runs(s, 0):
                    transpose_h(s, k, b, 0)
                if runs(s, 1):
                    fold_logits(t)
                if runs(s, 0):
                    transpose_h(s, k, b, 1)
                if runs(s, 1):
                    hidden(t, 2)
                    pe.wait_ge(v_cf, 2 * t + 2)
                    for j in range(NSUB):
                        last = nc.tensor.transpose(C_L[0:3 * NX, j * P:(j + 1) * P], c_cf[:, j, :], ident[:])
                    last.then_inc(v_ct, 1)
                if runs(s, 0):
                    transpose_h(s, k, b, 2)
                    transpose_h(s, k, b, 3)
                if runs(s, 1):
                    spread(t, 0)
                    hidden(t, 3)
                    if runs(s, 0):
                        pe.wait_ge(t1act, 2 * s + 2)
                        pe.wait_ge(t1dve, 2 * s + 2)
                    spread(t, 1)
                    spread(t, 2)
                if runs(s, 0):
                    project(s, 0)
                if runs(s, 1):
                    spread(t, 3)
                if runs(s, 0):
                    for j in range(1, NSUB):
                        project(s, j)
                if runs(s, 1):
                    for j in range(NSUB - 1):
                        expert_out(s, t, j)
                if runs(s, 0):
                    transpose_x(s, b, 0)
                    transpose_x(s, b, 1)
                if runs(s, 1):
                    expert_out(s, t, NSUB - 1)

            pipeline(pe, step, NT)


_INS = ['x', 'src', 'dst', 'edge_attr_32', 'edge_attr_4',
        'L0_gnn_W_pre0', 'L0_gnn_b_pre0', 'L0_gnn_W_pre1', 'L0_gnn_W_nd0', 'L0_gnn_b_nd0', 'L0_gnn_W_nd1',
        'L0_gnn_W_g1', 'L0_gnn_b_g1', 'L0_gnn_W_g2', 'L0_gnn_b_g2', 'L0_gnn_W_f1', 'L0_gnn_W_f2',
        'L0_gnn_W_s1', 'L0_gnn_W_s2', 'L0_gnn_W_o0', 'L0_gnn_b_o0', 'L0_gnn_W_o1',
        'L0_ffn_Wg', 'L0_ffn_W1', 'L0_ffn_b1', 'L0_ffn_W2', 'L0_ffn_b2',
        'L0_ffn_ln_g', 'L0_ffn_ln_b', 'L0_ffn_out_g', 'L0_ffn_out_b']


def kernel(**inputs):
    import numpy as _np
    import concourse.bacc as _bacc
    from concourse import mybir as _mybir
    from concourse.bass_utils import run_bass_kernel_spmd as _run

    nc = _bacc.Bacc("TRN2", target_bir_lowering=False, num_devices=1)
    arrays, args = {}, []
    for name in _INS:
        a = _np.ascontiguousarray(inputs[name])
        arrays[f"in_{name}"] = a
        args.append(nc.dram_tensor(f"in_{name}", a.shape, _mybir.dt.from_np(a.dtype), kind="ExternalInput").ap())
    args.append(nc.dram_tensor("out_x", (N, D), FP32, kind="ExternalOutput").ap())
    gnn_ffn_kernel(nc, *args)
    r = _run(nc, [arrays], core_ids=[0])
    return r.results[0]["out_x"]
```
